# Optimizing a Trainium2 kernel written in Bass

```python
import numpy as np
import jax
import jax.numpy as jnp

def _softmax(x, axis=-1):
    return jax.nn.softmax(x, axis=axis)

def _gelu(x):
    return jax.nn.gelu(x, approximate=True)

def _silu(x):
    return jax.nn.silu(x)

def _sigmoid(x):
    return jax.nn.sigmoid(x)

def _layernorm(x, axis=-1, eps=1e-05):
    m = jnp.mean(x, axis=axis, keepdims=True)
    v = jnp.var(x, axis=axis, keepdims=True)
    return (x - m) / jnp.sqrt(v + eps)

def _scatter_add(tgt, idx, src, axis=0):
    return tgt.at[idx].add(src)

def _segment_sum(src, seg, n):
    return jax.ops.segment_sum(src, seg, n)
kernel_name = 'mk_xattn_ffn_d1_seqx_r4_61affb'

def setup_inputs(seed: int=0):
    np.random.seed(seed)
    _w = jnp.asarray

    def _rec_inputs():
        import jax
        import jax.numpy as jnp
        _rk = jax.random.key(seed)
        x = -0.000125 + 0.9999 * jax.random.normal(jax.random.fold_in(_rk, 1), (4, 512, 512), jnp.float32)
        _lenS = 512 - jax.random.randint(jax.random.fold_in(_rk, 7), (4,), 0, max(1, 512 // 4) + 1, jnp.int32)
        _lenS2 = 512 - jax.random.randint(jax.random.fold_in(_rk, 8), (4,), 0, max(1, 512 // 4) + 1, jnp.int32)
        itok_BxS_13_99985 = jax.random.randint(jax.random.fold_in(_rk, 11), (4, 512), 13, 99986, jnp.int32)
        _ctx_2048P = jax.random.normal(jax.random.fold_in(_rk, 12), (4, 16, 512), jnp.float32)
        _ctx_2048c = jax.random.dirichlet(jax.random.fold_in(_rk, 512), 0.3 * jnp.ones((16,), jnp.float32), (4, 512))
        _ctx_2048t = jnp.einsum('bsk,bkd->bsd', _ctx_2048c, _ctx_2048P)
        _ctx_2048t = _ctx_2048t * jax.lax.rsqrt(jnp.mean(jnp.square(_ctx_2048t)) + 1e-12) * 0.953939
        ctx_2048 = 6.82029e-06 + 0.0200006 * (_ctx_2048t + 0.3 * jax.random.normal(jax.random.fold_in(_rk, 612), (4, 512, 512), jnp.float32))
        return (x, itok_BxS_13_99985, ctx_2048)
    x, itok_BxS_13_99985, ctx_2048 = _rec_inputs()

    def _L0_xattn_setup():
        import jax, jax.numpy as jnp
        import numpy as np
        B, S, D = (4, 1024, 512)
        E = 4
        F = 2048 // E
        VOCAB = 25000
        key = jax.random.key(seed)
        k1, k2, k3, k4, k5 = jax.random.split(key, 5)
        hidden_states = jax.random.normal(k1, (B, S, D), dtype=jnp.float32)
        token_ids = jax.random.randint(k2, (B, S), 0, VOCAB, dtype=jnp.int64)
        Wg = jax.random.normal(k3, (E, F, D), dtype=jnp.float32) * 0.02
        Wu = jax.random.normal(k4, (E, F, D), dtype=jnp.float32) * 0.02
        Wd = jax.random.normal(k5, (E, D, F), dtype=jnp.float32) * 0.02
        return {'hidden_states': hidden_states, 'token_ids': token_ids, 'Wg': Wg, 'Wu': Wu, 'Wd': Wd}
    _L0_xattn_all = _L0_xattn_setup()
    _L0_xattn_in = {k: v for k, v in _L0_xattn_all.items() if k in ()}
    del _L0_xattn_all

    def _L0_ffn_setup():
        import jax, jax.numpy as jnp
        import numpy as np
        H = 512
        I = 256
        E = 32
        K = 4
        N_SHARED = 1
        EPS = 1e-06

        def _rmsnorm(x, w, eps=EPS):
            var = jnp.mean(jnp.square(x), axis=-1, keepdims=True)
            return x * jax.lax.rsqrt(var + eps) * w

        def _moe_core(x, gate_w, w13, w2):
            T = x.shape[0]
            N = T * K
            C = 2 * N // E
            logits = jnp.einsum('th,eh->te', x.astype(jnp.float32), gate_w.astype(jnp.float32))
            scores = jax.nn.softmax(logits, axis=-1)
            topk_w, topk_ids = jax.lax.top_k(scores, K)
            topk_w = topk_w / jnp.sum(topk_w, axis=-1, keepdims=True)
            flat_ids = topk_ids.reshape(-1)
            flat_w = topk_w.reshape(-1)
            order = jnp.argsort(flat_ids)
            sorted_eid = flat_ids[order]
            tok = order // K
            counts = jnp.zeros((E,), jnp.int32).at[flat_ids].add(1)
            starts = jnp.cumsum(counts) - counts
            pos = jnp.arange(N) - starts[sorted_eid]
            buf = jnp.zeros((E, C, x.shape[1]), x.dtype).at[sorted_eid, pos].set(x[tok], mode='drop')
            gu = jnp.einsum('ech,ehf->ecf', buf, w13)
            g, u = jnp.split(gu, 2, axis=-1)
            act = jax.nn.silu(g) * u
            eo = jnp.einsum('eci,eih->ech', act, w2)
            out_slots = eo[sorted_eid, pos]
            routed = jnp.zeros_like(x).at[tok].add(out_slots * flat_w[order][:, None])
            return routed
        key = jax.random.key(seed)
        ks = jax.random.split(key, 8)
        s = 1.0 / np.sqrt(H)
        si = 1.0 / np.sqrt(I)
        return {'hidden_states': jax.random.normal(ks[0], (1, 1024, H), jnp.float32), 'norm_w': jnp.ones((H,), jnp.float32), 'gate_w': jax.random.normal(ks[1], (E, H), jnp.float32) * s, 'w13': jax.random.normal(ks[2], (E, H, 2 * I), jnp.float32) * s, 'w2': jax.random.normal(ks[3], (E, I, H), jnp.float32) * si, 'shared_gate_w': jax.random.normal(ks[4], (H, I * N_SHARED), jnp.float32) * s, 'shared_up_w': jax.random.normal(ks[5], (H, I * N_SHARED), jnp.float32) * s, 'shared_down_w': jax.random.normal(ks[6], (I * N_SHARED, H), jnp.float32) * si}
    _L0_ffn_all = _L0_ffn_setup()
    _L0_ffn_in = {k: v for k, v in _L0_ffn_all.items() if k in ('norm_w', 'gate_w', 'w13', 'w2', 'shared_gate_w', 'shared_up_w', 'shared_down_w')}
    del _L0_ffn_all
    return {'x': x, 'itok_BxS_13_99985': itok_BxS_13_99985, 'ctx_2048': ctx_2048, 'L0_ffn_norm_w': _L0_ffn_in['norm_w'], 'L0_ffn_gate_w': _L0_ffn_in['gate_w'], 'L0_ffn_w13': _L0_ffn_in['w13'], 'L0_ffn_w2': _L0_ffn_in['w2'], 'L0_ffn_shared_gate_w': _L0_ffn_in['shared_gate_w'], 'L0_ffn_shared_up_w': _L0_ffn_in['shared_up_w'], 'L0_ffn_shared_down_w': _L0_ffn_in['shared_down_w']}

def reference(x, itok_BxS_13_99985, ctx_2048, L0_ffn_norm_w, L0_ffn_gate_w, L0_ffn_w13, L0_ffn_w2, L0_ffn_shared_gate_w, L0_ffn_shared_up_w, L0_ffn_shared_down_w):
    import jax
    import jax.numpy as jnp

    def _L0_xattn_ref(hidden_states, token_ids, Wg, Wu, Wd):
        import jax, jax.numpy as jnp
        import numpy as np
        B, S, D = (4, 1024, 512)
        E = 4
        F = 2048 // E
        VOCAB = 25000
        tokens_per_expert = VOCAB // E
        tid = jnp.clip(token_ids, 0, VOCAB - 1)
        expert_ids = jnp.minimum(tid // tokens_per_expert, E - 1)
        out = jnp.zeros_like(hidden_states)
        for e in range(E):
            g = jax.nn.silu(jnp.einsum('bsd,fd->bsf', hidden_states, Wg[e]))
            u = jnp.einsum('bsd,fd->bsf', hidden_states, Wu[e])
            y = jnp.einsum('bsf,df->bsd', g * u, Wd[e])
            out = jnp.where((expert_ids == e)[..., None], y, out)
        return out

    def _L0_ffn_ref(hidden_states, norm_w, gate_w, w13, w2, shared_gate_w, shared_up_w, shared_down_w):
        import jax, jax.numpy as jnp
        import numpy as np
        H = 512
        I = 256
        E = 32
        K = 4
        N_SHARED = 1
        EPS = 1e-06

        def _rmsnorm(x, w, eps=EPS):
            var = jnp.mean(jnp.square(x), axis=-1, keepdims=True)
            return x * jax.lax.rsqrt(var + eps) * w

        def _moe_core(x, gate_w, w13, w2):
            T = x.shape[0]
            N = T * K
            C = 2 * N // E
            logits = jnp.einsum('th,eh->te', x.astype(jnp.float32), gate_w.astype(jnp.float32))
            scores = jax.nn.softmax(logits, axis=-1)
            topk_w, topk_ids = jax.lax.top_k(scores, K)
            topk_w = topk_w / jnp.sum(topk_w, axis=-1, keepdims=True)
            flat_ids = topk_ids.reshape(-1)
            flat_w = topk_w.reshape(-1)
            order = jnp.argsort(flat_ids)
            sorted_eid = flat_ids[order]
            tok = order // K
            counts = jnp.zeros((E,), jnp.int32).at[flat_ids].add(1)
            starts = jnp.cumsum(counts) - counts
            pos = jnp.arange(N) - starts[sorted_eid]
            buf = jnp.zeros((E, C, x.shape[1]), x.dtype).at[sorted_eid, pos].set(x[tok], mode='drop')
            gu = jnp.einsum('ech,ehf->ecf', buf, w13)
            g, u = jnp.split(gu, 2, axis=-1)
            act = jax.nn.silu(g) * u
            eo = jnp.einsum('eci,eih->ech', act, w2)
            out_slots = eo[sorted_eid, pos]
            routed = jnp.zeros_like(x).at[tok].add(out_slots * flat_w[order][:, None])
            return routed
        B, S, Hd = hidden_states.shape
        residual = hidden_states
        h = _rmsnorm(hidden_states, norm_w)
        x = h.reshape(-1, Hd)
        routed = _moe_core(x, gate_w, w13, w2)
        shared = jax.nn.silu(x @ shared_gate_w) * (x @ shared_up_w) @ shared_down_w
        out = residual + (routed + shared).reshape(B, S, Hd)
        return out
    x = x + _L0_xattn_ref(_layernorm(x, axis=-1), itok_BxS_13_99985, ctx_2048, ctx_2048, ctx_2048)
    x = x + _L0_ffn_ref(_layernorm(x, axis=-1), L0_ffn_norm_w, L0_ffn_gate_w, L0_ffn_w13, L0_ffn_w2, L0_ffn_shared_gate_w, L0_ffn_shared_up_w, L0_ffn_shared_down_w)
    return x

_drawn_inputs = setup_inputs


def setup_inputs(seed=0):
    import zlib

    import numpy as np

    out = dict(_drawn_inputs(seed))
    spreads = {'L0_ffn_norm_w': (1.0, 0.2)}
    factors = {}
    for name, (base, spread) in spreads.items():
        noise = np.random.default_rng([zlib.crc32(name.encode()), seed]).standard_normal(out[name].shape)
        drawn = base * np.exp(spread * noise) if base else spread * noise
        out[name] = jnp.asarray(drawn.astype(out[name].dtype))
    for name, factor in factors.items():
        out[name] = (out[name] * factor).astype(out[name].dtype)
    return out
```

```python
from contextlib import ExitStack

import concourse.bass as bass
from concourse import mybir

F32 = mybir.dt.float32
F32R = mybir.dt.float32r
BF16 = mybir.dt.bfloat16
I32 = mybir.dt.int32
U32 = mybir.dt.uint32
ALU = mybir.AluOpType
ACT = mybir.ActivationFunctionType
AX = mybir.AxisListType

P = 128
D = 512
C = D // P
TOKENS = 2048
G = TOKENS // P
E1 = 4
VOCAB = 25000
PER_EXPERT = VOCAB // E1
E2 = 32
K = 4
INNER = 256
CI = INNER // P
CAP = 2 * TOKENS * K // E2
MAX1 = 20
MAX2 = 96
MIN_PAIRS = 8
LOOK_BACK = 3
STEP_PAIRS = MAX2 // 2 + 1
PAD = P
LN_EPS = 1e-5
RMS_EPS = 1e-6
W_SETS = 3
HL = C + CI


class Memory:
    pass


class Tile:

    def __init__(self, pair, off):
        self.off = off
        self.n = 2 * pair + off
        self.half = pair + off // 2
        self.par = off % 2


def wait(eng, sem, value):
    if isinstance(value, int) and value <= 0:
        return
    eng.wait_ge(sem, value)


def pipeline(eng, pairs, skews, emit, look=lambda pair: None):
    deepest = max(s for _, s in skews)
    first = (deepest + 3) // 2
    for pair in range(first):
        look(pair)
        for b in range(2):
            for part, s in skews:
                if 2 * pair + b - s >= 0:
                    emit(part, Tile(pair, b - s))
    with eng.Fori(first, pairs) as pair:
        look(pair)
        for b in range(2):
            for part, s in skews:
                emit(part, Tile(pair, b - s))
    look(pairs)
    for b in range(deepest):
        for part, s in skews:
            if b - s < 0:
                emit(part, Tile(pairs, b - s))


class Chain:

    def __init__(self, eng, sem):
        self.eng, self.sem, self.n = eng, sem, 0

    def __call__(self, ins):
        self.n += 1
        ins.then_inc(self.sem, 1)
        self.eng.wait_ge(self.sem, self.n)




def tensors(nc, m, top):
    sb = m.sb
    m.ident = sb("ident", [P, P], F32, top)
    m.before = sb("before", [P, P], F32, top)
    m.ones = sb("ones", [P, P], F32, top)
    m.iota_row = sb("iota_row", [P, P], F32, top)
    m.part_id = sb("part_id", [P, 1], F32, top)
    m.pad_row = sb("pad_row", [P, 1], F32, top)
    m.minus_half = sb("minus_half", [P, 1], F32, top)
    m.tokcol = sb("tokcol", [P, G], F32, top)
    m.normw = sb("normw", [P, D], F32, top)
    m.gT = sb("gT", [P, C, E2], F32, top)
    m.gather1 = sb("gather1", [P, MAX1], I32, top)
    m.scatter1 = sb("scatter1", [P, MAX1], I32, top)
    m.tab1 = sb("tab1", [1, 2, MAX1], I32, top)
    m.gather2 = sb("gather2", [P, MAX2], I32, top)
    m.scatter2 = sb("scatter2", [P, MAX2], I32, top)
    m.weight2 = sb("weight2", [P, MAX2], F32, top)
    m.tab2 = sb("tab2", [1, 3, STEP_PAIRS], I32, top)
    m.over_row = sb("over_row", [P, K, G], I32, top)
    m.over_tok = sb("over_tok", [P, K, G], I32, top)
    m.topw = sb("topw", [P, G, K], F32, top)
    m.topk = sb("topk", [P, K, G], F32, top)
    m.wh_s = sb("wh_s", [P, HL, D], F32R, top)
    m.wl_s = sb("wl_s", [P, HL, D], F32R, top)


def number_of_pairs(eng, entry, most):
    return eng.value_load(entry, min_val=0, max_val=most // 2 - MIN_PAIRS) + MIN_PAIRS


def semaphores(nc, stack, prefix, names):
    return {n: stack.enter_context(nc.semaphore(prefix + n)) for n in names}


def three_products(pe, acc, left_hi, left_lo, right_hi, right_lo, start, stop):
    pe.matmul(acc, left_hi, right_hi, start=start, stop=False)
    pe.matmul(acc, left_hi, right_lo, start=False, stop=False)
    return pe.matmul(acc, left_lo, right_hi, start=False, stop=stop)


def setup(nc, m):
    with ExitStack() as st:
        def ps(name, shape, dt=F32):
            return st.enter_context(nc.psum_tensor(name, shape, dt))
        craw = m.sb("craw", [P, 2, C, D], F32, st)
        sraw = m.sb("sraw", [P, HL, D], F32, st)
        graw = m.sb("graw", [E2, D], F32, st)
        zeros = m.sb("zeros", [P, D], F32, st)
        tidi = m.sb("tidi", [P, G], I32, st)
        tidf = m.sb("tidf", [P, G], F32, st)
        M = m.sb("M1", [P, G, E1], F32, st)
        reach = m.sb("reach1", [P, E1 + 1, G], F32, st)
        slots = m.sb("slots1", [P, G, E1], F32, st)
        row = m.sb("row1", [P, 8, E1], F32, st)
        rowi = m.sb("row1i", [P, E1], I32, st)
        sel = m.sb("sel1", [P, 4, G], F32, st)
        seli = m.sb("sel1i", [P, 3, G], I32, st)
        hot = m.sb("hot1", [P, 2, P + MAX1], F32, st)
        tabf = m.sb("tab1f", [P, 3, MAX1], F32, st)
        cmp = m.sb("cmp1", [1, MAX1, E1], F32, st)
        tbf = m.sb("tb1f", [1, 2, MAX1], F32, st)
        psC = [ps(f"psC{i}", [P, D]) for i in range(3)]
        psG = ps("psG", [P, E2])
        psP = ps("psP", [P, 2, E1])
        psR = ps("psR", [P, MAX1])
        block = st.enter_context(nc.Block())

        @block.sync
        def _(sp):
            sp.dma_start(tidi[:], m.tid).then_inc(m.s["tid_loaded"], 16)
            for e in range(E1):
                if e >= 2:
                    sp.wait_ge(m.s["ctx_turned"], 4 * (e - 1))
                sp.dma_start(craw[:, e % 2], m.ctx_w[e].rearrange("(c p) n -> p c n", p=P)).then_inc(
                    m.s[f"ctx_loaded{e % 2}"], 16)
                if e == 0:
                    sp.dma_start(graw[:], m.gate_w).then_inc(m.s["gate_loaded"], 16)
                    sp.dma_start(m.normw[:], m.norm_w.to_broadcast([P, D])).then_inc(m.s["norm_loaded"], 16)
            sp.dma_start(sraw[:, 0:C, 0:INNER], m.sg.rearrange("(c p) n -> p c n", p=P)).then_inc(m.s["sh_loaded"], 16)
            sp.dma_start(sraw[:, 0:C, INNER:D], m.su.rearrange("(c p) n -> p c n", p=P)).then_inc(m.s["sh_loaded"], 16)
            sp.dma_start(sraw[:, C:HL, :], m.sd.rearrange("(c p) n -> p c n", p=P)).then_inc(m.s["sh_loaded"], 16)
            sp.wait_ge(m.s["consts"], 1)
            sp.dma_start(m.out[TOKENS:TOKENS + PAD, :], zeros[:]).then_inc(m.s["zero_pad"], 16)
            sp.dma_start(m.last_dram, zeros[0:MAX2, :]).then_inc(m.s["zero_pad"], 16)
            sp.wait_ge(m.s["zero_pad"], 32)

        @block.gpsimd
        def _(pool):
            k = Chain(pool, m.s["chain0"])
            nc.gpsimd.memset(zeros[:], 0.0).then_inc(m.s["consts"], 1)
            nc.gpsimd.memset(m.minus_half[:], -0.5)
            k(nc.gpsimd.memset(m.ones[:], 1.0))
            k(nc.gpsimd.affine_select(out=m.ident[:], in_=m.ones[:], compare_op=ALU.is_equal, fill=0.0, base=0,
                                      pattern=[[-1, P]], channel_multiplier=1))
            k(nc.gpsimd.affine_select(out=m.before[:], in_=m.ones[:], compare_op=ALU.is_gt, fill=0.0, base=0,
                                      pattern=[[1, P]], channel_multiplier=-1))
            nc.gpsimd.iota(m.iota_row[:], pattern=[[1, P]], base=0, channel_multiplier=0,
                           allow_small_or_imprecise_dtypes=True)
            nc.gpsimd.iota(m.part_id[:], pattern=[[0, 1]], base=0, channel_multiplier=1,
                           allow_small_or_imprecise_dtypes=True)
            nc.gpsimd.iota(m.pad_row[:], pattern=[[0, 1]], base=TOKENS + 1, channel_multiplier=1,
                           allow_small_or_imprecise_dtypes=True)
            nc.gpsimd.iota(m.tokcol[:], pattern=[[1, G]], base=1, channel_multiplier=G,
                           allow_small_or_imprecise_dtypes=True).then_inc(m.s["consts"], 1)
            pool.wait_ge(m.s["sh_hi"], 1)
            nc.gpsimd.tensor_tensor(m.wl_s[:], sraw[:], m.wh_s[:].bitcast(F32), ALU.subtract)

        @block.tensor
        def _(pe):
            pe.wait_ge(m.s["consts"], 2)
            pe.wait_ge(m.s["counted"], 1)
            pe.matmul(psP[:, 0, :], m.before[:], row[:, 0, :], start=True, stop=True)
            pe.matmul(psP[:, 1, :], m.ones[:], row[:, 0, :], start=True, stop=True).then_inc(m.s["prefix"], 1)
            for e in range(E1):
                pe.wait_ge(m.s[f"ctx_loaded{e % 2}"], 16 * (e // 2 + 1))
                for c in range(C):
                    n = e * C + c
                    if n >= 3:
                        pe.wait_ge(m.s["ctx_split"], n - 2)
                    for r in range(C):
                        mm = pe.transpose(psC[n % 3][:, r * P:(r + 1) * P],
                                          craw[:, e % 2, r, c * P:(c + 1) * P], m.ident[:])
                    mm.then_inc(m.s["ctx_turned"], 1)
                    if n == 2:
                        for i in range(G):
                            pe.wait_ge(m.s["onehot"], i + 1)
                            mm = pe.matmul(psR[:], hot[:, i % 2, 0:P], hot[:, i % 2, P:P + MAX1],
                                           start=(i == 0), stop=(i == G - 1)).then_inc(m.s["table"], 1)
                        pe.wait_ge(m.s["gate_loaded"], 16)
                        for c in range(C):
                            if c:
                                pe.wait_ge(m.s["gate_done"], c)
                            pe.transpose(psG[:, :], graw[:, c * P:(c + 1) * P], m.ident[0:E2, 0:E2]).then_inc(
                                m.s["gate_turned"], 1)

        @block.scalar
        def _(act):
            def gate(c):
                act.wait_ge(m.s["gate_turned"], c + 1)
                nc.scalar.activation(m.gT[:, c, :], psG[:], ACT.Copy).then_inc(m.s["gate_done"], 1)
            for n in range(E1 * C):
                act.wait_ge(m.s["ctx_turned"], n + 1)
                nc.scalar.activation(m.cth[:, n // C, n % C, :], psC[n % 3][:], ACT.Copy).then_inc(m.s["ctx_hi"], 1)
                if n == 2:
                    for c in range(C):
                        gate(c)
            act.wait_ge(m.s["sh_loaded"], 48)
            nc.scalar.activation(m.wh_s[:], sraw[:], ACT.Copy).then_inc(m.s["sh_hi"], 1)

        @block.vector
        def _(dve):
            k = Chain(dve, m.s["chain1"])

            def low(n):
                dve.wait_ge(m.s["ctx_hi"], n + 1)
                dve.tensor_tensor(m.ctl[:, n // C, n % C, :], psC[n % 3][:], m.cth[:, n // C, n % C, :].bitcast(F32),
                                  ALU.subtract).then_inc(m.s["ctx_split"], 1)
            dve.wait_ge(m.s["tid_loaded"], 16)
            k(dve.tensor_copy(tidf[:], tidi[:]))
            dve.memset(reach[:, 0, :], 1.0)
            dve.memset(reach[:, E1, :], 0.0)
            for e in range(1, E1):
                ins = dve.tensor_scalar(reach[:, e, :], tidf[:], float(e * PER_EXPERT), None, ALU.is_ge)
            k(ins)
            k(dve.tensor_tensor(M[:], reach[:, 0:E1, :].rearrange("p e g -> p g e"),
                                reach[:, 1:E1 + 1, :].rearrange("p e g -> p g e"), ALU.subtract))
            dve.tensor_reduce(row[:, 0, :], M[:].rearrange("p g e -> p e g"), AX.X, ALU.add).then_inc(m.s["counted"], 1)
            k(dve.memset(slots[:, 0, :], 0.0))
            for g in range(1, G):
                k(dve.tensor_tensor(slots[:, g, :], slots[:, g - 1, :], M[:, g - 1, :], ALU.add))
            dve.wait_ge(m.s["prefix"], 1)
            k(dve.tensor_scalar(row[:, 1, :], psP[:, 1, :], float(P - 1), None, ALU.add))
            k(dve.tensor_copy(rowi[:], row[:, 1, :]))
            k(dve.tensor_scalar(rowi[:], rowi[:], 7, None, ALU.logical_shift_right))
            k(dve.tensor_copy(row[:, 2, :], rowi[:]))
            k(dve.memset(row[:, 3, :], 0.0))
            k(dve.tensor_tensor_scan(row[:, 4, :], row[:, 2, :], row[:, 3, :], 0.0, ALU.add, ALU.add))
            k(dve.tensor_tensor(row[:, 5, :], row[:, 4, :], row[:, 2, :], ALU.subtract))
            k(dve.scalar_tensor_tensor(out=row[:, 6, :], in0=row[:, 5, :], scalar=float(P), in1=psP[:, 0, :],
                                       op0=ALU.mult, op1=ALU.add))
            k(dve.tensor_tensor(slots[:], slots[:], row[:, 6:7, :].to_broadcast([P, G, E1]), ALU.add))
            k(dve.tensor_tensor(slots[:], slots[:], M[:], ALU.mult))
            k(dve.tensor_reduce(sel[:, 0, :], slots[:], AX.X, ALU.add))
            k(dve.tensor_copy(seli[:, 0, :], sel[:, 0, :]))
            dve.tensor_scalar(seli[:, 1, :], seli[:, 0, :], 7, None, ALU.logical_shift_right)
            k(dve.tensor_scalar(seli[:, 2, :], seli[:, 0, :], P - 1, None, ALU.bitwise_and))
            dve.tensor_copy(sel[:, 1, :], seli[:, 1, :])
            k(dve.tensor_copy(sel[:, 2, :], seli[:, 2, :]))
            dve.wait_ge(m.s["consts"], 2)
            for i in range(G):
                if i >= 2:
                    dve.wait_ge(m.s["table"], i - 1)
                dve.tensor_scalar(hot[:, i % 2, 0:P], m.iota_row[:], sel[:, 2, i:i + 1], None, ALU.is_equal)
                dve.tensor_scalar(hot[:, i % 2, P:P + MAX1], m.iota_row[:, 0:MAX1], sel[:, 1, i:i + 1],
                                  m.tokcol[:, i:i + 1], ALU.is_equal, ALU.mult).then_inc(m.s["onehot"], 1)
            for n in range(4):
                low(n)
            dve.wait_ge(m.s["table"], G)
            k(dve.tensor_scalar(tabf[:, 0, :], psR[:], 0.0, m.pad_row[:, 0:1], ALU.is_equal, ALU.mult))
            k(dve.scalar_tensor_tensor(out=tabf[:, 1, :], in0=psR[:], scalar=-1.0, in1=tabf[:, 0, :],
                                       op0=ALU.add, op1=ALU.add))
            dve.tensor_copy(m.scatter1[:], tabf[:, 1, :])
            k(dve.tensor_scalar(tabf[:, 2, :], tabf[:, 1, :], float(TOKENS - 1), None, ALU.min))
            dve.tensor_copy(m.gather1[:], tabf[:, 2, :])
            k(dve.tensor_tensor(cmp[:], m.iota_row[0:1, 0:MAX1].rearrange("p (n o) -> p n o", o=1).to_broadcast([1, MAX1, E1]),
                                row[0:1, 4:5, :].to_broadcast([1, MAX1, E1]), ALU.is_ge))
            k(dve.tensor_reduce(tbf[:, 0, :], cmp[:], AX.X, ALU.add))
            k(dve.tensor_scalar(tbf[:, 0, :], tbf[:, 0, :], float(E1 - 1), None, ALU.min))
            k(dve.tensor_scalar(tbf[:, 1, :], row[0:1, 4, E1 - 1:E1].to_broadcast([1, MAX1]), float(1 - 2 * MIN_PAIRS), None, ALU.add))
            k(dve.tensor_copy(m.tab1[:], tbf[:]))
            k(dve.tensor_scalar(m.tab1[:, 1, :], m.tab1[:, 1, :], 1, None, ALU.logical_shift_right))
            for n in range(4, E1 * C):
                low(n)



def build(nc, m):
    with ExitStack() as top:
        m.sb = lambda name, shape, dt, stack: stack.enter_context(nc.sbuf_tensor(name, shape, dt))
        tensors(nc, m, top)
        m.s = {n: top.enter_context(nc.semaphore(n)) for n in (
            "consts", "chain0", "chain1", "ctx_turned", "ctx_hi", "ctx_split", "gate_turned", "gate_done", "counted",
            "onehot", "table", "tid_loaded", "norm_loaded", "gate_loaded", "sh_loaded", "sh_hi", "prefix", "zero_pad",
            "ctx_loaded0", "carried", "ctx_loaded1")}
        m.carry = lambda eng: eng.sem_inc(m.s["carried"], 1)
        with ExitStack() as st:
            m.cth = m.sb("cth", [P, E1, C, D], F32R, st)
            m.ctl = m.sb("ctl", [P, E1, C, D], F32R, st)
            setup(nc, m)
            context(nc, m)
        with ExitStack() as st:
            m.wh = m.sb("wh", [P, W_SETS, HL, D], F32R, st)
            m.wl = m.sb("wl", [P, W_SETS, HL, D], F32R, st)
            m.raw = m.sb("raw", [P, 2, HL, D], F32, st)
            shared_and_routing(nc, m)
            experts(nc, m)
        overflow(nc, m)


def context(nc, m):
    with ExitStack() as st:
        def sb(name, shape, dt=F32):
            return m.sb(name, shape, dt, st)

        def ps(name, shape):
            return st.enter_context(nc.psum_tensor(name, shape, F32))

        s = semaphores(nc, st, "c_", (
            "gx0", "gx1", "xr", "stat1", "mv1", "var1", "rstd1", "h", "t1", "t1hi", "t1lo", "g1", "sil", "a",
            "t2", "t2hi", "t2lo", "g2", "x1", "stat2", "mv2", "var2", "rstd2", "x2", "ss", "ms", "rrms", "hn",
            "t3", "t3c", "lg", "lc", "base", "sh0", "sh1", "sb0", "sb1", "gi", "shi", "sbi"))
        gx, sh, sbl = (s["gx0"], s["gx1"]), (s["sh0"], s["sh1"]), (s["sb0"], s["sb1"])
        xg = sb("c_xg", [P, 2, D])
        xr = sb("c_xr", [P, 4, D])
        h = sb("c_h", [P, 2, D])
        hth = sb("c_hth", [P, 2, C, P], F32R)
        htl = sb("c_htl", [P, 2, C, P], F32R)
        a = sb("c_a", [P, 2, D])
        ath = sb("c_ath", [P, 2, C, P], F32R)
        atl = sb("c_atl", [P, 2, C, P], F32R)
        x1 = sb("c_x1", [P, 2, D])
        x2 = sb("c_x2", [P, 2, D])
        hn = sb("c_hn", [P, 2, D])
        hnt = sb("c_hnt", [P, 2, C, P])
        bl = sb("c_bl", [P, 2, D + E2])
        sq = sb("c_sq", [P, D])
        stat = sb("c_stat", [P, 2, 6])
        mv = sb("c_mv", [P, 2, 2, 2])
        rs = sb("c_rs", [P, 3, 2, 2])
        ss = sb("c_ss", [P, 2])
        gidx = sb("c_gidx", [P, 2], I32)
        hidx = sb("c_hidx", [P, 2], I32)
        bidx = sb("c_bidx", [P, 2], I32)
        ps_t1, ps_t2, ps_t3, ps_z = (ps(n, [P, D]) for n in ("ps_t1", "ps_t2", "ps_t3", "ps_z"))
        ps_y = [ps(f"ps_y{i}", [P, D]) for i in range(2)]
        ps_l = ps("ps_l", [P, E2])
        block = st.enter_context(nc.Block())

        @block.gpsimd
        def _(pool):
            pairs = number_of_pairs(pool, m.tab1[0:1, 1, 0:1], MAX1)

            def power(which, t, src, offset, scale, sem_mid, sem_out):
                m.carry(pool)
                nc.gpsimd.tensor_scalar(rs[:, which, t.par, 0:1], src, scale, offset, ALU.mult, ALU.add).then_inc(sem_mid, 1)
                pool.wait_ge(sem_mid, t.n + 1)
                nc.gpsimd.tensor_tensor(rs[:, which, t.par, 1:2], rs[:, which, t.par, 0:1], m.minus_half[:], ALU.pow).then_inc(sem_out, 1)

            def emit(part, t):
                if part == "gather":
                    wait(pool, s["xr"], t.n - 1)
                    wait(pool, s["h"], t.n - 1)
                    wait(pool, gx[t.par], 16 * t.half)
                    m.carry(pool)
                    nc.gpsimd.tensor_copy(gidx[:, t.par:t.par + 1], m.gather1[:, bass.ds(t.n, 1)]).then_inc(s["gi"], 1)
                    pool.wait_ge(s["gi"], t.n + 1)
                    m.carry(pool)
                    pool.indirect_dma_start(xg[:, t.par], None, m.x, bass.IndirectOffsetOnAxis(ap=gidx[:, t.par:t.par + 1], axis=0)
                                            ).then_inc(gx[t.par], 16)
                elif part == "rstd1":
                    pool.wait_ge(s["mv1"], t.n + 1)
                    power(0, t, mv[:, 0, t.par, 1:2], LN_EPS, 1.0, s["var1"], s["rstd1"])
                elif part == "rstd2":
                    pool.wait_ge(s["mv2"], t.n + 1)
                    power(1, t, mv[:, 1, t.par, 1:2], LN_EPS, 1.0, s["var2"], s["rstd2"])
                elif part == "rrms":
                    pool.wait_ge(s["ss"], t.n + 1)
                    power(2, t, ss[:, t.par:t.par + 1], RMS_EPS, 1.0 / D, s["ms"], s["rrms"])
                elif part == "base":
                    pool.wait_ge(s["x2"], t.n + 1)
                    wait(pool, sbl[t.par], 16 * t.half)
                    nc.gpsimd.tensor_tensor(bl[:, t.par, 0:D], x1[:, t.par], x2[:, t.par], ALU.add).then_inc(s["base"], 1)
                elif part == "scatter_hn":
                    wait(pool, sh[t.par], 16 * t.half)
                    m.carry(pool)
                    nc.gpsimd.tensor_copy(hidx[:, t.par:t.par + 1], m.scatter1[:, bass.ds(t.n, 1)]).then_inc(s["shi"], 1)
                    pool.wait_ge(s["shi"], t.n + 1)
                    pool.wait_ge(s["hn"], t.n + 1)
                    m.carry(pool)
                    pool.indirect_dma_start(m.hn_dram, bass.IndirectOffsetOnAxis(ap=hidx[:, t.par:t.par + 1], axis=0), hn[:, t.par], None,
                                            bounds_check=TOKENS - 1, oob_is_err=False).then_inc(sh[t.par], 16)
                elif part == "scatter_base":
                    wait(pool, sbl[t.par], 16 * t.half)
                    m.carry(pool)
                    nc.gpsimd.tensor_copy(bidx[:, t.par:t.par + 1], m.scatter1[:, bass.ds(t.n, 1)]).then_inc(s["sbi"], 1)
                    pool.wait_ge(s["sbi"], t.n + 1)
                    pool.wait_ge(s["lc"], t.n + 1)
                    pool.wait_ge(s["base"], t.n + 1)
                    m.carry(pool)
                    pool.indirect_dma_start(m.bl_dram, bass.IndirectOffsetOnAxis(ap=bidx[:, t.par:t.par + 1], axis=0), bl[:, t.par], None,
                                            bounds_check=TOKENS - 1, oob_is_err=False).then_inc(sbl[t.par], 16)

            pipeline(pool, pairs, [("gather", 0), ("rstd2", 4), ("rstd1", 1), ("rrms", 4), ("scatter_hn", 5),
                                   ("base", 5), ("scatter_base", 6)], emit)
            for q in (*sh, *sbl):
                pool.wait_ge(q, 16 * pairs)
            pool.sem_inc(s["gi"], 1)

        @block.tensor
        def _(pe):
            pairs = number_of_pairs(pe, m.tab1[0:1, 1, 0:1], MAX1)

            def expert(t):
                return pe.value_load(m.tab1[0:1, 0, bass.ds(t.n, 1)], min_val=0, max_val=E1 - 1)

            def turn(dst, src):
                for c in range(C):
                    mm = pe.transpose(dst[:, c * P:(c + 1) * P], src[:, c * P:(c + 1) * P], m.ident[:])
                return mm

            def product(dst, hi, lo, t):
                e = bass.ds(expert(t), 1)
                for c in range(C):
                    mm = three_products(pe, dst[:], hi[:, t.par, c], lo[:, t.par, c], m.cth[:, e, c, :], m.ctl[:, e, c, :],
                                        c == 0, c == C - 1)
                return mm

            def emit(part, t):
                if part == "t1":
                    pe.wait_ge(s["h"], t.n + 1)
                    wait(pe, s["t1lo"], t.n)
                    turn(ps_t1, h[:, t.par]).then_inc(s["t1"], 1)
                elif part == "g1":
                    pe.wait_ge(s["t1lo"], t.n + 1)
                    wait(pe, s["a"], t.n)
                    product(ps_z, hth, htl, t).then_inc(s["g1"], 1)
                elif part == "t2":
                    pe.wait_ge(s["a"], t.n + 1)
                    wait(pe, s["t2lo"], t.n)
                    turn(ps_t2, a[:, t.par]).then_inc(s["t2"], 1)
                elif part == "g2":
                    pe.wait_ge(s["t2lo"], t.n + 1)
                    wait(pe, s["x1"], t.n - 1)
                    product(ps_y[t.par], ath, atl, t).then_inc(s["g2"], 1)
                elif part == "t3":
                    pe.wait_ge(s["hn"], t.n + 1)
                    wait(pe, s["t3c"], t.n)
                    turn(ps_t3, hn[:, t.par]).then_inc(s["t3"], 1)
                elif part == "logits":
                    pe.wait_ge(s["t3c"], t.n + 1)
                    wait(pe, s["lc"], t.n)
                    for c in range(C):
                        mm = pe.matmul(ps_l[:], hnt[:, t.par, c], m.gT[:, c, :], start=(c == 0), stop=(c == C - 1))
                    mm.then_inc(s["lg"], 1)

            pipeline(pe, pairs, [("t1", 0), ("g2", 2), ("t2", 1), ("t3", 3), ("g1", 0), ("logits", 3)], emit)

        @block.scalar
        def _(act):
            pairs = number_of_pairs(act, m.tab1[0:1, 1, 0:1], MAX1)

            def emit(part, t):
                if part == "keep":
                    act.wait_ge(gx[t.par], 16 * (t.half + 1))
                    wait(act, s["x1"], t.n - 3)
                    kept = xr[:, bass.ds(t.n % 4, 1), :]
                    nc.scalar.activation(kept, xg[:, t.par:t.par + 1, :], ACT.Copy).then_inc(s["xr"], 1)
                elif part == "silu":
                    act.wait_ge(s["g1"], t.n + 1)
                    wait(act, s["t2"], t.n - 1)
                    nc.scalar.activation(a[:, t.par], ps_z[:], ACT.Silu).then_inc(s["sil"], 1)
                elif part == "t1hi":
                    act.wait_ge(s["t1"], t.n + 1)
                    wait(act, s["g1"], t.n - 1)
                    nc.scalar.activation(hth[:, t.par].rearrange("p c n -> p (c n)"), ps_t1[:], ACT.Copy).then_inc(s["t1hi"], 1)
                elif part == "t2hi":
                    act.wait_ge(s["t2"], t.n + 1)
                    wait(act, s["g2"], t.n - 1)
                    nc.scalar.activation(ath[:, t.par].rearrange("p c n -> p (c n)"), ps_t2[:], ACT.Copy).then_inc(s["t2hi"], 1)
                elif part == "squares":
                    act.wait_ge(s["x2"], t.n + 1)
                    nc.scalar.activation(sq[:], x2[:, t.par], ACT.Square, accum_out=ss[:, t.par:t.par + 1]).then_inc(s["ss"], 1)
                elif part == "t3c":
                    act.wait_ge(s["t3"], t.n + 1)
                    wait(act, s["lg"], t.n - 1)
                    nc.scalar.activation(hnt[:, t.par].rearrange("p c n -> p (c n)"), ps_t3[:], ACT.Copy).then_inc(s["t3c"], 1)
                elif part == "logits":
                    act.wait_ge(s["lg"], t.n + 1)
                    wait(act, sbl[t.par], 16 * t.half)
                    nc.scalar.activation(bl[:, t.par, D:D + E2], ps_l[:], ACT.Copy).then_inc(s["lc"], 1)

            pipeline(act, pairs, [("keep", 0), ("silu", 1), ("t1hi", 0), ("t2hi", 1), ("squares", 2), ("t3c", 3),
                                  ("logits", 3)], emit)

        @block.vector
        def _(dve):
            pairs = number_of_pairs(dve, m.tab1[0:1, 1, 0:1], MAX1)

            def emit(part, t):
                if part == "stats1":
                    dve.wait_ge(gx[t.par], 16 * (t.half + 1))
                    dve.bn_stats(stat[:, 0, :], xg[:, t.par]).then_inc(s["stat1"], 1)
                    dve.wait_ge(s["stat1"], t.n + 1)
                    m.carry(dve)
                    dve.bn_aggr(mv[:, 0, t.par, :], stat[:, 0, :]).then_inc(s["mv1"], 1)
                elif part == "h":
                    dve.wait_ge(s["rstd1"], t.n + 1)
                    wait(dve, s["t1"], t.n - 1)
                    dve.tensor_scalar(h[:, t.par], xg[:, t.par], mv[:, 0, t.par, 0:1], rs[:, 0, t.par, 1:2],
                                      ALU.subtract, ALU.mult).then_inc(s["h"], 1)
                elif part == "a":
                    dve.wait_ge(s["sil"], t.n + 1)
                    dve.tensor_tensor(a[:, t.par], a[:, t.par], ps_z[:], ALU.mult).then_inc(s["a"], 1)
                elif part == "t1lo":
                    dve.wait_ge(s["t1hi"], t.n + 1)
                    dve.tensor_tensor(htl[:, t.par].rearrange("p c n -> p (c n)"), ps_t1[:],
                                      hth[:, t.par].rearrange("p c n -> p (c n)").bitcast(F32), ALU.subtract).then_inc(s["t1lo"], 1)
                elif part == "t2lo":
                    dve.wait_ge(s["t2hi"], t.n + 1)
                    dve.tensor_tensor(atl[:, t.par].rearrange("p c n -> p (c n)"), ps_t2[:],
                                      ath[:, t.par].rearrange("p c n -> p (c n)").bitcast(F32), ALU.subtract).then_inc(s["t2lo"], 1)
                elif part == "x1":
                    dve.wait_ge(s["g2"], t.n + 1)
                    dve.wait_ge(s["xr"], t.n + 1)
                    wait(dve, s["base"], t.n - 1)
                    kept = xr[:, bass.ds(t.n % 4, 1), :]
                    dve.tensor_tensor(x1[:, t.par:t.par + 1, :], kept, ps_y[t.par][:].rearrange("p (o n) -> p o n", o=1),
                                      ALU.add).then_inc(s["x1"], 1)
                    dve.wait_ge(s["x1"], t.n + 1)
                    dve.bn_stats(stat[:, 1, :], x1[:, t.par]).then_inc(s["stat2"], 1)
                    dve.wait_ge(s["stat2"], t.n + 1)
                    m.carry(dve)
                    dve.bn_aggr(mv[:, 1, t.par, :], stat[:, 1, :]).then_inc(s["mv2"], 1)
                elif part == "x2":
                    dve.wait_ge(s["rstd2"], t.n + 1)
                    dve.tensor_scalar(x2[:, t.par], x1[:, t.par], mv[:, 1, t.par, 0:1], rs[:, 1, t.par, 1:2],
                                      ALU.subtract, ALU.mult).then_inc(s["x2"], 1)
                elif part == "hn":
                    dve.wait_ge(s["rrms"], t.n + 1)
                    wait(dve, s["t3"], t.n - 1)
                    wait(dve, sh[t.par], 16 * t.half)
                    dve.scalar_tensor_tensor(out=hn[:, t.par], in0=x2[:, t.par], scalar=rs[:, 2, t.par, 1:2], in1=m.normw[:],
                                             op0=ALU.mult, op1=ALU.mult).then_inc(s["hn"], 1)

            pipeline(dve, pairs, [("a", 2), ("t1lo", 1), ("t2lo", 2), ("x1", 3), ("stats1", 0), ("x2", 3), ("h", 0),
                                  ("hn", 3)], emit)



def shared_and_routing(nc, m):
    with ExitStack() as st:
        def sb(name, shape, dt=F32):
            return m.sb(name, shape, dt, st)

        def ps(name, shape):
            return st.enter_context(nc.psum_tensor(name, shape, F32))

        s = semaphores(nc, st, "s_", (
            "gx0", "gx1", "bs0", "bs1", "t1", "t1raw", "t1hi", "t1lo", "g1", "u", "sil", "a", "t2", "t2raw", "t2hi",
            "t2lo", "g2", "y", "o", "st0", "st1", "logits", "chain", "shifted", "exp", "counted", "prefix", "hot",
            "table", "raw0", "raw1", "w_hi", "w_lo"))
        gx, bsl, stl = (s["gx0"], s["gx1"]), (s["bs0"], s["bs1"]), (s["st0"], s["st1"])
        SKEW_HOT = 6
        xg = sb("s_xg", [P, 2, D])
        bs = sb("s_bs", [P, 2, D])
        traw = sb("s_traw", [P, 2, D])
        xth = sb("s_xth", [P, 2, C, P], F32R)
        xtl = sb("s_xtl", [P, 2, C, P], F32R)
        sg_ = sb("s_silu", [P, 2, INNER])
        u_ = sb("s_u", [P, 2, INNER])
        a = sb("s_a", [P, 2, INNER])
        araw = sb("s_araw", [P, 2, INNER])
        ath = sb("s_ath", [P, 2, CI, P], F32R)
        atl = sb("s_atl", [P, 2, CI, P], F32R)
        y = sb("s_y", [P, 2, D])
        o = sb("s_o", [P, 2, D])
        prob = sb("r_prob", [P, G, E2])
        red = sb("r_red", [P, 4, G])
        top8 = sb("r_top8", [P, G, 8])
        idx8 = sb("r_idx8", [P, G, 8], U32)
        eid = sb("r_eid", [P, G, 8])
        oh = sb("r_oh", [P, K, G, E2])
        M = sb("r_m", [P, G, E2])
        rank = sb("r_rank", [P, G, E2])
        tmp = sb("r_tmp", [P, G, E2])
        row = sb("r_row", [P, 8, E2])
        rowi = sb("r_rowi", [P, E2], I32)
        sel = sb("r_sel", [P, 3, G, K])
        seli = sb("r_seli", [P, 3, G, K], I32)
        ovr = sb("r_ovr", [P, 2, K, G])
        hot = sb("r_hot", [P, K, P + 2 * MAX2])
        tabf = sb("r_tabf", [P, 3, MAX2])
        tbf = sb("r_tbf", [1, 6, 2 * STEP_PAIRS + 2])
        ps_t1, ps_t2, ps_gu = (ps(n, [P, D]) for n in ("sps_t1", "sps_t2", "sps_gu"))
        ps_y = [ps(f"sps_y{i}", [P, D]) for i in range(2)]
        ps_p = ps("sps_p", [P, 2, E2])
        ps_r = ps("sps_r", [P, 2 * MAX2])
        block = st.enter_context(nc.Block())
        pairs = TOKENS // P // 2

        @block.sync
        def _(sp):
            sp.dma_start(prob[:], m.bl_dram.rearrange("(p g) n -> p g n", g=G)[:, :, D:D + E2]).then_inc(s["logits"], 16)
            raw_sem = (s["raw0"], s["raw1"])
            for e in range(2):
                sp.dma_start(m.raw[:, e, 0:C], m.w13[e].rearrange("(c p) n -> p c n", p=P)).then_inc(raw_sem[e], 16)
                sp.dma_start(m.raw[:, e, C:HL], m.w2[e].rearrange("(c p) n -> p c n", p=P)).then_inc(raw_sem[e], 16)

            def emit(part, t):
                rows = bass.ds(t.n * P, P)
                if part == "load":
                    wait(sp, s["t1"], t.n - 1)
                    sp.dma_start(xg[:, t.par], m.hn_dram[rows, :]).then_inc(gx[t.par], 16)
                elif part == "load_base":
                    wait(sp, s["o"], t.n - 1)
                    sp.dma_start(bs[:, t.par], m.bl_dram[rows, 0:D]).then_inc(bsl[t.par], 16)
                elif part == "store":
                    sp.wait_ge(s["o"], t.n + 1)
                    sp.dma_start(m.out[rows, :], o[:, t.par]).then_inc(stl[t.par], 16)

            pipeline(sp, pairs, [("load", 0), ("store", 3), ("load_base", 1)], emit)
            for q in stl:
                sp.wait_ge(q, 16 * pairs)
            sp.wait_ge(s["w_lo"], 1)
            sp.dma_start(m.raw[:, 0, 0:C], m.w13[2].rearrange("(c p) n -> p c n", p=P)).then_inc(raw_sem[0], 16)
            sp.dma_start(m.raw[:, 0, C:HL], m.w2[2].rearrange("(c p) n -> p c n", p=P)).then_inc(raw_sem[0], 16)

        @block.gpsimd
        def _(pool):
            def emit(part, t):
                if part == "a":
                    pool.wait_ge(s["u"], t.n + 1)
                    wait(pool, s["t2"], t.n - 1)
                    nc.gpsimd.tensor_tensor(a[:, t.par], sg_[:, t.par], u_[:, t.par], ALU.mult).then_inc(s["a"], 1)
                elif part == "t1lo":
                    pool.wait_ge(s["t1hi"], t.n + 1)
                    wait(pool, s["g1"], t.n - 1)
                    nc.gpsimd.tensor_tensor(xtl[:, t.par].rearrange("p c n -> p (c n)"), traw[:, t.par],
                                            xth[:, t.par].rearrange("p c n -> p (c n)").bitcast(F32), ALU.subtract).then_inc(s["t1lo"], 1)
                elif part == "t2lo":
                    pool.wait_ge(s["t2hi"], t.n + 1)
                    wait(pool, s["g2"], t.n - 1)
                    nc.gpsimd.tensor_tensor(atl[:, t.par].rearrange("p c n -> p (c n)"), araw[:, t.par],
                                            ath[:, t.par].rearrange("p c n -> p (c n)").bitcast(F32), ALU.subtract).then_inc(s["t2lo"], 1)
                elif part == "o":
                    pool.wait_ge(s["y"], t.n + 1)
                    pool.wait_ge(bsl[t.par], 16 * (t.half + 1))
                    wait(pool, stl[t.par], 16 * t.half)
                    nc.gpsimd.tensor_tensor(o[:, t.par], y[:, t.par], bs[:, t.par], ALU.add).then_inc(s["o"], 1)

            pipeline(pool, pairs, [("a", 1), ("t1lo", 0), ("t2lo", 1), ("o", 2)], emit)
            for e in range(W_SETS):
                pool.wait_ge(s["w_hi"], e + 1)
                nc.gpsimd.tensor_tensor(m.wl[:, e], m.raw[:, e % 2], m.wh[:, e].bitcast(F32), ALU.subtract).then_inc(s["w_lo"], 1)

        @block.tensor
        def _(pe):
            def turn(dst, src, n):
                for c in range(n):
                    mm = pe.transpose(dst[:, c * P:(c + 1) * P], src[:, c * P:(c + 1) * P], m.ident[:])
                return mm

            def emit(part, t):
                if part == "t1":
                    pe.wait_ge(gx[t.par], 16 * (t.half + 1))
                    wait(pe, s["t1hi"], t.n)
                    turn(ps_t1, xg[:, t.par], C).then_inc(s["t1"], 1)
                elif part == "g1":
                    pe.wait_ge(s["t1lo"], t.n + 1)
                    wait(pe, s["u"], t.n)
                    for c in range(C):
                        mm = three_products(pe, ps_gu[:], xth[:, t.par, c], xtl[:, t.par, c], m.wh_s[:, c], m.wl_s[:, c],
                                            c == 0, c == C - 1)
                    mm.then_inc(s["g1"], 1)
                elif part == "t2":
                    pe.wait_ge(s["a"], t.n + 1)
                    wait(pe, s["t2hi"], t.n)
                    turn(ps_t2, a[:, t.par], CI).then_inc(s["t2"], 1)
                elif part == "g2":
                    pe.wait_ge(s["t2lo"], t.n + 1)
                    wait(pe, s["y"], t.n - 1)
                    for c in range(CI):
                        mm = three_products(pe, ps_y[t.par][:], ath[:, t.par, c], atl[:, t.par, c], m.wh_s[:, C + c],
                                            m.wl_s[:, C + c], c == 0, c == CI - 1)
                    mm.then_inc(s["g2"], 1)
                elif part == "hot":
                    first = isinstance(t.n, int) and t.n == 0
                    if first:
                        pe.wait_ge(s["counted"], 1)
                        pe.matmul(ps_p[:, 0, :], m.before[:], row[:, 0, :], start=True, stop=True)
                        pe.matmul(ps_p[:, 1, :], m.ones[:], row[:, 0, :], start=True, stop=True).then_inc(s["prefix"], 1)
                    for k in range(K):
                        pe.wait_ge(s["hot"], t.n * K + k + 1)
                        pe.matmul(ps_r[:], hot[:, k, 0:P], hot[:, k, P:], start=(first and k == 0), stop=False,
                                  skip_group_check=True).then_inc(s["table"], 1)

            pipeline(pe, pairs, [("t1", 0), ("g2", 2), ("t2", 1), ("g1", 0), ("hot", SKEW_HOT)], emit)

        @block.scalar
        def _(act):
            act.wait_ge(s["shifted"], 1)
            nc.scalar.activation(prob[:], prob[:], ACT.Exp).then_inc(s["exp"], 1)

            def emit(part, t):
                if part == "silu":
                    act.wait_ge(s["g1"], t.n + 1)
                    wait(act, s["a"], t.n - 1)
                    nc.scalar.activation(sg_[:, t.par], ps_gu[:, 0:INNER], ACT.Silu)
                    nc.scalar.activation(u_[:, t.par], ps_gu[:, INNER:D], ACT.Copy).then_inc(s["u"], 1)
                elif part == "t1":
                    act.wait_ge(s["t1"], t.n + 1)
                    wait(act, s["t1lo"], t.n - 1)
                    nc.scalar.activation(traw[:, t.par], ps_t1[:], ACT.Copy)
                    wait(act, s["g1"], t.n - 1)
                    nc.scalar.activation(xth[:, t.par].rearrange("p c n -> p (c n)"), ps_t1[:], ACT.Copy).then_inc(s["t1hi"], 1)
                elif part == "t2":
                    act.wait_ge(s["t2"], t.n + 1)
                    wait(act, s["t2lo"], t.n - 1)
                    nc.scalar.activation(araw[:, t.par], ps_t2[:, 0:INNER], ACT.Copy)
                    wait(act, s["g2"], t.n - 1)
                    nc.scalar.activation(ath[:, t.par].rearrange("p c n -> p (c n)"), ps_t2[:, 0:INNER], ACT.Copy).then_inc(s["t2hi"], 1)
                elif part == "y":
                    act.wait_ge(s["g2"], t.n + 1)
                    wait(act, s["o"], t.n - 1)
                    nc.scalar.activation(y[:, t.par], ps_y[t.par][:], ACT.Copy).then_inc(s["y"], 1)

            pipeline(act, pairs, [("silu", 1), ("t1", 0), ("y", 2), ("t2", 1)], emit)
            for e in range(W_SETS):
                act.wait_ge((s["raw0"], s["raw1"])[e % 2], 32 * (e // 2 + 1))
                nc.scalar.activation(m.wh[:, e], m.raw[:, e % 2], ACT.Copy).then_inc(s["w_hi"], 1)

        @block.vector
        def _(dve):
            k_ = Chain(dve, s["chain"])
            flat = "p g e -> p (g e)"

            def over_experts(ap):
                return ap.rearrange("p (g o) -> p g o", o=1).to_broadcast([P, G, E2])

            def over_tokens(ap):
                return ap.to_broadcast([P, G, E2])

            dve.wait_ge(s["logits"], 16)
            k_(dve.tensor_reduce(red[:, 0, :], prob[:], AX.X, ALU.max))
            dve.tensor_tensor(prob[:], prob[:], over_experts(red[:, 0, :]), ALU.subtract).then_inc(s["shifted"], 1)
            dve.wait_ge(s["exp"], 1)
            k_(dve.tensor_reduce(red[:, 1, :], prob[:], AX.X, ALU.add))
            k_(dve.reciprocal(red[:, 2, :], red[:, 1, :]))
            k_(dve.tensor_tensor(prob[:], prob[:], over_experts(red[:, 2, :]), ALU.mult))
            for g in range(G):
                last = dve.max(top8[:, g, :], prob[:, g, :])
            k_(last)
            for g in range(G):
                last = dve.max_index(idx8[:, g, :], top8[:, g, :], prob[:, g, :])
            k_(last)
            dve.tensor_copy(eid[:], idx8[:])
            k_(dve.tensor_reduce(red[:, 3, :], top8[:, :, 0:K], AX.X, ALU.add))
            k_(dve.reciprocal(red[:, 3, :], red[:, 3, :]))
            dve.tensor_tensor(m.topw[:], top8[:, :, 0:K], red[:, 3, :].rearrange("p (g o) -> p g o", o=1).to_broadcast([P, G, K]), ALU.mult)
            for k in range(K):
                last = dve.tensor_tensor(oh[:, k], m.iota_row[:, 0:E2].rearrange("p (o e) -> p o e", o=1).to_broadcast([P, G, E2]),
                                         eid[:, :, k:k + 1].to_broadcast([P, G, E2]), ALU.is_equal)
            k_(last)
            k_(dve.tensor_tensor(M[:], oh[:, 0], oh[:, 1], ALU.add))
            k_(dve.tensor_tensor(tmp[:], oh[:, 2], oh[:, 3], ALU.add))
            k_(dve.tensor_tensor(M[:], M[:], tmp[:], ALU.add))
            dve.tensor_reduce(row[:, 0, :], M[:].rearrange("p g e -> p e g"), AX.X, ALU.add).then_inc(s["counted"], 1)
            k_(dve.memset(rank[:, 0, :], 0.0))
            for g in range(1, G):
                k_(dve.tensor_tensor(rank[:, g, :], rank[:, g - 1, :], M[:, g - 1, :], ALU.add))
            dve.wait_ge(s["prefix"], 1)
            k_(dve.tensor_scalar(row[:, 1, :], ps_p[:, 1, :], float(m.cap), float(P - 1), ALU.min, ALU.add))
            k_(dve.tensor_copy(rowi[:], row[:, 1, :]))
            k_(dve.tensor_scalar(rowi[:], rowi[:], 7, None, ALU.logical_shift_right))
            k_(dve.tensor_copy(row[:, 2, :], rowi[:]))
            k_(dve.tensor_scalar(row[:, 2, :], row[:, 2, :], 1.0, None, ALU.max))
            k_(dve.memset(row[:, 3, :], 0.0))
            k_(dve.tensor_tensor_scan(row[:, 4, :], row[:, 2, :], row[:, 3, :], 0.0, ALU.add, ALU.add))
            k_(dve.tensor_tensor(row[:, 5, :], row[:, 4, :], row[:, 2, :], ALU.subtract))
            k_(dve.tensor_copy(row[:, 7, :], ps_p[:, 0, :]))
            k_(dve.tensor_tensor(rank[:], rank[:], over_tokens(row[:, 7:8, :]), ALU.add))
            k_(dve.tensor_scalar(tmp[:], rank[:], float(m.cap), float(MAX2 * P), ALU.is_ge, ALU.mult))
            k_(dve.tensor_scalar(row[:, 6, :], row[:, 5, :], float(P), None, ALU.mult))
            k_(dve.tensor_tensor(rank[:], rank[:], over_tokens(row[:, 6:7, :]), ALU.add))
            k_(dve.tensor_tensor(rank[:], rank[:], tmp[:], ALU.add))
            k_(dve.tensor_scalar(rank[:], rank[:], float(MAX2 * P), None, ALU.min))
            for k in range(K):
                k_(dve.tensor_tensor(tmp[:], oh[:, k], rank[:], ALU.mult))
                k_(dve.tensor_reduce(sel[:, 0, :, k], tmp[:], AX.X, ALU.add))
            k_(dve.tensor_copy(seli[:, 0], sel[:, 0]))
            dve.tensor_scalar(seli[:, 1], seli[:, 0], 7, None, ALU.logical_shift_right)
            k_(dve.tensor_scalar(seli[:, 2], seli[:, 0], P - 1, None, ALU.bitwise_and))
            dve.tensor_copy(sel[:, 1], seli[:, 1])
            k_(dve.tensor_copy(sel[:, 2], seli[:, 2]))

            def one_hot(g):
                for k in range(K):
                    column = lambda t: t[:, bass.ds(g, 1), k:k + 1].rearrange("p a b -> p (a b)")
                    wait(dve, s["table"], (g - 1) * K + k + 1)
                    dve.tensor_scalar(hot[:, k, 0:P], m.iota_row[:], column(sel[:, 2]), None, ALU.is_equal)
                    dve.tensor_scalar(hot[:, k, P:P + MAX2], m.iota_row[:, 0:MAX2], column(sel[:, 1]),
                                      m.tokcol[:, bass.ds(g, 1)], ALU.is_equal, ALU.mult)
                    dve.tensor_scalar(hot[:, k, P + MAX2:], m.iota_row[:, 0:MAX2], column(sel[:, 1]),
                                      column(m.topw), ALU.is_equal, ALU.mult).then_inc(s["hot"], 1)

            one_hot(0)
            with dve.Fori(1, G) as g:
                one_hot(g)

            k_(dve.tensor_scalar(row[:, 6, :], row[:, 4, :], -1.0, None, ALU.add))
            k_(dve.tensor_scalar(red[:, 0, :], m.tokcol[:], m.pad_row[:, 0:1], None, ALU.subtract))
            for k in range(K):
                k_(dve.tensor_tensor(tmp[:], oh[:, k], over_tokens(row[:, 6:7, :]), ALU.mult))
                k_(dve.tensor_reduce(ovr[:, 0, k, :], tmp[:], AX.X, ALU.add))
                k_(dve.tensor_scalar(red[:, 1, :], sel[:, 0, :, k], float(MAX2 * P), None, ALU.is_equal))
                k_(dve.tensor_tensor(ovr[:, 1, k, :], red[:, 1, :], red[:, 0, :], ALU.mult))
            k_(dve.tensor_scalar(ovr[:, 1], ovr[:, 1], m.pad_row[:, 0:1], -1.0, ALU.add, ALU.add))
            dve.tensor_copy(m.over_row[:], ovr[:, 0])
            dve.tensor_copy(m.over_tok[:], ovr[:, 1])
            k_(dve.tensor_copy(m.topk[:], m.topw[:].rearrange("p g k -> p k g")))
            k_(dve.memset(tbf[:], 0.0))
            for first, n in ((0, STEP_PAIRS), (STEP_PAIRS, STEP_PAIRS - 1)):
                cmp = oh[0:1].rearrange("p k g e -> p (k g e)")[:, 0:n * E2].rearrange("p (n e) -> p n e", e=E2)
                k_(dve.tensor_tensor(cmp, m.iota_row[0:1, first:first + n].rearrange("p (n o) -> p n o", o=1).to_broadcast([1, n, E2]),
                                     row[0:1, 4:5, :].to_broadcast([1, n, E2]), ALU.is_ge))
                k_(dve.tensor_reduce(tbf[:, 0, LOOK_BACK + first:LOOK_BACK + first + n], cmp, AX.X, ALU.add))
            k_(dve.tensor_scalar(tbf[:, 0, :], tbf[:, 0, :], float(E2 - 1), None, ALU.min))
            k_(dve.tensor_tensor(tbf[:, 1, LOOK_BACK + 1:], tbf[:, 0, LOOK_BACK + 1:], tbf[:, 0, LOOK_BACK:-1], ALU.subtract))
            k_(dve.tensor_scalar(tbf[:, 2, :], tbf[:, 0, :], 2.0, None, ALU.add))
            k_(dve.tensor_tensor(tbf[:, 1, :], tbf[:, 1, :], tbf[:, 2, :], ALU.mult))
            k_(dve.tensor_scalar(tbf[:, 2, :], tbf[:, 1, :], float(E2 - 1), None, ALU.is_le))
            k_(dve.tensor_tensor(tbf[:, 1, :], tbf[:, 1, :], tbf[:, 2, :], ALU.mult))
            for r in range(2):
                two = tbf[:, r, :].rearrange("p (q b) -> p b q", b=2)
                digits = (two[:, 0, 0:STEP_PAIRS], two[:, 1, 0:STEP_PAIRS], two[:, 0, 1:], two[:, 1, 1:])
                packed = tbf[:, 2 + r, 0:STEP_PAIRS]
                k_(dve.tensor_copy(packed, digits[3]))
                for digit in digits[2::-1]:
                    k_(dve.scalar_tensor_tensor(out=packed, in0=packed, scalar=float(E2), in1=digit, op0=ALU.mult, op1=ALU.add))
            k_(dve.tensor_copy(m.tab2[:, 0:2, :], tbf[:, 2:4, 0:STEP_PAIRS]))
            k_(dve.tensor_scalar(tbf[:, 4, 0:1], row[0:1, 4, E2 - 1:E2], float(1 - 2 * MIN_PAIRS), None, ALU.add))
            k_(dve.tensor_copy(m.tab2[:, 2, 0:1], tbf[:, 4, 0:1]))
            k_(dve.tensor_scalar(m.tab2[:, 2, 0:1], m.tab2[:, 2, 0:1], 1, None, ALU.logical_shift_right))
            k_(dve.tensor_reduce(tbf[:, 5, 0:1], ps_p[0:1, 1, :], AX.X, ALU.max))
            k_(dve.tensor_scalar(tbf[:, 5, 0:1], tbf[:, 5, 0:1], float(m.cap), None, ALU.is_gt))
            k_(dve.tensor_copy(m.tab2[:, 2, 1:2], tbf[:, 5, 0:1]))
            dve.wait_ge(s["table"], G * K)
            k_(dve.tensor_scalar(tabf[:, 0, :], ps_r[:, 0:MAX2], 0.0, m.pad_row[:, 0:1], ALU.is_equal, ALU.mult))
            k_(dve.scalar_tensor_tensor(out=tabf[:, 1, :], in0=ps_r[:, 0:MAX2], scalar=-1.0, in1=tabf[:, 0, :],
                                        op0=ALU.add, op1=ALU.add))
            dve.tensor_copy(m.scatter2[:], tabf[:, 1, :])
            k_(dve.tensor_scalar(tabf[:, 2, :], tabf[:, 1, :], float(TOKENS - 1), None, ALU.min))
            dve.tensor_copy(m.gather2[:], tabf[:, 2, :])
            k_(dve.tensor_copy(m.weight2[:], ps_r[:, MAX2:]))


def experts(nc, m):
    with ExitStack() as st:
        def sb(name, shape, dt=F32):
            return m.sb(name, shape, dt, st)

        def ps(name, shape):
            return st.enter_context(nc.psum_tensor(name, shape, F32))

        s = semaphores(nc, st, "e_", (
            "gx0", "gx1", "gi", "si", "add0", "add1", "t1", "t1hi", "t1lo", "g1", "sil", "a", "t2", "t2hi", "t2lo", "g2",
            "y", "last0", "last1", "raw", "w_hi", "w_lo", "lastrow", "carried"))
        gx, add, lst = (s["gx0"], s["gx1"]), (s["add0"], s["add1"]), (s["last0"], s["last1"])
        xg = sb("e_xg", [P, 2, D])
        xth = sb("e_xth", [P, 2, C, P], F32R)
        xtl = sb("e_xtl", [P, 2, C, P], F32R)
        a = sb("e_a", [P, 2, INNER])
        ath = sb("e_ath", [P, 2, CI, P], F32R)
        atl = sb("e_atl", [P, 2, CI, P], F32R)
        y = sb("e_y", [P, 2, D])
        lastrow = sb("e_lastrow", [P, 2, D])
        gidx = sb("e_gidx", [P, 2], I32)
        sidx = sb("e_sidx", [P, 2], I32)
        ps_t1, ps_t2, ps_gu = (ps(n, [P, D]) for n in ("eps_t1", "eps_t2", "eps_gu"))
        ps_y = [ps(f"eps_y{i}", [P, D]) for i in range(2)]
        block = st.enter_context(nc.Block())

        ROWS = {"rows_c": (4, 5), "rows_b": (2, 3), "rows_a": (0, 1)}
        ROW_SKEWS = [("rows_c", 3), ("rows_b", 2), ("rows_a", 1)]

        def looked_up(eng, row, found):
            def look(pair):
                v = eng.value_load(m.tab2[0:1, row, bass.ds(pair, 1)], min_val=0, max_val=E2 ** (LOOK_BACK + 1) - 1)
                for i in range(LOOK_BACK + 1):
                    found[i - LOOK_BACK] = (v // E2 ** i) % E2
            return look

        @block.sync
        def _(sp):
            pairs = number_of_pairs(sp, m.tab2[0:1, 2, 0:1], MAX2)
            split = {}

            def load(e, par):
                ex = bass.ds(e, 1)
                sp.dma_start(m.raw[:, par, 0:C], m.w13[ex].rearrange("o (c p) n -> p (o c) n", p=P)).then_inc(s["raw"], 16)
                sp.dma_start(m.raw[:, par, C:HL], m.w2[ex].rearrange("o (c p) n -> p (o c) n", p=P)).then_inc(s["raw"], 16)

            def emit(part, t):
                if part == "load":
                    e = split[t.off]
                    with sp.If(e > 0):
                        with sp.If(e < E2 - 2):
                            sp.wait_ge(s["w_lo"], HL * e + HL)
                            sp.wait_ge(s["raw"], 32 * e + 64)
                            load((e + 2) % E2, bass.ds(e % 2, 1))
                elif part == "last_row":
                    sp.wait_ge(s["lastrow"], t.n + 1)
                    sp.dma_start(m.last_dram[bass.ds(t.n, 1), :], lastrow[P - 1:P, t.par]).then_inc(lst[t.par], 16)

            sp.sem_inc(s["raw"], 32 * W_SETS)
            load(W_SETS, slice(1, 2))
            sp.wait_ge(s["raw"], 32 * (W_SETS + 1))
            load(W_SETS + 1, slice(0, 1))
            pipeline(sp, pairs, [("load", 1), ("last_row", 2)], emit, looked_up(sp, 1, split))
            for q in lst:
                sp.wait_ge(q, 16 * pairs)
            sp.sem_inc(s["carried"], 1)

        @block.gpsimd
        def _(pool):
            pairs = number_of_pairs(pool, m.tab2[0:1, 2, 0:1], MAX2)

            def emit(part, t):
                if part == "gather":
                    wait(pool, s["t1"], t.n - 1)
                    wait(pool, gx[t.par], 16 * t.half)
                    m.carry(pool)
                    nc.gpsimd.tensor_copy(gidx[:, t.par:t.par + 1], m.gather2[:, bass.ds(t.n, 1)]).then_inc(s["gi"], 1)
                    pool.wait_ge(s["gi"], t.n + 1)
                    m.carry(pool)
                    pool.indirect_dma_start(xg[:, t.par], None, m.hn_dram, bass.IndirectOffsetOnAxis(ap=gidx[:, t.par:t.par + 1], axis=0)
                                            ).then_inc(gx[t.par], 16)
                elif part == "add":
                    wait(pool, add[t.par], 16 * t.half)
                    m.carry(pool)
                    nc.gpsimd.tensor_copy(sidx[:, t.par:t.par + 1], m.scatter2[:, bass.ds(t.n, 1)]).then_inc(s["si"], 1)
                    pool.wait_ge(s["si"], t.n + 1)
                    pool.wait_ge(s["y"], t.n + 1)
                    wait(pool, add[1 - t.par], 16 * (t.half + t.par))
                    m.carry(pool)
                    pool.indirect_dma_start(m.out, bass.IndirectOffsetOnAxis(ap=sidx[:, t.par:t.par + 1], axis=0), y[:, t.par], None,
                                            compute_op=ALU.add).then_inc(add[t.par], 16)

            pipeline(pool, pairs, [("gather", 0), ("add", 6)], emit)
            for q in add:
                pool.wait_ge(q, 16 * pairs)
            m.carry(pool)

        @block.tensor
        def _(pe):
            pairs = number_of_pairs(pe, m.tab2[0:1, 2, 0:1], MAX2)

            def turn(dst, src, n):
                for c in range(n):
                    mm = pe.transpose(dst[:, c * P:(c + 1) * P], src[:, c * P:(c + 1) * P], m.ident[:])
                return mm

            expert = {}

            def emit(part, t):
                if part == "t1":
                    pe.wait_ge(gx[t.par], 16 * (t.half + 1))
                    wait(pe, s["t1lo"], t.n)
                    turn(ps_t1, xg[:, t.par], C).then_inc(s["t1"], 1)
                elif part == "g1":
                    w = bass.ds(expert[t.off] % W_SETS, 1)
                    pe.wait_ge(s["w_lo"], HL * expert[t.off] + C)
                    pe.wait_ge(s["t1lo"], t.n + 1)
                    wait(pe, s["a"], t.n)
                    for c in range(C):
                        mm = three_products(pe, ps_gu[:], xth[:, t.par, c], xtl[:, t.par, c], m.wh[:, w, c, :], m.wl[:, w, c, :],
                                            c == 0, c == C - 1)
                    mm.then_inc(s["g1"], 1)
                elif part == "t2":
                    pe.wait_ge(s["a"], t.n + 1)
                    wait(pe, s["t2lo"], t.n)
                    turn(ps_t2, a[:, t.par], CI).then_inc(s["t2"], 1)
                elif part == "g2":
                    w = bass.ds(expert[t.off] % W_SETS, 1)
                    pe.wait_ge(s["w_lo"], HL * expert[t.off] + HL)
                    pe.wait_ge(s["t2lo"], t.n + 1)
                    wait(pe, s["lastrow"], t.n - 1)
                    for c in range(CI):
                        mm = three_products(pe, ps_y[t.par][:], ath[:, t.par, c], atl[:, t.par, c], m.wh[:, w, C + c, :],
                                            m.wl[:, w, C + c, :], c == 0, c == CI - 1)
                    mm.then_inc(s["g2"], 1)

            pipeline(pe, pairs, [("t1", 0), ("t2", 2), ("g1", 1), ("g2", 3)], emit, looked_up(pe, 0, expert))

        @block.scalar
        def _(act):
            pairs = number_of_pairs(act, m.tab2[0:1, 2, 0:1], MAX2)
            act.sem_inc(s["w_hi"], HL * W_SETS)
            split = {}

            def emit(part, t):
                if part == "silu":
                    act.wait_ge(s["g1"], t.n + 1)
                    wait(act, s["t2"], t.n - 1)
                    nc.scalar.activation(a[:, t.par], ps_gu[:, 0:INNER], ACT.Silu).then_inc(s["sil"], 1)
                elif part == "t1hi":
                    act.wait_ge(s["t1"], t.n + 1)
                    wait(act, s["g1"], t.n - 1)
                    nc.scalar.activation(xth[:, t.par].rearrange("p c n -> p (c n)"), ps_t1[:], ACT.Copy).then_inc(s["t1hi"], 1)
                elif part == "t2hi":
                    act.wait_ge(s["t2"], t.n + 1)
                    wait(act, s["g2"], t.n - 1)
                    nc.scalar.activation(ath[:, t.par].rearrange("p c n -> p (c n)"), ps_t2[:, 0:INNER], ACT.Copy).then_inc(s["t2hi"], 1)
                elif part == "y":
                    act.wait_ge(s["g2"], t.n + 1)
                    wait(act, add[t.par], 16 * t.half)
                    nc.scalar.activation(y[:, t.par], ps_y[t.par][:], ACT.Copy, scale=m.weight2[:, bass.ds(t.n, 1)]).then_inc(s["y"], 1)
                    wait(act, lst[t.par], 16 * t.half)
                    nc.scalar.activation(lastrow[96:P, t.par], ps_y[t.par][96:P, :], ACT.Copy).then_inc(s["lastrow"], 1)
                elif part in ROWS:
                    e = split[t.off]
                    with act.If(e > 0):
                        act.wait_ge(s["raw"], 32 * e + 32)
                        wait(act, s["g2" if part == "rows_c" else "g1"], t.n)
                        for r in ROWS[part]:
                            nc.scalar.activation(m.wh[:, bass.ds(e % W_SETS, 1), r, :], m.raw[:, bass.ds(e % 2, 1), r, :],
                                                 ACT.Copy).then_inc(s["w_hi"], 1)

            pipeline(act, pairs, [("t1hi", 0), ("t2hi", 2), *ROW_SKEWS, ("y", 4), ("silu", 1)], emit,
                     looked_up(act, 1, split))

        @block.vector
        def _(dve):
            pairs = number_of_pairs(dve, m.tab2[0:1, 2, 0:1], MAX2)
            dve.sem_inc(s["w_lo"], HL * W_SETS)
            split = {}

            def emit(part, t):
                if part == "a":
                    dve.wait_ge(s["sil"], t.n + 1)
                    dve.tensor_tensor(a[:, t.par], a[:, t.par], ps_gu[:, INNER:D], ALU.mult).then_inc(s["a"], 1)
                elif part == "t1lo":
                    dve.wait_ge(s["t1hi"], t.n + 1)
                    dve.tensor_tensor(xtl[:, t.par].rearrange("p c n -> p (c n)"), ps_t1[:],
                                      xth[:, t.par].rearrange("p c n -> p (c n)").bitcast(F32), ALU.subtract).then_inc(s["t1lo"], 1)
                elif part == "t2lo":
                    dve.wait_ge(s["t2hi"], t.n + 1)
                    dve.tensor_tensor(atl[:, t.par].rearrange("p c n -> p (c n)"), ps_t2[:, 0:INNER],
                                      ath[:, t.par].rearrange("p c n -> p (c n)").bitcast(F32), ALU.subtract).then_inc(s["t2lo"], 1)
                elif part in ROWS:
                    e = split[t.off]
                    w = bass.ds(e % W_SETS, 1)
                    with dve.If(e > 0):
                        for r in ROWS[part]:
                            dve.wait_ge(s["w_hi"], HL * e + (r + 1))
                            dve.tensor_tensor(m.wl[:, w, r, :], m.raw[:, bass.ds(e % 2, 1), r, :],
                                              m.wh[:, w, r, :].bitcast(F32), ALU.subtract).then_inc(s["w_lo"], 1)

            pipeline(dve, pairs, [("t1lo", 0), ("t2lo", 2), *ROW_SKEWS, ("a", 1)], emit,
                     looked_up(dve, 1, split))


def overflow(nc, m):
    with ExitStack() as st:
        s = semaphores(nc, st, "o_", ("rows", "add", "idx", "y"))
        rows = m.sb("o_rows", [P, D], F32, st)
        y = m.sb("o_y", [P, D], F32, st)
        ridx = m.sb("o_ridx", [P, 1], I32, st)
        tidx = m.sb("o_tidx", [P, 1], I32, st)
        wcol = m.sb("o_wcol", [P, 1], F32, st)
        block = st.enter_context(nc.Block())

        @block.gpsimd
        def _(pool):
            flag = pool.value_load(m.tab2[0:1, 2, 1:2], min_val=0, max_val=1)
            with pool.If(flag > 0):
                with pool.Fori(0, K * G) as i:
                    one = bass.ds(i, 1)
                    nc.gpsimd.tensor_copy(ridx[:], m.over_row[:].rearrange("p k g -> p (k g)")[:, one])
                    nc.gpsimd.tensor_copy(tidx[:], m.over_tok[:].rearrange("p k g -> p (k g)")[:, one])
                    nc.gpsimd.tensor_copy(wcol[:], m.topk[:].rearrange("p k g -> p (k g)")[:, one]).then_inc(s["idx"], 1)
                    pool.wait_ge(s["idx"], i + 1)
                    m.carry(pool)
                    pool.indirect_dma_start(rows[:], None, m.last_dram, bass.IndirectOffsetOnAxis(ap=ridx[:, 0:1], axis=0)
                                            ).then_inc(s["rows"], 16)
                    pool.wait_ge(s["rows"], 16 * (i + 1))
                    m.carry(pool)
                    nc.gpsimd.tensor_scalar(y[:], rows[:], wcol[:, 0:1], 0.0, ALU.mult, ALU.add).then_inc(s["y"], 1)
                    pool.wait_ge(s["y"], i + 1)
                    m.carry(pool)
                    pool.indirect_dma_start(m.out, bass.IndirectOffsetOnAxis(ap=tidx[:, 0:1], axis=0), y[:], None,
                                            compute_op=ALU.add).then_inc(s["add"], 16)
                    pool.wait_ge(s["add"], 16 * (i + 1))
                    m.carry(pool)



def kernel(x, itok_BxS_13_99985, ctx_2048, L0_ffn_norm_w, L0_ffn_gate_w, L0_ffn_w13, L0_ffn_w2,
           L0_ffn_shared_gate_w, L0_ffn_shared_up_w, L0_ffn_shared_down_w):
    import numpy as np
    import concourse.bacc as bacc
    from concourse.bass_utils import run_bass_kernel_spmd

    nc = bacc.Bacc("TRN2", target_bir_lowering=False, num_devices=1)
    arrays = {
        "x": x.reshape(TOKENS, D), "tid": itok_BxS_13_99985.reshape(P, G), "ctx_w": ctx_2048,
        "norm_w": L0_ffn_norm_w.reshape(1, D), "gate_w": L0_ffn_gate_w, "w13": L0_ffn_w13, "w2": L0_ffn_w2,
        "sg": L0_ffn_shared_gate_w, "su": L0_ffn_shared_up_w, "sd": L0_ffn_shared_down_w,
    }
    arrays = {"in_" + n: np.ascontiguousarray(a) for n, a in arrays.items()}
    given = {n: nc.dram_tensor(n, a.shape, mybir.dt.from_np(a.dtype), kind="ExternalInput").ap() for n, a in arrays.items()}
    m = Memory()
    m.cap = CAP
    m.x, m.tid, m.ctx_w, m.norm_w = given["in_x"], given["in_tid"], given["in_ctx_w"], given["in_norm_w"]
    m.gate_w, m.w13, m.w2 = given["in_gate_w"], given["in_w13"], given["in_w2"]
    m.sg, m.su, m.sd = given["in_sg"], given["in_su"], given["in_sd"]
    m.out = nc.dram_tensor("out", (TOKENS + PAD, D), F32, kind="ExternalOutput").ap()
    m.hn_dram = nc.dram_tensor("hn_dram", (TOKENS, D), F32, kind="Internal").ap()
    m.bl_dram = nc.dram_tensor("bl_dram", (TOKENS, D + E2), F32, kind="Internal").ap()
    m.last_dram = nc.dram_tensor("last_dram", (MAX2, D), F32, kind="Internal").ap()
    build(nc, m)
    result = run_bass_kernel_spmd(nc, [arrays], core_ids=[0])
    return result.results[0]["out"][:TOKENS].reshape(4, 512, D)
```

```python
from contextlib import ExitStack

import concourse.bass as bass
from concourse import mybir

F32 = mybir.dt.float32
F32R = mybir.dt.float32r
BF16 = mybir.dt.bfloat16
I32 = mybir.dt.int32
U32 = mybir.dt.uint32
ALU = mybir.AluOpType
ACT = mybir.ActivationFunctionType
AX = mybir.AxisListType

P = 128
D = 512
C = D // P
TOKENS = 2048
G = TOKENS // P
E1 = 4
VOCAB = 25000
PER_EXPERT = VOCAB // E1
E2 = 32
K = 4
INNER = 256
CI = INNER // P
CAP = 2 * TOKENS * K // E2
MAX1 = 20
MAX2 = 96
MIN_PAIRS = 8
BACK1 = 5
BACK2 = 3
STEP_PAIRS1 = MAX1 // 2 + 1
STEP_PAIRS = MAX2 // 2 + 1
PAD = P
LN_EPS = 1e-5
RMS_EPS = 1e-6
W_SETS = 3
HL = C + CI


class Memory:
    pass


class Tile:

    def __init__(self, pair, off):
        self.off = off
        self.n = 2 * pair + off
        self.half = pair + off // 2
        self.par = off % 2


def wait(eng, sem, value):
    if isinstance(value, int) and value <= 0:
        return
    eng.wait_ge(sem, value)


def pipeline(eng, pairs, skews, emit, look=lambda pair: None):
    deepest = max(s for _, s in skews)
    first = (deepest + 3) // 2
    for pair in range(first):
        look(pair)
        for b in range(2):
            for part, s in skews:
                if 2 * pair + b - s >= 0:
                    emit(part, Tile(pair, b - s))
    with eng.Fori(first, pairs) as pair:
        look(pair)
        for b in range(2):
            for part, s in skews:
                emit(part, Tile(pair, b - s))
    look(pairs)
    for b in range(deepest):
        for part, s in skews:
            if b - s < 0:
                emit(part, Tile(pairs, b - s))


class Chain:

    def __init__(self, eng, sem):
        self.eng, self.sem, self.n = eng, sem, 0

    def __call__(self, ins):
        self.n += 1
        ins.then_inc(self.sem, 1)
        self.eng.wait_ge(self.sem, self.n)




def tensors(nc, m, top):
    sb = m.sb
    m.ident = sb("ident", [P, P], F32, top)
    m.before = sb("before", [P, P], F32, top)
    m.ones = sb("ones", [P, P], F32, top)
    m.iota_row = sb("iota_row", [P, P], F32, top)
    m.part_id = sb("part_id", [P, 1], F32, top)
    m.pad_row = sb("pad_row", [P, 1], F32, top)
    m.minus_half = sb("minus_half", [P, 1], F32, top)
    m.tokcol = sb("tokcol", [P, G], F32, top)
    m.normw = sb("normw", [P, D], F32, top)
    m.ghl = sb("ghl", [P, C, 2 * E2], F32R, top)
    m.gather1 = sb("gather1", [P, MAX1], I32, top)
    m.scatter1 = sb("scatter1", [P, MAX1], I32, top)
    m.tab1 = sb("tab1", [1, 2, STEP_PAIRS1], I32, top)
    m.gather2 = sb("gather2", [P, MAX2], I32, top)
    m.scatter2 = sb("scatter2", [P, MAX2], I32, top)
    m.weight2 = sb("weight2", [P, MAX2], F32, top)
    m.tab2 = sb("tab2", [1, 3, STEP_PAIRS], I32, top)
    m.over_row = sb("over_row", [P, K, G], I32, top)
    m.over_tok = sb("over_tok", [P, K, G], I32, top)
    m.topw = sb("topw", [P, G, K], F32, top)
    m.topk = sb("topk", [P, K, G], F32, top)
    m.wh_s = sb("wh_s", [P, HL, D], F32R, top)
    m.wl_s = sb("wl_s", [P, HL, D], F32R, top)


def number_of_pairs(eng, entry, most):
    return eng.value_load(entry, min_val=0, max_val=most // 2 - MIN_PAIRS) + MIN_PAIRS


def pack(dve, k, packed, entries, back, base, pairs):
    two = entries.rearrange("p (q b) -> p b q", b=2)
    digit = lambda i: two[:, i % 2, i // 2:i // 2 + pairs]
    k(dve.tensor_copy(packed, digit(back)))
    for i in range(back - 1, -1, -1):
        k(dve.scalar_tensor_tensor(out=packed, in0=packed, scalar=float(base), in1=digit(i), op0=ALU.mult, op1=ALU.add))


def looked_up(eng, row, back, base, found):
    def look(pair):
        v = eng.value_load(row[:, bass.ds(pair, 1)], min_val=0, max_val=base ** (back + 1) - 1)
        for i in range(back + 1):
            found[i - back] = (v // base ** i) % base
    return look


def semaphores(nc, stack, prefix, names):
    return {n: stack.enter_context(nc.semaphore(prefix + n)) for n in names}


def three_products(pe, acc, left_hi, left_lo, right_hi, right_lo, start, stop):
    pe.matmul(acc, left_hi, right_hi, start=start, stop=False)
    pe.matmul(acc, left_hi, right_lo, start=False, stop=False)
    return pe.matmul(acc, left_lo, right_hi, start=False, stop=stop)


def setup(nc, m):
    with ExitStack() as st:
        def ps(name, shape, dt=F32):
            return st.enter_context(nc.psum_tensor(name, shape, dt))
        craw = m.sb("craw", [P, 2, C, D], F32, st)
        sraw = m.sb("sraw", [P, HL, D], F32, st)
        graw = m.sb("graw", [E2, D], F32, st)
        zeros = m.sb("zeros", [P, D], F32, st)
        tidi = m.sb("tidi", [P, G], I32, st)
        tidf = m.sb("tidf", [P, G], F32, st)
        M = m.sb("M1", [P, G, E1], F32, st)
        reach = m.sb("reach1", [P, E1 + 1, G], F32, st)
        slots = m.sb("slots1", [P, G, E1], F32, st)
        row = m.sb("row1", [P, 8, E1], F32, st)
        rowi = m.sb("row1i", [P, E1], I32, st)
        sel = m.sb("sel1", [P, 4, G], F32, st)
        seli = m.sb("sel1i", [P, 3, G], I32, st)
        hot = m.sb("hot1", [P, 2, P + MAX1], F32, st)
        tabf = m.sb("tab1f", [P, 3, MAX1], F32, st)
        cmp = m.sb("cmp1", [1, MAX1 + 1, E1], F32, st)
        tbf = m.sb("tb1f", [1, 2, BACK1 + MAX1 + 1], F32, st)
        psC = [ps(f"psC{i}", [P, D]) for i in range(3)]
        psG = ps("psG", [P, E2])
        psP = ps("psP", [P, 2, E1])
        psR = ps("psR", [P, MAX1])
        block = st.enter_context(nc.Block())

        @block.sync
        def _(sp):
            sp.dma_start(tidi[:], m.tid).then_inc(m.s["tid_loaded"], 16)
            for e in range(E1):
                if e >= 2:
                    sp.wait_ge(m.s["ctx_turned"], 4 * (e - 1))
                sp.dma_start(craw[:, e % 2], m.ctx_w[e].rearrange("(c p) n -> p c n", p=P)).then_inc(
                    m.s[f"ctx_loaded{e % 2}"], 16)
                if e == 0:
                    sp.dma_start(graw[:], m.gate_w).then_inc(m.s["gate_loaded"], 16)
                    sp.dma_start(m.normw[:], m.norm_w.to_broadcast([P, D])).then_inc(m.s["norm_loaded"], 16)
            sp.dma_start(sraw[:, 0:C, 0:INNER], m.sg.rearrange("(c p) n -> p c n", p=P)).then_inc(m.s["sh_loaded"], 16)
            sp.dma_start(sraw[:, 0:C, INNER:D], m.su.rearrange("(c p) n -> p c n", p=P)).then_inc(m.s["sh_loaded"], 16)
            sp.dma_start(sraw[:, C:HL, :], m.sd.rearrange("(c p) n -> p c n", p=P)).then_inc(m.s["sh_loaded"], 16)
            sp.wait_ge(m.s["consts"], 1)
            sp.dma_start(m.out[TOKENS:TOKENS + PAD, :], zeros[:]).then_inc(m.s["zero_pad"], 16)
            sp.dma_start(m.last_dram, zeros[0:MAX2, :]).then_inc(m.s["zero_pad"], 16)
            sp.wait_ge(m.s["zero_pad"], 32)

        @block.gpsimd
        def _(pool):
            k = Chain(pool, m.s["chain0"])
            nc.gpsimd.memset(zeros[:], 0.0).then_inc(m.s["consts"], 1)
            nc.gpsimd.memset(m.minus_half[:], -0.5)
            k(nc.gpsimd.memset(m.ones[:], 1.0))
            k(nc.gpsimd.affine_select(out=m.ident[:], in_=m.ones[:], compare_op=ALU.is_equal, fill=0.0, base=0,
                                      pattern=[[-1, P]], channel_multiplier=1))
            k(nc.gpsimd.affine_select(out=m.before[:], in_=m.ones[:], compare_op=ALU.is_gt, fill=0.0, base=0,
                                      pattern=[[1, P]], channel_multiplier=-1))
            nc.gpsimd.iota(m.iota_row[:], pattern=[[1, P]], base=0, channel_multiplier=0,
                           allow_small_or_imprecise_dtypes=True)
            nc.gpsimd.iota(m.part_id[:], pattern=[[0, 1]], base=0, channel_multiplier=1,
                           allow_small_or_imprecise_dtypes=True)
            nc.gpsimd.iota(m.pad_row[:], pattern=[[0, 1]], base=TOKENS + 1, channel_multiplier=1,
                           allow_small_or_imprecise_dtypes=True)
            nc.gpsimd.iota(m.tokcol[:], pattern=[[1, G]], base=1, channel_multiplier=G,
                           allow_small_or_imprecise_dtypes=True).then_inc(m.s["consts"], 1)
            pool.wait_ge(m.s["sh_hi"], 1)
            nc.gpsimd.tensor_tensor(m.wl_s[:], sraw[:], m.wh_s[:].bitcast(F32), ALU.subtract)

        @block.tensor
        def _(pe):
            pe.wait_ge(m.s["consts"], 2)
            pe.wait_ge(m.s["counted"], 1)
            pe.matmul(psP[:, 0, :], m.before[:], row[:, 0, :], start=True, stop=True)
            pe.matmul(psP[:, 1, :], m.ones[:], row[:, 0, :], start=True, stop=True).then_inc(m.s["prefix"], 1)
            for e in range(E1):
                pe.wait_ge(m.s[f"ctx_loaded{e % 2}"], 16 * (e // 2 + 1))
                for c in range(C):
                    n = e * C + c
                    if n >= 3:
                        pe.wait_ge(m.s["ctx_split"], n - 2)
                    for r in range(C):
                        mm = pe.transpose(psC[n % 3][:, r * P:(r + 1) * P],
                                          craw[:, e % 2, r, c * P:(c + 1) * P], m.ident[:])
                    mm.then_inc(m.s["ctx_turned"], 1)
                    if n == 2:
                        for i in range(G):
                            pe.wait_ge(m.s["onehot"], i + 1)
                            mm = pe.matmul(psR[:], hot[:, i % 2, 0:P], hot[:, i % 2, P:P + MAX1],
                                           start=(i == 0), stop=(i == G - 1)).then_inc(m.s["table"], 1)
                        pe.wait_ge(m.s["gate_loaded"], 16)
                        for c in range(C):
                            if c:
                                pe.wait_ge(m.s["gate_done"], c)
                            pe.transpose(psG[:, :], graw[:, c * P:(c + 1) * P], m.ident[0:E2, 0:E2]).then_inc(
                                m.s["gate_turned"], 1)

        @block.scalar
        def _(act):
            def gate(c):
                act.wait_ge(m.s["gate_turned"], c + 1)
                nc.scalar.activation(m.ghl[:, c, 0:E2], psG[:], ACT.Copy).then_inc(m.s["gate_hi"], 1)
            for n in range(E1 * C):
                act.wait_ge(m.s["ctx_turned"], n + 1)
                nc.scalar.activation(m.cth[:, n // C, n % C, :], psC[n % 3][:], ACT.Copy).then_inc(m.s["ctx_hi"], 1)
                if n == 2:
                    for c in range(C):
                        gate(c)
            act.wait_ge(m.s["sh_loaded"], 48)
            nc.scalar.activation(m.wh_s[:], sraw[:], ACT.Copy).then_inc(m.s["sh_hi"], 1)

        @block.vector
        def _(dve):
            k = Chain(dve, m.s["chain1"])

            def low(n):
                dve.wait_ge(m.s["ctx_hi"], n + 1)
                dve.tensor_tensor(m.ctl[:, n // C, n % C, :], psC[n % 3][:], m.cth[:, n // C, n % C, :].bitcast(F32),
                                  ALU.subtract).then_inc(m.s["ctx_split"], 1)

            def gate_low(c):
                dve.wait_ge(m.s["gate_hi"], c + 1)
                dve.tensor_tensor(m.ghl[:, c, E2:], psG[:], m.ghl[:, c, 0:E2].bitcast(F32), ALU.subtract).then_inc(m.s["gate_done"], 1)

            dve.wait_ge(m.s["tid_loaded"], 16)
            k(dve.tensor_copy(tidf[:], tidi[:]))
            dve.memset(reach[:, 0, :], 1.0)
            dve.memset(reach[:, E1, :], 0.0)
            for e in range(1, E1):
                ins = dve.tensor_scalar(reach[:, e, :], tidf[:], float(e * PER_EXPERT), None, ALU.is_ge)
            k(ins)
            k(dve.tensor_tensor(M[:], reach[:, 0:E1, :].rearrange("p e g -> p g e"),
                                reach[:, 1:E1 + 1, :].rearrange("p e g -> p g e"), ALU.subtract))
            dve.tensor_reduce(row[:, 0, :], M[:].rearrange("p g e -> p e g"), AX.X, ALU.add).then_inc(m.s["counted"], 1)
            k(dve.memset(slots[:, 0, :], 0.0))
            for g in range(1, G):
                k(dve.tensor_tensor(slots[:, g, :], slots[:, g - 1, :], M[:, g - 1, :], ALU.add))
            dve.wait_ge(m.s["prefix"], 1)
            k(dve.tensor_scalar(row[:, 1, :], psP[:, 1, :], float(P - 1), None, ALU.add))
            k(dve.tensor_copy(rowi[:], row[:, 1, :]))
            k(dve.tensor_scalar(rowi[:], rowi[:], 7, None, ALU.logical_shift_right))
            k(dve.tensor_copy(row[:, 2, :], rowi[:]))
            k(dve.memset(row[:, 3, :], 0.0))
            k(dve.tensor_tensor_scan(row[:, 4, :], row[:, 2, :], row[:, 3, :], 0.0, ALU.add, ALU.add))
            k(dve.tensor_tensor(row[:, 5, :], row[:, 4, :], row[:, 2, :], ALU.subtract))
            k(dve.scalar_tensor_tensor(out=row[:, 6, :], in0=row[:, 5, :], scalar=float(P), in1=psP[:, 0, :],
                                       op0=ALU.mult, op1=ALU.add))
            k(dve.tensor_tensor(slots[:], slots[:], row[:, 6:7, :].to_broadcast([P, G, E1]), ALU.add))
            k(dve.tensor_tensor(slots[:], slots[:], M[:], ALU.mult))
            k(dve.tensor_reduce(sel[:, 0, :], slots[:], AX.X, ALU.add))
            k(dve.tensor_copy(seli[:, 0, :], sel[:, 0, :]))
            dve.tensor_scalar(seli[:, 1, :], seli[:, 0, :], 7, None, ALU.logical_shift_right)
            k(dve.tensor_scalar(seli[:, 2, :], seli[:, 0, :], P - 1, None, ALU.bitwise_and))
            dve.tensor_copy(sel[:, 1, :], seli[:, 1, :])
            k(dve.tensor_copy(sel[:, 2, :], seli[:, 2, :]))
            dve.wait_ge(m.s["consts"], 2)
            for i in range(G):
                if i >= 2:
                    dve.wait_ge(m.s["table"], i - 1)
                dve.tensor_scalar(hot[:, i % 2, 0:P], m.iota_row[:], sel[:, 2, i:i + 1], None, ALU.is_equal)
                dve.tensor_scalar(hot[:, i % 2, P:P + MAX1], m.iota_row[:, 0:MAX1], sel[:, 1, i:i + 1],
                                  m.tokcol[:, i:i + 1], ALU.is_equal, ALU.mult).then_inc(m.s["onehot"], 1)
            for n in range(3):
                low(n)
            for c in range(C):
                gate_low(c)
            low(3)
            dve.wait_ge(m.s["table"], G)
            k(dve.tensor_scalar(tabf[:, 0, :], psR[:], 0.0, m.pad_row[:, 0:1], ALU.is_equal, ALU.mult))
            k(dve.scalar_tensor_tensor(out=tabf[:, 1, :], in0=psR[:], scalar=-1.0, in1=tabf[:, 0, :],
                                       op0=ALU.add, op1=ALU.add))
            dve.tensor_copy(m.scatter1[:], tabf[:, 1, :])
            k(dve.tensor_scalar(tabf[:, 2, :], tabf[:, 1, :], float(TOKENS - 1), None, ALU.min))
            dve.tensor_copy(m.gather1[:], tabf[:, 2, :])
            k(dve.tensor_tensor(cmp[:], m.iota_row[0:1, 0:MAX1 + 1].rearrange("p (n o) -> p n o", o=1).to_broadcast([1, MAX1 + 1, E1]),
                                row[0:1, 4:5, :].to_broadcast([1, MAX1 + 1, E1]), ALU.is_ge))
            k(dve.memset(tbf[:], 0.0))
            k(dve.tensor_reduce(tbf[:, 0, BACK1:], cmp[:], AX.X, ALU.add))
            k(dve.tensor_scalar(tbf[:, 0, :], tbf[:, 0, :], float(E1 - 1), None, ALU.min))
            pack(dve, k, tbf[:, 1, 0:STEP_PAIRS1], tbf[:, 0, :], BACK1, E1, STEP_PAIRS1)
            k(dve.tensor_copy(m.tab1[:, 0, :], tbf[:, 1, 0:STEP_PAIRS1]))
            k(dve.tensor_scalar(tbf[:, 1, 0:1], row[0:1, 4, E1 - 1:E1], float(1 - 2 * MIN_PAIRS), None, ALU.add))
            k(dve.tensor_copy(m.tab1[:, 1, 0:1], tbf[:, 1, 0:1]))
            k(dve.tensor_scalar(m.tab1[:, 1, 0:1], m.tab1[:, 1, 0:1], 1, None, ALU.logical_shift_right))
            for n in range(4, E1 * C):
                low(n)



def build(nc, m):
    with ExitStack() as top:
        m.sb = lambda name, shape, dt, stack: stack.enter_context(nc.sbuf_tensor(name, shape, dt))
        tensors(nc, m, top)
        m.s = {n: top.enter_context(nc.semaphore(n)) for n in (
            "consts", "chain0", "chain1", "ctx_turned", "ctx_hi", "ctx_split", "gate_turned", "gate_hi", "gate_done", "counted",
            "onehot", "table", "tid_loaded", "norm_loaded", "gate_loaded", "sh_loaded", "sh_hi", "prefix", "zero_pad",
            "ctx_loaded0", "carried", "ctx_loaded1")}
        m.carry = lambda eng: eng.sem_inc(m.s["carried"], 1)
        with ExitStack() as st:
            m.cth = m.sb("cth", [P, E1, C, D], F32R, st)
            m.ctl = m.sb("ctl", [P, E1, C, D], F32R, st)
            setup(nc, m)
            context(nc, m)
        with ExitStack() as st:
            m.wh = m.sb("wh", [P, W_SETS, HL, D], F32R, st)
            m.wl = m.sb("wl", [P, W_SETS, HL, D], F32R, st)
            m.raw = m.sb("raw", [P, 2, HL, D], F32, st)
            shared_and_routing(nc, m)
            experts(nc, m)
        overflow(nc, m)


def context(nc, m):
    with ExitStack() as st:
        def sb(name, shape, dt=F32):
            return m.sb(name, shape, dt, st)

        def ps(name, shape):
            return st.enter_context(nc.psum_tensor(name, shape, F32))

        s = semaphores(nc, st, "c_", (
            "gx0", "gx1", "xr", "stat1", "mv1", "var1", "rstd1", "h", "t1", "t1hi", "t1lo", "g1", "sil", "a",
            "t2", "t2hi", "t2lo", "g2", "x1", "stat2", "mv2", "var2", "rstd2", "affine", "x2", "ss", "ms", "rrms",
            "hn", "base", "hb0", "hb1", "gi", "si"))
        gx, hbs = (s["gx0"], s["gx1"]), (s["hb0"], s["hb1"])
        KEPT = 8
        xg = sb("c_xg", [P, 2, D])
        xr = sb("c_xr", [P, KEPT, D])
        h = sb("c_h", [P, 2, D])
        hth = sb("c_hth", [P, 2, C, P], F32R)
        htl = sb("c_htl", [P, 2, C, P], F32R)
        a = sb("c_a", [P, 2, D])
        ath = sb("c_ath", [P, 2, C, P], F32R)
        atl = sb("c_atl", [P, 2, C, P], F32R)
        x1 = sb("c_x1", [P, 2, D])
        x2 = sb("c_x2", [P, 2, D])
        hb = sb("c_hb", [P, 2, 2, D])
        sq = sb("c_sq", [P, D])
        stat = sb("c_stat", [P, 2, 6])
        mv = sb("c_mv", [P, 2, 2, 2])
        rs = sb("c_rs", [P, 3, 2, 2])
        affine = sb("c_affine", [P, 2, 2])
        ss = sb("c_ss", [P, 2])
        gidx = sb("c_gidx", [P, 2], I32)
        sidx = sb("c_sidx", [P, 2], I32)
        ps_t1, ps_t2, ps_z = (ps(n, [P, D]) for n in ("ps_t1", "ps_t2", "ps_z"))
        ps_y = [ps(f"ps_y{i}", [P, D]) for i in range(2)]
        block = st.enter_context(nc.Block())

        @block.gpsimd
        def _(pool):
            pairs = number_of_pairs(pool, m.tab1[0:1, 1, 0:1], MAX1)

            def power(which, t, src, offset, scale, sem_mid, sem_out):
                m.carry(pool)
                nc.gpsimd.tensor_scalar(rs[:, which, t.par, 0:1], src, scale, offset, ALU.mult, ALU.add).then_inc(sem_mid, 1)
                pool.wait_ge(sem_mid, t.n + 1)
                nc.gpsimd.tensor_tensor(rs[:, which, t.par, 1:2], rs[:, which, t.par, 0:1], m.minus_half[:], ALU.pow).then_inc(sem_out, 1)

            def emit(part, t):
                if part == "gather":
                    wait(pool, s["xr"], t.n - 1)
                    wait(pool, s["h"], t.n - 1)
                    wait(pool, gx[t.par], 16 * t.half)
                    m.carry(pool)
                    nc.gpsimd.tensor_copy(gidx[:, t.par:t.par + 1], m.gather1[:, bass.ds(t.n, 1)]).then_inc(s["gi"], 1)
                    pool.wait_ge(s["gi"], t.n + 1)
                    m.carry(pool)
                    pool.indirect_dma_start(xg[:, t.par], None, m.x, bass.IndirectOffsetOnAxis(ap=gidx[:, t.par:t.par + 1], axis=0)
                                            ).then_inc(gx[t.par], 16)
                elif part == "rstd1":
                    pool.wait_ge(s["mv1"], t.n + 1)
                    power(0, t, mv[:, 0, t.par, 1:2], LN_EPS, 1.0, s["var1"], s["rstd1"])
                elif part == "rstd2":
                    pool.wait_ge(s["mv2"], t.n + 1)
                    power(1, t, mv[:, 1, t.par, 1:2], LN_EPS, 1.0, s["var2"], s["rstd2"])
                elif part == "affine":
                    pool.wait_ge(s["rstd2"], t.n + 1)
                    wait(pool, s["base"], t.n - 1)
                    m.carry(pool)
                    nc.gpsimd.tensor_scalar(affine[:, t.par, 0:1], rs[:, 1, t.par, 1:2], 1.0, None, ALU.add)
                    nc.gpsimd.tensor_scalar(affine[:, t.par, 1:2], mv[:, 1, t.par, 0:1], rs[:, 1, t.par, 1:2], -1.0,
                                            ALU.mult, ALU.mult).then_inc(s["affine"], 1)
                elif part == "rrms":
                    pool.wait_ge(s["ss"], t.n + 1)
                    power(2, t, ss[:, t.par:t.par + 1], RMS_EPS, 1.0 / D, s["ms"], s["rrms"])
                elif part == "scatter":
                    wait(pool, hbs[t.par], 16 * t.half)
                    m.carry(pool)
                    nc.gpsimd.tensor_copy(sidx[:, t.par:t.par + 1], m.scatter1[:, bass.ds(t.n, 1)]).then_inc(s["si"], 1)
                    pool.wait_ge(s["si"], t.n + 1)
                    pool.wait_ge(s["hn"], t.n + 1)
                    pool.wait_ge(s["base"], t.n + 1)
                    m.carry(pool)
                    pool.indirect_dma_start(m.hb_dram, bass.IndirectOffsetOnAxis(ap=sidx[:, t.par:t.par + 1], axis=0),
                                            hb[:, t.par].rearrange("p a n -> p (a n)"), None,
                                            bounds_check=TOKENS - 1, oob_is_err=False).then_inc(hbs[t.par], 16)

            pipeline(pool, pairs, [("gather", 0), ("rstd2", 6), ("rstd1", 1), ("affine", 6), ("scatter", 7), ("rrms", 6)], emit)
            for q in hbs:
                pool.wait_ge(q, 16 * pairs)
            pool.sem_inc(s["gi"], 1)

        @block.tensor
        def _(pe):
            pairs = number_of_pairs(pe, m.tab1[0:1, 1, 0:1], MAX1)

            expert = {}

            def turn(dst, src):
                for c in range(C):
                    mm = pe.transpose(dst[:, c * P:(c + 1) * P], src[:, c * P:(c + 1) * P], m.ident[:])
                return mm

            def product(dst, hi, lo, t):
                e = bass.ds(expert[t.off], 1)
                for c in range(C):
                    mm = three_products(pe, dst[:], hi[:, t.par, c], lo[:, t.par, c], m.cth[:, e, c, :], m.ctl[:, e, c, :],
                                        c == 0, c == C - 1)
                return mm

            def emit(part, t):
                if part == "t1":
                    pe.wait_ge(s["h"], t.n + 1)
                    wait(pe, s["t1lo"], t.n)
                    turn(ps_t1, h[:, t.par]).then_inc(s["t1"], 1)
                elif part == "g1":
                    pe.wait_ge(s["t1lo"], t.n + 1)
                    wait(pe, s["a"], t.n)
                    product(ps_z, hth, htl, t).then_inc(s["g1"], 1)
                elif part == "t2":
                    pe.wait_ge(s["a"], t.n + 1)
                    wait(pe, s["t2lo"], t.n)
                    turn(ps_t2, a[:, t.par]).then_inc(s["t2"], 1)
                elif part == "g2":
                    pe.wait_ge(s["t2lo"], t.n + 1)
                    wait(pe, s["x1"], t.n - 1)
                    product(ps_y[t.par], ath, atl, t).then_inc(s["g2"], 1)

            pipeline(pe, pairs, [("t1", 2), ("t2", 4), ("g1", 3), ("g2", 5)], emit,
                     looked_up(pe, m.tab1[0:1, 0, :], BACK1, E1, expert))

        @block.scalar
        def _(act):
            pairs = number_of_pairs(act, m.tab1[0:1, 1, 0:1], MAX1)

            def emit(part, t):
                if part == "keep":
                    act.wait_ge(gx[t.par], 16 * (t.half + 1))
                    wait(act, s["x1"], t.n - KEPT + 1)
                    kept = xr[:, bass.ds(t.n % KEPT, 1), :]
                    nc.scalar.activation(kept, xg[:, t.par:t.par + 1, :], ACT.Copy).then_inc(s["xr"], 1)
                elif part == "silu":
                    act.wait_ge(s["g1"], t.n + 1)
                    wait(act, s["t2"], t.n - 1)
                    nc.scalar.activation(a[:, t.par], ps_z[:], ACT.Silu).then_inc(s["sil"], 1)
                elif part == "t1hi":
                    act.wait_ge(s["t1"], t.n + 1)
                    wait(act, s["g1"], t.n - 1)
                    nc.scalar.activation(hth[:, t.par].rearrange("p c n -> p (c n)"), ps_t1[:], ACT.Copy).then_inc(s["t1hi"], 1)
                elif part == "t2hi":
                    act.wait_ge(s["t2"], t.n + 1)
                    wait(act, s["g2"], t.n - 1)
                    nc.scalar.activation(ath[:, t.par].rearrange("p c n -> p (c n)"), ps_t2[:], ACT.Copy).then_inc(s["t2hi"], 1)
                elif part == "squares":
                    act.wait_ge(s["x2"], t.n + 1)
                    wait(act, s["ms"], t.n - 1)
                    nc.scalar.activation(sq[:], x2[:, t.par], ACT.Square, accum_out=ss[:, t.par:t.par + 1]).then_inc(s["ss"], 1)
                elif part == "base":
                    act.wait_ge(s["affine"], t.n + 1)
                    wait(act, hbs[t.par], 16 * t.half)
                    nc.scalar.activation(hb[:, t.par, 1], x1[:, t.par], ACT.Identity, bias=affine[:, t.par, 1:2],
                                         scale=affine[:, t.par, 0:1]).then_inc(s["base"], 1)

            pipeline(act, pairs, [("t1hi", 2), ("t2hi", 4), ("keep", 1), ("squares", 6), ("silu", 3), ("base", 6)], emit)

        @block.vector
        def _(dve):
            pairs = number_of_pairs(dve, m.tab1[0:1, 1, 0:1], MAX1)

            def emit(part, t):
                if part == "stats1":
                    dve.wait_ge(gx[t.par], 16 * (t.half + 1))
                    dve.bn_stats(stat[:, 0, :], xg[:, t.par]).then_inc(s["stat1"], 1)
                    dve.wait_ge(s["stat1"], t.n + 1)
                    m.carry(dve)
                    dve.bn_aggr(mv[:, 0, t.par, :], stat[:, 0, :]).then_inc(s["mv1"], 1)
                elif part == "h":
                    dve.wait_ge(s["rstd1"], t.n + 1)
                    wait(dve, s["t1"], t.n - 1)
                    dve.tensor_scalar(h[:, t.par], xg[:, t.par], mv[:, 0, t.par, 0:1], rs[:, 0, t.par, 1:2],
                                      ALU.subtract, ALU.mult).then_inc(s["h"], 1)
                elif part == "a":
                    dve.wait_ge(s["sil"], t.n + 1)
                    dve.tensor_tensor(a[:, t.par], a[:, t.par], ps_z[:], ALU.mult).then_inc(s["a"], 1)
                elif part == "t1lo":
                    dve.wait_ge(s["t1hi"], t.n + 1)
                    dve.tensor_tensor(htl[:, t.par].rearrange("p c n -> p (c n)"), ps_t1[:],
                                      hth[:, t.par].rearrange("p c n -> p (c n)").bitcast(F32), ALU.subtract).then_inc(s["t1lo"], 1)
                elif part == "t2lo":
                    dve.wait_ge(s["t2hi"], t.n + 1)
                    dve.tensor_tensor(atl[:, t.par].rearrange("p c n -> p (c n)"), ps_t2[:],
                                      ath[:, t.par].rearrange("p c n -> p (c n)").bitcast(F32), ALU.subtract).then_inc(s["t2lo"], 1)
                elif part == "x1":
                    dve.wait_ge(s["g2"], t.n + 1)
                    dve.wait_ge(s["xr"], t.n + 1)
                    wait(dve, s["base"], t.n - 1)
                    kept = xr[:, bass.ds(t.n % KEPT, 1), :]
                    dve.tensor_tensor(x1[:, t.par:t.par + 1, :], kept, ps_y[t.par][:].rearrange("p (o n) -> p o n", o=1),
                                      ALU.add).then_inc(s["x1"], 1)
                    dve.wait_ge(s["x1"], t.n + 1)
                    dve.bn_stats(stat[:, 1, :], x1[:, t.par]).then_inc(s["stat2"], 1)
                    dve.wait_ge(s["stat2"], t.n + 1)
                    m.carry(dve)
                    dve.bn_aggr(mv[:, 1, t.par, :], stat[:, 1, :]).then_inc(s["mv2"], 1)
                elif part == "x2":
                    dve.wait_ge(s["rstd2"], t.n + 1)
                    wait(dve, s["ss"], t.n - 1)
                    dve.tensor_scalar(x2[:, t.par], x1[:, t.par], mv[:, 1, t.par, 0:1], rs[:, 1, t.par, 1:2],
                                      ALU.subtract, ALU.mult).then_inc(s["x2"], 1)
                elif part == "hn":
                    dve.wait_ge(s["rrms"], t.n + 1)
                    wait(dve, hbs[t.par], 16 * t.half)
                    dve.scalar_tensor_tensor(out=hb[:, t.par, 0], in0=x2[:, t.par], scalar=rs[:, 2, t.par, 1:2], in1=m.normw[:],
                                             op0=ALU.mult, op1=ALU.mult).then_inc(s["hn"], 1)

            pipeline(dve, pairs, [("x1", 6), ("stats1", 1), ("t1lo", 2), ("x2", 6), ("t2lo", 4), ("h", 1), ("a", 3),
                                  ("hn", 6)], emit)


def shared_and_routing(nc, m):
    with ExitStack() as st:
        def sb(name, shape, dt=F32):
            return m.sb(name, shape, dt, st)

        def ps(name, shape):
            return st.enter_context(nc.psum_tensor(name, shape, F32))

        s = semaphores(nc, st, "s_", (
            "gx0", "gx1", "bs0", "bs1", "t1", "t1raw", "t1hi", "t1lo", "g1", "u", "sil", "a", "t2", "t2raw", "t2hi",
            "t2lo", "g2", "y", "o", "st0", "st1", "lx0", "lx1", "lt", "lthi", "ltlo", "logits", "lcopied", "low_copied", "chain", "shifted", "exp", "counted", "prefix", "hot",
            "table", "raw0", "raw1", "w_hi", "w_lo"))
        gx, bsl, stl = (s["gx0"], s["gx1"]), (s["bs0"], s["bs1"]), (s["st0"], s["st1"])
        COUNTED = 4
        lx_sem = (s["lx0"], s["lx1"])
        free = m.wh[:].rearrange("p w r n -> p (w r n)")
        lx, lth, ltl = (free[:, i * 4 * D:(i + 1) * 4 * D].rearrange("p (b j n) -> p b j n", b=2, j=2) for i in range(3))
        lx = lx.bitcast(F32)
        xg = sb("s_xg", [P, 2, D])
        bs = sb("s_bs", [P, 2, D])
        traw = sb("s_traw", [P, 2, D])
        xth = sb("s_xth", [P, 2, C, P], F32R)
        xtl = sb("s_xtl", [P, 2, C, P], F32R)
        sg_ = sb("s_silu", [P, 2, INNER])
        u_ = sb("s_u", [P, 2, INNER])
        a = sb("s_a", [P, 2, INNER])
        araw = sb("s_araw", [P, 2, INNER])
        ath = sb("s_ath", [P, 2, CI, P], F32R)
        atl = sb("s_atl", [P, 2, CI, P], F32R)
        y = sb("s_y", [P, 2, D])
        o = sb("s_o", [P, 2, D])
        prob = sb("r_prob", [P, G, E2])
        low_part = sb("r_low_part", [P, 2, 2, E2])
        red = sb("r_red", [P, 4, G])
        top8 = sb("r_top8", [P, G, 8])
        idx8 = sb("r_idx8", [P, G, 8], U32)
        eid = sb("r_eid", [P, G, 8])
        oh = sb("r_oh", [P, K, G, E2])
        M = sb("r_m", [P, G, E2])
        rank = sb("r_rank", [P, G, E2])
        tmp = sb("r_tmp", [P, G, E2])
        row = sb("r_row", [P, 8, E2])
        rowi = sb("r_rowi", [P, E2], I32)
        sel = sb("r_sel", [P, 3, G, K])
        seli = sb("r_seli", [P, 3, G, K], I32)
        ovr = sb("r_ovr", [P, 2, K, G])
        hot = sb("r_hot", [P, K, P + 2 * MAX2])
        slotval = sb("r_slotval", [P, G, K, 2])
        tabf = sb("r_tabf", [P, 3, MAX2])
        tbf = sb("r_tbf", [1, 6, 2 * STEP_PAIRS + 2])
        ps_t1, ps_t2, ps_gu = (ps(n, [P, D]) for n in ("sps_t1", "sps_t2", "sps_gu"))
        ps_y = [ps(f"sps_y{i}", [P, D]) for i in range(2)]
        ps_p = ps("sps_p", [P, 2, E2])
        ps_r = ps("sps_r", [P, 2 * MAX2])
        ps_l = [ps("sps_l", [P, 4 * E2]), ps_r[:, 0:4 * E2]]
        block = st.enter_context(nc.Block())
        pairs = TOKENS // P // 2

        @block.sync
        def _(sp):
            def columns(part, t):
                wait(sp, s["lt"], 2 * t.n - 2)
                sp.dma_start(lx[:, t.par], m.hb_dram.rearrange("(p g) n -> p g n", g=G)[:, bass.ds(2 * t.n, 2), 0:D]
                             ).then_inc(lx_sem[t.par], 16)

            pipeline(sp, G // 4, [("columns", 0)], columns)
            raw_sem = (s["raw0"], s["raw1"])
            for e in range(2):
                sp.dma_start(m.raw[:, e, 0:C], m.w13[e].rearrange("(c p) n -> p c n", p=P)).then_inc(raw_sem[e], 16)
                sp.dma_start(m.raw[:, e, C:HL], m.w2[e].rearrange("(c p) n -> p c n", p=P)).then_inc(raw_sem[e], 16)

            def emit(part, t):
                rows = bass.ds(t.n * P, P)
                if part == "load":
                    wait(sp, s["t1"], t.n - 1)
                    sp.dma_start(xg[:, t.par], m.hb_dram[rows, 0:D]).then_inc(gx[t.par], 16)
                elif part == "load_base":
                    wait(sp, s["o"], t.n - 1)
                    sp.dma_start(bs[:, t.par], m.hb_dram[rows, D:2 * D]).then_inc(bsl[t.par], 16)
                elif part == "store":
                    sp.wait_ge(s["o"], t.n + 1)
                    sp.dma_start(m.out[rows, :], o[:, t.par]).then_inc(stl[t.par], 16)

            pipeline(sp, pairs, [("load", 0), ("store", 7), ("load_base", 5)], emit)
            for q in stl:
                sp.wait_ge(q, 16 * pairs)
            sp.wait_ge(s["w_lo"], 1)
            sp.dma_start(m.raw[:, 0, 0:C], m.w13[2].rearrange("(c p) n -> p c n", p=P)).then_inc(raw_sem[0], 16)
            sp.dma_start(m.raw[:, 0, C:HL], m.w2[2].rearrange("(c p) n -> p c n", p=P)).then_inc(raw_sem[0], 16)

        @block.gpsimd
        def _(pool):
            def emit(part, t):
                if part == "a":
                    pool.wait_ge(s["u"], t.n + 1)
                    wait(pool, s["t2"], t.n - 1)
                    nc.gpsimd.tensor_tensor(a[:, t.par], sg_[:, t.par], u_[:, t.par], ALU.mult).then_inc(s["a"], 1)
                elif part == "t1lo":
                    pool.wait_ge(s["t1hi"], t.n + 1)
                    wait(pool, s["g1"], t.n - 1)
                    nc.gpsimd.tensor_tensor(xtl[:, t.par].rearrange("p c n -> p (c n)"), traw[:, t.par],
                                            xth[:, t.par].rearrange("p c n -> p (c n)").bitcast(F32), ALU.subtract).then_inc(s["t1lo"], 1)
                elif part == "t2lo":
                    pool.wait_ge(s["t2hi"], t.n + 1)
                    wait(pool, s["g2"], t.n - 1)
                    nc.gpsimd.tensor_tensor(atl[:, t.par].rearrange("p c n -> p (c n)"), araw[:, t.par],
                                            ath[:, t.par].rearrange("p c n -> p (c n)").bitcast(F32), ALU.subtract).then_inc(s["t2lo"], 1)
                elif part == "o":
                    pool.wait_ge(s["y"], t.n + 1)
                    pool.wait_ge(bsl[t.par], 16 * (t.half + 1))
                    wait(pool, stl[t.par], 16 * t.half)
                    nc.gpsimd.tensor_tensor(o[:, t.par], y[:, t.par], bs[:, t.par], ALU.add).then_inc(s["o"], 1)

            pipeline(pool, pairs, [("t1lo", 0), ("t2lo", 2), ("o", 4), ("a", 1)], emit)
            for e in range(W_SETS):
                pool.wait_ge(s["w_hi"], e + 1)
                nc.gpsimd.tensor_tensor(m.wl[:, e], m.raw[:, e % 2], m.wh[:, e].bitcast(F32), ALU.subtract).then_inc(s["w_lo"], 1)

        @block.tensor
        def _(pe):
            def turn(dst, src, n):
                for c in range(n):
                    mm = pe.transpose(dst[:, c * P:(c + 1) * P], src[:, c * P:(c + 1) * P], m.ident[:])
                return mm

            def emit(part, t):
                if part == "t1":
                    pe.wait_ge(gx[t.par], 16 * (t.half + 1))
                    wait(pe, s["t1hi"], t.n)
                    turn(ps_t1, xg[:, t.par], C).then_inc(s["t1"], 1)
                elif part == "g1":
                    pe.wait_ge(s["t1lo"], t.n + 1)
                    wait(pe, s["u"], t.n)
                    for c in range(C):
                        mm = three_products(pe, ps_gu[:], xth[:, t.par, c], xtl[:, t.par, c], m.wh_s[:, c], m.wl_s[:, c],
                                            c == 0, c == C - 1)
                    mm.then_inc(s["g1"], 1)
                elif part == "t2":
                    pe.wait_ge(s["a"], t.n + 1)
                    wait(pe, s["t2hi"], t.n)
                    turn(ps_t2, a[:, t.par], CI).then_inc(s["t2"], 1)
                elif part == "g2":
                    pe.wait_ge(s["t2lo"], t.n + 1)
                    wait(pe, s["y"], t.n - 1)
                    for c in range(CI):
                        mm = three_products(pe, ps_y[t.par][:], ath[:, t.par, c], atl[:, t.par, c], m.wh_s[:, C + c],
                                            m.wl_s[:, C + c], c == 0, c == CI - 1)
                    mm.then_inc(s["g2"], 1)
                elif part == "prefix" and isinstance(t.n, int) and t.n == COUNTED:
                    pe.wait_ge(s["counted"], 1)
                    pe.matmul(ps_p[:, 0, :], m.before[:], row[:, 0, :], start=True, stop=True)
                    pe.matmul(ps_p[:, 1, :], m.ones[:], row[:, 0, :], start=True, stop=True).then_inc(s["prefix"], 1)

            def logits(part, t):
                if part == "turn":
                    pe.wait_ge(lx_sem[t.par], 16 * (t.half + 1))
                    for j, dst in enumerate((ps_t1, ps_t2)):
                        wait(pe, s["ltlo"], 2 * t.n + (j - 1))
                        turn(dst, lx[:, t.par, j], C).then_inc(s["lt"], 1)
                else:
                    pe.wait_ge(s["ltlo"], 2 * t.n + 2)
                    wait(pe, s["lcopied"], t.n - 1)
                    for j in range(2):
                        both = ps_l[t.par][:, 2 * j * E2:2 * (j + 1) * E2]
                        for c in range(C):
                            rows = slice(c * P, (c + 1) * P)
                            pe.matmul(both, lth[:, t.par, j, rows], m.ghl[:, c, :], start=(c == 0), stop=False,
                                      skip_group_check=True)
                            mm = pe.matmul(both[:, 0:E2], ltl[:, t.par, j, rows], m.ghl[:, c, 0:E2], start=False,
                                           stop=(c == C - 1), skip_group_check=True)
                    mm.then_inc(s["logits"], 1)

            pipeline(pe, G // 4, [("turn", 0), ("logits", 1)], logits)
            pipeline(pe, pairs, [("t1", 0), ("t2", 2), ("g1", 1), ("g2", 3), ("prefix", 0)], emit)

            def slots(g, first):
                for k in range(K):
                    pe.wait_ge(s["hot"], g * K + (k + 1))
                    pe.matmul(ps_r[:], hot[:, k, 0:P], hot[:, k, P:], start=(first and k == 0), stop=False,
                              skip_group_check=True).then_inc(s["table"], 1)

            slots(0, True)
            with pe.Fori(1, G) as g:
                slots(g, False)

        @block.scalar
        def _(act):
            def logits(part, t):
                for j, src in enumerate((ps_t1, ps_t2)):
                    act.wait_ge(s["lt"], 2 * t.n + (j + 1))
                    wait(act, s["logits"], t.n - 1)
                    nc.scalar.activation(lth[:, t.par, j], src[:], ACT.Copy).then_inc(s["lthi"], 1)

            pipeline(act, G // 4, [("columns", 0)], logits)
            act.wait_ge(s["shifted"], 1)
            nc.scalar.activation(prob[:], prob[:], ACT.Exp).then_inc(s["exp"], 1)

            def emit(part, t):
                if part == "silu":
                    act.wait_ge(s["g1"], t.n + 1)
                    wait(act, s["a"], t.n - 1)
                    nc.scalar.activation(sg_[:, t.par], ps_gu[:, 0:INNER], ACT.Silu)
                    nc.scalar.activation(u_[:, t.par], ps_gu[:, INNER:D], ACT.Copy).then_inc(s["u"], 1)
                elif part == "t1":
                    act.wait_ge(s["t1"], t.n + 1)
                    wait(act, s["t1lo"], t.n - 1)
                    nc.scalar.activation(traw[:, t.par], ps_t1[:], ACT.Copy)
                    wait(act, s["g1"], t.n - 1)
                    nc.scalar.activation(xth[:, t.par].rearrange("p c n -> p (c n)"), ps_t1[:], ACT.Copy).then_inc(s["t1hi"], 1)
                elif part == "t2":
                    act.wait_ge(s["t2"], t.n + 1)
                    wait(act, s["t2lo"], t.n - 1)
                    nc.scalar.activation(araw[:, t.par], ps_t2[:, 0:INNER], ACT.Copy)
                    wait(act, s["g2"], t.n - 1)
                    nc.scalar.activation(ath[:, t.par].rearrange("p c n -> p (c n)"), ps_t2[:, 0:INNER], ACT.Copy).then_inc(s["t2hi"], 1)
                elif part == "y":
                    act.wait_ge(s["g2"], t.n + 1)
                    wait(act, s["o"], t.n - 1)
                    nc.scalar.activation(y[:, t.par], ps_y[t.par][:], ACT.Copy).then_inc(s["y"], 1)

            pipeline(act, pairs, [("t1", 0), ("t2", 2), ("y", 4), ("silu", 1)], emit)
            for e in range(W_SETS):
                act.wait_ge((s["raw0"], s["raw1"])[e % 2], 32 * (e // 2 + 1))
                nc.scalar.activation(m.wh[:, e], m.raw[:, e % 2], ACT.Copy).then_inc(s["w_hi"], 1)

        @block.vector
        def _(dve):
            k_ = Chain(dve, s["chain"])
            flat = "p g e -> p (g e)"

            def over_experts(ap):
                return ap.rearrange("p (g o) -> p g o", o=1).to_broadcast([P, G, E2])

            def over_tokens(ap):
                return ap.to_broadcast([P, G, E2])

            def logits(part, t):
                if part == "copy":
                    dve.wait_ge(s["logits"], t.n + 1)
                    parts = ps_l[t.par][:, 0:4 * E2].rearrange("p (g b e) -> p g b e", b=2, e=E2)
                    dve.tensor_copy(low_part[:, t.par], parts[:, :, 1]).then_inc(s["low_copied"], 1)
                    dve.wait_ge(s["low_copied"], t.n + 1)
                    dve.tensor_tensor(prob[:, bass.ds(2 * t.n, 2), :], parts[:, :, 0], low_part[:, t.par], ALU.add).then_inc(s["lcopied"], 1)
                    return
                for j, src in enumerate((ps_t1, ps_t2)):
                    dve.wait_ge(s["lthi"], 2 * t.n + (j + 1))
                    dve.tensor_tensor(ltl[:, t.par, j], src[:], lth[:, t.par, j].bitcast(F32), ALU.subtract).then_inc(s["ltlo"], 1)

            pipeline(dve, G // 4, [("columns", 0), ("copy", 1)], logits)
            dve.wait_ge(s["lcopied"], G // 2)
            k_(dve.tensor_reduce(red[:, 0, :], prob[:], AX.X, ALU.max))
            dve.tensor_tensor(prob[:], prob[:], over_experts(red[:, 0, :]), ALU.subtract).then_inc(s["shifted"], 1)
            dve.wait_ge(s["exp"], 1)
            k_(dve.tensor_reduce(red[:, 1, :], prob[:], AX.X, ALU.add))
            k_(dve.reciprocal(red[:, 2, :], red[:, 1, :]))
            k_(dve.tensor_tensor(prob[:], prob[:], over_experts(red[:, 2, :]), ALU.mult))
            for g in range(G):
                last = dve.max(top8[:, g, :], prob[:, g, :])
            k_(last)
            for g in range(G):
                last = dve.max_index(idx8[:, g, :], top8[:, g, :], prob[:, g, :])
            k_(last)
            dve.tensor_copy(eid[:], idx8[:])
            k_(dve.tensor_reduce(red[:, 3, :], top8[:, :, 0:K], AX.X, ALU.add))
            k_(dve.reciprocal(red[:, 3, :], red[:, 3, :]))
            dve.tensor_tensor(m.topw[:], top8[:, :, 0:K], red[:, 3, :].rearrange("p (g o) -> p g o", o=1).to_broadcast([P, G, K]), ALU.mult)
            for k in range(K):
                last = dve.tensor_tensor(oh[:, k], m.iota_row[:, 0:E2].rearrange("p (o e) -> p o e", o=1).to_broadcast([P, G, E2]),
                                         eid[:, :, k:k + 1].to_broadcast([P, G, E2]), ALU.is_equal)
            k_(last)
            k_(dve.tensor_tensor(M[:], oh[:, 0], oh[:, 1], ALU.add))
            k_(dve.tensor_tensor(tmp[:], oh[:, 2], oh[:, 3], ALU.add))
            k_(dve.tensor_tensor(M[:], M[:], tmp[:], ALU.add))
            dve.tensor_reduce(row[:, 0, :], M[:].rearrange("p g e -> p e g"), AX.X, ALU.add).then_inc(s["counted"], 1)
            k_(dve.memset(rank[:, 0, :], 0.0))
            for g in range(1, G):
                k_(dve.tensor_tensor(rank[:, g, :], rank[:, g - 1, :], M[:, g - 1, :], ALU.add))
            dve.wait_ge(s["prefix"], 1)
            k_(dve.tensor_scalar(row[:, 1, :], ps_p[:, 1, :], float(m.cap), float(P - 1), ALU.min, ALU.add))
            k_(dve.tensor_copy(rowi[:], row[:, 1, :]))
            k_(dve.tensor_scalar(rowi[:], rowi[:], 7, None, ALU.logical_shift_right))
            k_(dve.tensor_copy(row[:, 2, :], rowi[:]))
            k_(dve.tensor_scalar(row[:, 2, :], row[:, 2, :], 1.0, None, ALU.max))
            k_(dve.memset(row[:, 3, :], 0.0))
            k_(dve.tensor_tensor_scan(row[:, 4, :], row[:, 2, :], row[:, 3, :], 0.0, ALU.add, ALU.add))
            k_(dve.tensor_tensor(row[:, 5, :], row[:, 4, :], row[:, 2, :], ALU.subtract))
            k_(dve.tensor_copy(row[:, 7, :], ps_p[:, 0, :]))
            k_(dve.tensor_tensor(rank[:], rank[:], over_tokens(row[:, 7:8, :]), ALU.add))
            k_(dve.tensor_scalar(tmp[:], rank[:], float(m.cap), float(MAX2 * P), ALU.is_ge, ALU.mult))
            k_(dve.tensor_scalar(row[:, 6, :], row[:, 5, :], float(P), None, ALU.mult))
            k_(dve.tensor_tensor(rank[:], rank[:], over_tokens(row[:, 6:7, :]), ALU.add))
            k_(dve.tensor_tensor(rank[:], rank[:], tmp[:], ALU.add))
            k_(dve.tensor_scalar(rank[:], rank[:], float(MAX2 * P), None, ALU.min))
            for k in range(K):
                k_(dve.tensor_tensor(tmp[:], oh[:, k], rank[:], ALU.mult))
                k_(dve.tensor_reduce(sel[:, 0, :, k], tmp[:], AX.X, ALU.add))
            k_(dve.tensor_copy(seli[:, 0], sel[:, 0]))
            dve.tensor_scalar(seli[:, 1], seli[:, 0], 7, None, ALU.logical_shift_right)
            k_(dve.tensor_scalar(seli[:, 2], seli[:, 0], P - 1, None, ALU.bitwise_and))
            dve.tensor_copy(sel[:, 1], seli[:, 1])
            k_(dve.tensor_copy(sel[:, 2], seli[:, 2]))

            dve.tensor_copy(slotval[:, :, :, 0], m.tokcol[:].rearrange("p (g o) -> p g o", o=1).to_broadcast([P, G, K]))
            k_(dve.tensor_copy(slotval[:, :, :, 1], m.topw[:]))

            def one_hot(g):
                for k in range(K):
                    column = lambda t: t[:, bass.ds(g, 1), k:k + 1].rearrange("p a b -> p (a b)")
                    wait(dve, s["table"], (g - 1) * K + k + 1)
                    dve.tensor_scalar(hot[:, k, 0:P], m.iota_row[:], column(sel[:, 2]), None, ALU.is_equal)
                    dve.scalar_tensor_tensor(out=hot[:, k, P:].rearrange("p (v n) -> p v n", v=2),
                                             in0=m.iota_row[:, 0:MAX2].rearrange("p (o n) -> p o n", o=1).to_broadcast([P, 2, MAX2]),
                                             scalar=column(sel[:, 1]),
                                             in1=slotval[:, bass.ds(g, 1), k].rearrange("p a (v o) -> p (a v) o", o=1).to_broadcast([P, 2, MAX2]),
                                             op0=ALU.is_equal, op1=ALU.mult).then_inc(s["hot"], 1)

            one_hot(0)
            with dve.Fori(1, G) as g:
                one_hot(g)

            k_(dve.tensor_scalar(row[:, 6, :], row[:, 4, :], -1.0, None, ALU.add))
            k_(dve.tensor_scalar(red[:, 0, :], m.tokcol[:], m.pad_row[:, 0:1], None, ALU.subtract))
            for k in range(K):
                k_(dve.tensor_tensor(tmp[:], oh[:, k], over_tokens(row[:, 6:7, :]), ALU.mult))
                k_(dve.tensor_reduce(ovr[:, 0, k, :], tmp[:], AX.X, ALU.add))
                k_(dve.tensor_scalar(red[:, 1, :], sel[:, 0, :, k], float(MAX2 * P), None, ALU.is_equal))
                k_(dve.tensor_tensor(ovr[:, 1, k, :], red[:, 1, :], red[:, 0, :], ALU.mult))
            k_(dve.tensor_scalar(ovr[:, 1], ovr[:, 1], m.pad_row[:, 0:1], -1.0, ALU.add, ALU.add))
            dve.tensor_copy(m.over_row[:], ovr[:, 0])
            dve.tensor_copy(m.over_tok[:], ovr[:, 1])
            k_(dve.tensor_copy(m.topk[:], m.topw[:].rearrange("p g k -> p k g")))
            k_(dve.memset(tbf[:], 0.0))
            for first, n in ((0, STEP_PAIRS), (STEP_PAIRS, STEP_PAIRS - 1)):
                cmp = oh[0:1].rearrange("p k g e -> p (k g e)")[:, 0:n * E2].rearrange("p (n e) -> p n e", e=E2)
                k_(dve.tensor_tensor(cmp, m.iota_row[0:1, first:first + n].rearrange("p (n o) -> p n o", o=1).to_broadcast([1, n, E2]),
                                     row[0:1, 4:5, :].to_broadcast([1, n, E2]), ALU.is_ge))
                k_(dve.tensor_reduce(tbf[:, 0, BACK2 + first:BACK2 + first + n], cmp, AX.X, ALU.add))
            k_(dve.tensor_scalar(tbf[:, 0, :], tbf[:, 0, :], float(E2 - 1), None, ALU.min))
            k_(dve.tensor_tensor(tbf[:, 1, BACK2 + 1:], tbf[:, 0, BACK2 + 1:], tbf[:, 0, BACK2:-1], ALU.subtract))
            k_(dve.tensor_scalar(tbf[:, 2, :], tbf[:, 0, :], 2.0, None, ALU.add))
            k_(dve.tensor_tensor(tbf[:, 1, :], tbf[:, 1, :], tbf[:, 2, :], ALU.mult))
            k_(dve.tensor_scalar(tbf[:, 2, :], tbf[:, 1, :], float(E2 - 1), None, ALU.is_le))
            k_(dve.tensor_tensor(tbf[:, 1, :], tbf[:, 1, :], tbf[:, 2, :], ALU.mult))
            for r in range(2):
                pack(dve, k_, tbf[:, 2 + r, 0:STEP_PAIRS], tbf[:, r, :], BACK2, E2, STEP_PAIRS)
            k_(dve.tensor_copy(m.tab2[:, 0:2, :], tbf[:, 2:4, 0:STEP_PAIRS]))
            k_(dve.tensor_scalar(tbf[:, 4, 0:1], row[0:1, 4, E2 - 1:E2], float(1 - 2 * MIN_PAIRS), None, ALU.add))
            k_(dve.tensor_copy(m.tab2[:, 2, 0:1], tbf[:, 4, 0:1]))
            k_(dve.tensor_scalar(m.tab2[:, 2, 0:1], m.tab2[:, 2, 0:1], 1, None, ALU.logical_shift_right))
            k_(dve.tensor_reduce(tbf[:, 5, 0:1], ps_p[0:1, 1, :], AX.X, ALU.max))
            k_(dve.tensor_scalar(tbf[:, 5, 0:1], tbf[:, 5, 0:1], float(m.cap), None, ALU.is_gt))
            k_(dve.tensor_copy(m.tab2[:, 2, 1:2], tbf[:, 5, 0:1]))
            dve.wait_ge(s["table"], G * K)
            k_(dve.tensor_scalar(tabf[:, 0, :], ps_r[:, 0:MAX2], 0.0, m.pad_row[:, 0:1], ALU.is_equal, ALU.mult))
            k_(dve.scalar_tensor_tensor(out=tabf[:, 1, :], in0=ps_r[:, 0:MAX2], scalar=-1.0, in1=tabf[:, 0, :],
                                        op0=ALU.add, op1=ALU.add))
            dve.tensor_copy(m.scatter2[:], tabf[:, 1, :])
            k_(dve.tensor_scalar(tabf[:, 2, :], tabf[:, 1, :], float(TOKENS - 1), None, ALU.min))
            k_(dve.tensor_scalar(m.gather2[:], tabf[:, 2, :], 2.0, None, ALU.mult))
            k_(dve.tensor_copy(m.weight2[:], ps_r[:, MAX2:]))


def experts(nc, m):
    with ExitStack() as st:
        def sb(name, shape, dt=F32):
            return m.sb(name, shape, dt, st)

        def ps(name, shape):
            return st.enter_context(nc.psum_tensor(name, shape, F32))

        s = semaphores(nc, st, "e_", (
            "gx0", "gx1", "gi", "si", "add0", "add1", "t1", "t1hi", "t1lo", "g1", "sil", "a", "t2", "t2hi", "t2lo", "g2",
            "y", "last0", "last1", "raw", "w_hi", "w_lo", "lastrow", "carried"))
        gx, add, lst = (s["gx0"], s["gx1"]), (s["add0"], s["add1"]), (s["last0"], s["last1"])
        xg = sb("e_xg", [P, 2, D])
        xth = sb("e_xth", [P, 2, C, P], F32R)
        xtl = sb("e_xtl", [P, 2, C, P], F32R)
        a = sb("e_a", [P, 2, INNER])
        ath = sb("e_ath", [P, 2, CI, P], F32R)
        atl = sb("e_atl", [P, 2, CI, P], F32R)
        y = sb("e_y", [P, 2, D])
        lastrow = sb("e_lastrow", [P, 2, D])
        gidx = sb("e_gidx", [P, 2], I32)
        sidx = sb("e_sidx", [P, 2], I32)
        ps_t1, ps_t2, ps_gu = (ps(n, [P, D]) for n in ("eps_t1", "eps_t2", "eps_gu"))
        ps_y = [ps(f"eps_y{i}", [P, D]) for i in range(2)]
        hn_rows = m.hb_dram.rearrange("t (a n) -> (t a) n", a=2)
        block = st.enter_context(nc.Block())

        ROWS = {"rows_c": (4, 5), "rows_b": (2, 3), "rows_a": (0, 1)}
        ROW_SKEWS = [("rows_c", 3), ("rows_b", 2), ("rows_a", 1)]

        @block.sync
        def _(sp):
            pairs = number_of_pairs(sp, m.tab2[0:1, 2, 0:1], MAX2)
            split = {}

            def load(e, par):
                ex = bass.ds(e, 1)
                sp.dma_start(m.raw[:, par, 0:C], m.w13[ex].rearrange("o (c p) n -> p (o c) n", p=P)).then_inc(s["raw"], 16)
                sp.dma_start(m.raw[:, par, C:HL], m.w2[ex].rearrange("o (c p) n -> p (o c) n", p=P)).then_inc(s["raw"], 16)

            def emit(part, t):
                if part == "load":
                    e = split[t.off]
                    with sp.If(e > 0):
                        with sp.If(e < E2 - 2):
                            sp.wait_ge(s["w_lo"], HL * e + HL)
                            sp.wait_ge(s["raw"], 32 * e + 64)
                            load((e + 2) % E2, bass.ds(e % 2, 1))
                elif part == "last_row":
                    sp.wait_ge(s["lastrow"], t.n + 1)
                    sp.dma_start(m.last_dram[bass.ds(t.n, 1), :], lastrow[P - 1:P, t.par]).then_inc(lst[t.par], 16)

            sp.sem_inc(s["raw"], 32 * W_SETS)
            load(W_SETS, slice(1, 2))
            sp.wait_ge(s["raw"], 32 * (W_SETS + 1))
            load(W_SETS + 1, slice(0, 1))
            pipeline(sp, pairs, [("load", 1), ("last_row", 2)], emit, looked_up(sp, m.tab2[0:1, 1, :], BACK2, E2, split))
            for q in lst:
                sp.wait_ge(q, 16 * pairs)
            sp.sem_inc(s["carried"], 1)

        @block.gpsimd
        def _(pool):
            pairs = number_of_pairs(pool, m.tab2[0:1, 2, 0:1], MAX2)

            def emit(part, t):
                if part == "gather":
                    wait(pool, s["t1"], t.n - 1)
                    wait(pool, gx[t.par], 16 * t.half)
                    m.carry(pool)
                    nc.gpsimd.tensor_copy(gidx[:, t.par:t.par + 1], m.gather2[:, bass.ds(t.n, 1)]).then_inc(s["gi"], 1)
                    pool.wait_ge(s["gi"], t.n + 1)
                    m.carry(pool)
                    pool.indirect_dma_start(xg[:, t.par], None, hn_rows, bass.IndirectOffsetOnAxis(ap=gidx[:, t.par:t.par + 1], axis=0)
                                            ).then_inc(gx[t.par], 16)
                elif part == "add":
                    wait(pool, add[t.par], 16 * t.half)
                    m.carry(pool)
                    nc.gpsimd.tensor_copy(sidx[:, t.par:t.par + 1], m.scatter2[:, bass.ds(t.n, 1)]).then_inc(s["si"], 1)
                    pool.wait_ge(s["si"], t.n + 1)
                    pool.wait_ge(s["y"], t.n + 1)
                    wait(pool, add[1 - t.par], 16 * (t.half + t.par))
                    m.carry(pool)
                    pool.indirect_dma_start(m.out, bass.IndirectOffsetOnAxis(ap=sidx[:, t.par:t.par + 1], axis=0), y[:, t.par], None,
                                            compute_op=ALU.add).then_inc(add[t.par], 16)

            pipeline(pool, pairs, [("gather", 0), ("add", 6)], emit)
            for q in add:
                pool.wait_ge(q, 16 * pairs)
            m.carry(pool)

        @block.tensor
        def _(pe):
            pairs = number_of_pairs(pe, m.tab2[0:1, 2, 0:1], MAX2)

            def turn(dst, src, n):
                for c in range(n):
                    mm = pe.transpose(dst[:, c * P:(c + 1) * P], src[:, c * P:(c + 1) * P], m.ident[:])
                return mm

            expert = {}

            def emit(part, t):
                if part == "t1":
                    pe.wait_ge(gx[t.par], 16 * (t.half + 1))
                    wait(pe, s["t1lo"], t.n)
                    turn(ps_t1, xg[:, t.par], C).then_inc(s["t1"], 1)
                elif part == "g1":
                    w = bass.ds(expert[t.off] % W_SETS, 1)
                    pe.wait_ge(s["w_lo"], HL * expert[t.off] + C)
                    pe.wait_ge(s["t1lo"], t.n + 1)
                    wait(pe, s["a"], t.n)
                    for c in range(C):
                        mm = three_products(pe, ps_gu[:], xth[:, t.par, c], xtl[:, t.par, c], m.wh[:, w, c, :], m.wl[:, w, c, :],
                                            c == 0, c == C - 1)
                    mm.then_inc(s["g1"], 1)
                elif part == "t2":
                    pe.wait_ge(s["a"], t.n + 1)
                    wait(pe, s["t2lo"], t.n)
                    turn(ps_t2, a[:, t.par], CI).then_inc(s["t2"], 1)
                elif part == "g2":
                    w = bass.ds(expert[t.off] % W_SETS, 1)
                    pe.wait_ge(s["w_lo"], HL * expert[t.off] + HL)
                    pe.wait_ge(s["t2lo"], t.n + 1)
                    wait(pe, s["lastrow"], t.n - 1)
                    for c in range(CI):
                        mm = three_products(pe, ps_y[t.par][:], ath[:, t.par, c], atl[:, t.par, c], m.wh[:, w, C + c, :],
                                            m.wl[:, w, C + c, :], c == 0, c == CI - 1)
                    mm.then_inc(s["g2"], 1)

            pipeline(pe, pairs, [("t1", 0), ("t2", 2), ("g1", 1), ("g2", 3)], emit, looked_up(pe, m.tab2[0:1, 0, :], BACK2, E2, expert))

        @block.scalar
        def _(act):
            pairs = number_of_pairs(act, m.tab2[0:1, 2, 0:1], MAX2)
            act.sem_inc(s["w_hi"], HL * W_SETS)
            split = {}

            def emit(part, t):
                if part == "silu":
                    act.wait_ge(s["g1"], t.n + 1)
                    wait(act, s["t2"], t.n - 1)
                    nc.scalar.activation(a[:, t.par], ps_gu[:, 0:INNER], ACT.Silu).then_inc(s["sil"], 1)
                elif part == "t1hi":
                    act.wait_ge(s["t1"], t.n + 1)
                    wait(act, s["g1"], t.n - 1)
                    nc.scalar.activation(xth[:, t.par].rearrange("p c n -> p (c n)"), ps_t1[:], ACT.Copy).then_inc(s["t1hi"], 1)
                elif part == "t2hi":
                    act.wait_ge(s["t2"], t.n + 1)
                    wait(act, s["g2"], t.n - 1)
                    nc.scalar.activation(ath[:, t.par].rearrange("p c n -> p (c n)"), ps_t2[:, 0:INNER], ACT.Copy).then_inc(s["t2hi"], 1)
                elif part == "y":
                    act.wait_ge(s["g2"], t.n + 1)
                    wait(act, add[t.par], 16 * t.half)
                    nc.scalar.activation(y[:, t.par], ps_y[t.par][:], ACT.Copy, scale=m.weight2[:, bass.ds(t.n, 1)]).then_inc(s["y"], 1)
                    wait(act, lst[t.par], 16 * t.half)
                    nc.scalar.activation(lastrow[96:P, t.par], ps_y[t.par][96:P, :], ACT.Copy).then_inc(s["lastrow"], 1)
                elif part in ROWS:
                    e = split[t.off]
                    with act.If(e > 0):
                        act.wait_ge(s["raw"], 32 * e + 32)
                        wait(act, s["g2" if part == "rows_c" else "g1"], t.n)
                        for r in ROWS[part]:
                            nc.scalar.activation(m.wh[:, bass.ds(e % W_SETS, 1), r, :], m.raw[:, bass.ds(e % 2, 1), r, :],
                                                 ACT.Copy).then_inc(s["w_hi"], 1)

            pipeline(act, pairs, [("t1hi", 0), ("t2hi", 2), *ROW_SKEWS, ("y", 4), ("silu", 1)], emit,
                     looked_up(act, m.tab2[0:1, 1, :], BACK2, E2, split))

        @block.vector
        def _(dve):
            pairs = number_of_pairs(dve, m.tab2[0:1, 2, 0:1], MAX2)
            dve.sem_inc(s["w_lo"], HL * W_SETS)
            split = {}

            def emit(part, t):
                if part == "a":
                    dve.wait_ge(s["sil"], t.n + 1)
                    dve.tensor_tensor(a[:, t.par], a[:, t.par], ps_gu[:, INNER:D], ALU.mult).then_inc(s["a"], 1)
                elif part == "t1lo":
                    dve.wait_ge(s["t1hi"], t.n + 1)
                    dve.tensor_tensor(xtl[:, t.par].rearrange("p c n -> p (c n)"), ps_t1[:],
                                      xth[:, t.par].rearrange("p c n -> p (c n)").bitcast(F32), ALU.subtract).then_inc(s["t1lo"], 1)
                elif part == "t2lo":
                    dve.wait_ge(s["t2hi"], t.n + 1)
                    dve.tensor_tensor(atl[:, t.par].rearrange("p c n -> p (c n)"), ps_t2[:, 0:INNER],
                                      ath[:, t.par].rearrange("p c n -> p (c n)").bitcast(F32), ALU.subtract).then_inc(s["t2lo"], 1)
                elif part in ROWS:
                    e = split[t.off]
                    w = bass.ds(e % W_SETS, 1)
                    with dve.If(e > 0):
                        for r in ROWS[part]:
                            dve.wait_ge(s["w_hi"], HL * e + (r + 1))
                            dve.tensor_tensor(m.wl[:, w, r, :], m.raw[:, bass.ds(e % 2, 1), r, :],
                                              m.wh[:, w, r, :].bitcast(F32), ALU.subtract).then_inc(s["w_lo"], 1)

            pipeline(dve, pairs, [("t1lo", 0), ("t2lo", 2), *ROW_SKEWS, ("a", 1)], emit,
                     looked_up(dve, m.tab2[0:1, 1, :], BACK2, E2, split))


def overflow(nc, m):
    with ExitStack() as st:
        s = semaphores(nc, st, "o_", ("rows", "add", "idx", "y"))
        rows = m.sb("o_rows", [P, D], F32, st)
        y = m.sb("o_y", [P, D], F32, st)
        ridx = m.sb("o_ridx", [P, 1], I32, st)
        tidx = m.sb("o_tidx", [P, 1], I32, st)
        wcol = m.sb("o_wcol", [P, 1], F32, st)
        block = st.enter_context(nc.Block())

        @block.gpsimd
        def _(pool):
            flag = pool.value_load(m.tab2[0:1, 2, 1:2], min_val=0, max_val=1)
            with pool.If(flag > 0):
                with pool.Fori(0, K * G) as i:
                    one = bass.ds(i, 1)
                    nc.gpsimd.tensor_copy(ridx[:], m.over_row[:].rearrange("p k g -> p (k g)")[:, one])
                    nc.gpsimd.tensor_copy(tidx[:], m.over_tok[:].rearrange("p k g -> p (k g)")[:, one])
                    nc.gpsimd.tensor_copy(wcol[:], m.topk[:].rearrange("p k g -> p (k g)")[:, one]).then_inc(s["idx"], 1)
                    pool.wait_ge(s["idx"], i + 1)
                    m.carry(pool)
                    pool.indirect_dma_start(rows[:], None, m.last_dram, bass.IndirectOffsetOnAxis(ap=ridx[:, 0:1], axis=0)
                                            ).then_inc(s["rows"], 16)
                    pool.wait_ge(s["rows"], 16 * (i + 1))
                    m.carry(pool)
                    nc.gpsimd.tensor_scalar(y[:], rows[:], wcol[:, 0:1], 0.0, ALU.mult, ALU.add).then_inc(s["y"], 1)
                    pool.wait_ge(s["y"], i + 1)
                    m.carry(pool)
                    pool.indirect_dma_start(m.out, bass.IndirectOffsetOnAxis(ap=tidx[:, 0:1], axis=0), y[:], None,
                                            compute_op=ALU.add).then_inc(s["add"], 16)
                    pool.wait_ge(s["add"], 16 * (i + 1))
                    m.carry(pool)



def kernel(x, itok_BxS_13_99985, ctx_2048, L0_ffn_norm_w, L0_ffn_gate_w, L0_ffn_w13, L0_ffn_w2,
           L0_ffn_shared_gate_w, L0_ffn_shared_up_w, L0_ffn_shared_down_w):
    import numpy as np
    import concourse.bacc as bacc
    from concourse.bass_utils import run_bass_kernel_spmd

    nc = bacc.Bacc("TRN2", target_bir_lowering=False, num_devices=1)
    arrays = {
        "x": x.reshape(TOKENS, D), "tid": itok_BxS_13_99985.reshape(P, G), "ctx_w": ctx_2048,
        "norm_w": L0_ffn_norm_w.reshape(1, D), "gate_w": L0_ffn_gate_w, "w13": L0_ffn_w13, "w2": L0_ffn_w2,
        "sg": L0_ffn_shared_gate_w, "su": L0_ffn_shared_up_w, "sd": L0_ffn_shared_down_w,
    }
    arrays = {"in_" + n: np.ascontiguousarray(a) for n, a in arrays.items()}
    given = {n: nc.dram_tensor(n, a.shape, mybir.dt.from_np(a.dtype), kind="ExternalInput").ap() for n, a in arrays.items()}
    m = Memory()
    m.cap = CAP
    m.x, m.tid, m.ctx_w, m.norm_w = given["in_x"], given["in_tid"], given["in_ctx_w"], given["in_norm_w"]
    m.gate_w, m.w13, m.w2 = given["in_gate_w"], given["in_w13"], given["in_w2"]
    m.sg, m.su, m.sd = given["in_sg"], given["in_su"], given["in_sd"]
    m.out = nc.dram_tensor("out", (TOKENS + PAD, D), F32, kind="ExternalOutput").ap()
    m.hb_dram = nc.dram_tensor("hb_dram", (TOKENS, 2 * D), F32, kind="Internal").ap()
    m.last_dram = nc.dram_tensor("last_dram", (MAX2, D), F32, kind="Internal").ap()
    build(nc, m)
    result = run_bass_kernel_spmd(nc, [arrays], core_ids=[0])
    return result.results[0]["out"][:TOKENS].reshape(4, 512, D)
```

```python
from contextlib import ExitStack

import concourse.bass as bass
from concourse import mybir

F32 = mybir.dt.float32
F32R = mybir.dt.float32r
BF16 = mybir.dt.bfloat16
I32 = mybir.dt.int32
U32 = mybir.dt.uint32
ALU = mybir.AluOpType
ACT = mybir.ActivationFunctionType
AX = mybir.AxisListType

P = 128
D = 512
C = D // P
TOKENS = 2048
G = TOKENS // P
E1 = 4
VOCAB = 25000
PER_EXPERT = VOCAB // E1
E2 = 32
K = 4
INNER = 256
CI = INNER // P
CAP = 2 * TOKENS * K // E2
MAX1 = 20
MAX2 = 96
MIN_PAIRS = 8
BACK1 = 5
BACK2 = 3
STEP_PAIRS1 = MAX1 // 2 + 1
STEP_PAIRS = MAX2 // 2 + 1
PAD = P
LN_EPS = 1e-5
RMS_EPS = 1e-6
W_SETS = 3
HL = C + CI


class Memory:
    pass


class Tile:

    def __init__(self, pair, off):
        self.off = off
        self.n = 2 * pair + off
        self.half = pair + off // 2
        self.par = off % 2


def wait(eng, sem, value):
    if isinstance(value, int) and value <= 0:
        return
    eng.wait_ge(sem, value)


def pipeline(eng, pairs, skews, emit, look=lambda pair: None):
    deepest = max(s for _, s in skews)
    first = (deepest + 3) // 2
    for pair in range(first):
        look(pair)
        for b in range(2):
            for part, s in skews:
                if 2 * pair + b - s >= 0:
                    emit(part, Tile(pair, b - s))
    with eng.Fori(first, pairs) as pair:
        look(pair)
        for b in range(2):
            for part, s in skews:
                emit(part, Tile(pair, b - s))
    look(pairs)
    for b in range(deepest):
        for part, s in skews:
            if b - s < 0:
                emit(part, Tile(pairs, b - s))


class Chain:

    def __init__(self, eng, sem):
        self.eng, self.sem, self.n = eng, sem, 0

    def __call__(self, ins):
        self.n += 1
        ins.then_inc(self.sem, 1)
        self.eng.wait_ge(self.sem, self.n)


def tensors(nc, m, top):
    sb = m.sb
    m.ident = sb("ident", [P, P], F32, top)
    m.before = sb("before", [P, P], F32, top)
    m.ones = sb("ones", [P, P], F32, top)
    m.iota_row = sb("iota_row", [P, P], F32, top)
    m.part_id = sb("part_id", [P, 1], F32, top)
    m.pad_row = sb("pad_row", [P, 1], F32, top)
    m.minus_half = sb("minus_half", [P, 1], F32, top)
    m.tokcol = sb("tokcol", [P, G], F32, top)
    m.normw = sb("normw", [P, D], F32, top)
    m.ghl = sb("ghl", [P, C, 2 * E2], F32R, top)
    m.gather1 = sb("gather1", [P, MAX1], I32, top)
    m.scatter1 = sb("scatter1", [P, MAX1], I32, top)
    m.tab1 = sb("tab1", [1, 2, STEP_PAIRS1], I32, top)
    m.gather2 = sb("gather2", [P, MAX2], I32, top)
    m.scatter2 = sb("scatter2", [P, MAX2], I32, top)
    m.weight2 = sb("weight2", [P, MAX2], F32, top)
    m.tab2 = sb("tab2", [1, 3, STEP_PAIRS], I32, top)
    m.over_row = sb("over_row", [P, K, G], I32, top)
    m.over_tok = sb("over_tok", [P, K, G], I32, top)
    m.topw = sb("topw", [P, G, K], F32, top)
    m.topk = sb("topk", [P, K, G], F32, top)
    m.wh_s = sb("wh_s", [P, HL, D], F32R, top)
    m.wl_s = sb("wl_s", [P, HL, D], F32R, top)


def number_of_pairs(eng, entry, most):
    return eng.value_load(entry, min_val=0, max_val=most // 2 - MIN_PAIRS) + MIN_PAIRS


def pack(dve, k, packed, entries, back, base, pairs):
    two = entries.rearrange("p (q b) -> p b q", b=2)
    digit = lambda i: two[:, i % 2, i // 2:i // 2 + pairs]
    k(dve.tensor_copy(packed, digit(back)))
    for i in range(back - 1, -1, -1):
        k(dve.scalar_tensor_tensor(out=packed, in0=packed, scalar=float(base), in1=digit(i), op0=ALU.mult, op1=ALU.add))


def looked_up(eng, row, back, base, found):
    def look(pair):
        v = eng.value_load(row[:, bass.ds(pair, 1)], min_val=0, max_val=base ** (back + 1) - 1)
        for i in range(back + 1):
            found[i - back] = (v // base ** i) % base
    return look


def semaphores(nc, stack, prefix, names):
    return {n: stack.enter_context(nc.semaphore(prefix + n)) for n in names}


def three_products(pe, acc, left_hi, left_lo, right_hi, right_lo, start, stop):
    pe.matmul(acc, left_hi, right_hi, start=start, stop=False)
    pe.matmul(acc, left_hi, right_lo, start=False, stop=False)
    return pe.matmul(acc, left_lo, right_hi, start=False, stop=stop)


def setup(nc, m):
    with ExitStack() as st:
        def ps(name, shape, dt=F32):
            return st.enter_context(nc.psum_tensor(name, shape, dt))
        BUFS = 5
        craw = m.sb("craw", [P, E1, C, D], F32, st)
        sraw = m.sb("sraw", [P, HL, D], F32, st)
        graw = m.sb("graw", [E2, D], F32, st)
        zeros = m.sb("zeros", [P, D], F32, st)
        tidi = m.sb("tidi", [P, G], I32, st)
        tidf = m.sb("tidf", [P, G], F32, st)
        M = m.sb("M1", [P, G, E1], F32, st)
        reach = m.sb("reach1", [P, E1 + 1, G], F32, st)
        slots = m.sb("slots1", [P, G, E1], F32, st)
        row = m.sb("row1", [P, 8, E1], F32, st)
        rowi = m.sb("row1i", [P, E1], I32, st)
        sel = m.sb("sel1", [P, 4, G], F32, st)
        seli = m.sb("sel1i", [P, 3, G], I32, st)
        hot = m.sb("hot1", [P, G, P + MAX1], F32, st)
        tabf = m.sb("tab1f", [P, 3, MAX1], F32, st)
        cmp = m.sb("cmp1", [1, MAX1 + 1, E1], F32, st)
        tbf = m.sb("tb1f", [1, 2, BACK1 + MAX1 + 1], F32, st)
        psC = [ps(f"psC{i}", [P, D]) for i in range(BUFS)]
        psG = ps("psG", [P, C, E2])
        psP = ps("psP", [P, 2, E1])
        psR = ps("psR", [P, MAX1])
        block = st.enter_context(nc.Block())

        @block.sync
        def _(sp):
            sp.dma_start(tidi[:], m.tid).then_inc(m.s["tid_loaded"], 16)
            sp.dma_start(sraw[:, 0:C, 0:INNER], m.sg.rearrange("(c p) n -> p c n", p=P)).then_inc(m.s["sh_loaded"], 16)
            sp.dma_start(sraw[:, 0:C, INNER:D], m.su.rearrange("(c p) n -> p c n", p=P)).then_inc(m.s["sh_loaded"], 16)
            sp.dma_start(sraw[:, C:HL, :], m.sd.rearrange("(c p) n -> p c n", p=P)).then_inc(m.s["sh_loaded"], 16)
            for e in range(E1):
                if e >= 2:
                    sp.wait_ge(m.s[f"ctx_loaded{e % 2}"], 16)
                sp.dma_start(craw[:, e], m.ctx_w[e].rearrange("(c p) n -> p c n", p=P)).then_inc(m.s[f"ctx_loaded{e % 2}"], 16)
                if e == 1:
                    sp.dma_start(graw[:], m.gate_w).then_inc(m.s["gate_loaded"], 16)
                    sp.dma_start(m.normw[:], m.norm_w.to_broadcast([P, D])).then_inc(m.s["norm_loaded"], 16)
            sp.wait_ge(m.s["consts"], 1)
            sp.dma_start(m.out[TOKENS:TOKENS + PAD, :], zeros[:]).then_inc(m.s["zero_pad"], 16)
            sp.dma_start(m.last_dram, zeros[0:MAX2, :]).then_inc(m.s["zero_pad"], 16)
            sp.wait_ge(m.s["zero_pad"], 32)
            sp.wait_ge(m.s["norm_loaded"], 16)

        @block.gpsimd
        def _(pool):
            k = Chain(pool, m.s["chain0"])
            nc.gpsimd.memset(zeros[:], 0.0).then_inc(m.s["consts"], 1)
            nc.gpsimd.memset(m.minus_half[:], -0.5)
            k(nc.gpsimd.memset(m.ones[:], 1.0))
            k(nc.gpsimd.affine_select(out=m.ident[:], in_=m.ones[:], compare_op=ALU.is_equal, fill=0.0, base=0,
                                      pattern=[[-1, P]], channel_multiplier=1))
            k(nc.gpsimd.affine_select(out=m.before[:], in_=m.ones[:], compare_op=ALU.is_gt, fill=0.0, base=0,
                                      pattern=[[1, P]], channel_multiplier=-1))
            nc.gpsimd.iota(m.iota_row[:], pattern=[[1, P]], base=0, channel_multiplier=0,
                           allow_small_or_imprecise_dtypes=True)
            nc.gpsimd.iota(m.part_id[:], pattern=[[0, 1]], base=0, channel_multiplier=1,
                           allow_small_or_imprecise_dtypes=True)
            nc.gpsimd.iota(m.pad_row[:], pattern=[[0, 1]], base=TOKENS + 1, channel_multiplier=1,
                           allow_small_or_imprecise_dtypes=True)
            nc.gpsimd.iota(m.tokcol[:], pattern=[[1, G]], base=1, channel_multiplier=G,
                           allow_small_or_imprecise_dtypes=True).then_inc(m.s["consts"], 1)
            pool.wait_ge(m.s["sh_hi"], 1)
            nc.gpsimd.tensor_tensor(m.wl_s[:], sraw[:], m.wh_s[:].bitcast(F32), ALU.subtract)

        @block.tensor
        def _(pe):
            pe.wait_ge(m.s["consts"], 2)
            pe.wait_ge(m.s["counted"], 1)
            pe.matmul(psP[:, 0, :], m.before[:], row[:, 0, :], start=True, stop=True)
            pe.matmul(psP[:, 1, :], m.ones[:], row[:, 0, :], start=True, stop=True).then_inc(m.s["prefix"], 1)
            for e in range(E1):
                pe.wait_ge(m.s[f"ctx_loaded{e % 2}"], 16 * (e // 2 + 1))
                for c in range(C):
                    n = e * C + c
                    if n >= BUFS:
                        pe.wait_ge(m.s["ctx_split"], n - BUFS + 1)
                    for r in range(C):
                        mm = pe.transpose(psC[n % BUFS][:, r * P:(r + 1) * P],
                                          craw[:, e, r, c * P:(c + 1) * P], m.ident[:])
                    mm.then_inc(m.s["ctx_turned"], 1)
                    if n == BUFS - 1:
                        for i in range(G):
                            pe.wait_ge(m.s["onehot"], i + 1)
                            mm = pe.matmul(psR[:], hot[:, i, 0:P], hot[:, i, P:P + MAX1], start=(i == 0), stop=(i == G - 1))
                        mm.then_inc(m.s["table"], 1)
                        pe.wait_ge(m.s["gate_loaded"], 16)
                        for r in range(C):
                            mm = pe.transpose(psG[:, r, :], graw[:, r * P:(r + 1) * P], m.ident[0:E2, 0:E2])
                        mm.then_inc(m.s["gate_turned"], 1)

        @block.scalar
        def _(act):
            act.wait_ge(m.s["sh_loaded"], 48)
            nc.scalar.activation(m.wh_s[:], sraw[:], ACT.Copy).then_inc(m.s["sh_hi"], 1)
            for n in range(E1 * C):
                act.wait_ge(m.s["ctx_turned"], n + 1)
                nc.scalar.activation(m.cth[:, n // C, n % C, :], psC[n % BUFS][:], ACT.Copy).then_inc(m.s["ctx_hi"], 1)
                if n == BUFS - 1:
                    act.wait_ge(m.s["gate_turned"], 1)
                    nc.scalar.activation(m.ghl[:, :, 0:E2], psG[:], ACT.Copy).then_inc(m.s["gate_hi"], 1)

        @block.vector
        def _(dve):
            k = Chain(dve, m.s["chain1"])

            def low(n):
                dve.wait_ge(m.s["ctx_hi"], n + 1)
                dve.tensor_tensor(m.ctl[:, n // C, n % C, :], psC[n % BUFS][:], m.cth[:, n // C, n % C, :].bitcast(F32),
                                  ALU.subtract).then_inc(m.s["ctx_split"], 1)

            dve.wait_ge(m.s["tid_loaded"], 16)
            k(dve.tensor_copy(tidf[:], tidi[:]))
            dve.memset(reach[:, 0, :], 1.0)
            dve.memset(reach[:, E1, :], 0.0)
            for e in range(1, E1):
                ins = dve.tensor_scalar(reach[:, e, :], tidf[:], float(e * PER_EXPERT), None, ALU.is_ge)
            k(ins)
            k(dve.tensor_tensor(M[:], reach[:, 0:E1, :].rearrange("p e g -> p g e"),
                                reach[:, 1:E1 + 1, :].rearrange("p e g -> p g e"), ALU.subtract))
            dve.tensor_reduce(row[:, 0, :], M[:].rearrange("p g e -> p e g"), AX.X, ALU.add).then_inc(m.s["counted"], 1)
            k(dve.memset(slots[:, 0, :], 0.0))
            for g in range(1, G):
                k(dve.tensor_tensor(slots[:, g, :], slots[:, g - 1, :], M[:, g - 1, :], ALU.add))
            dve.wait_ge(m.s["prefix"], 1)
            k(dve.tensor_scalar(row[:, 1, :], psP[:, 1, :], float(P - 1), None, ALU.add))
            k(dve.tensor_copy(rowi[:], row[:, 1, :]))
            k(dve.tensor_scalar(rowi[:], rowi[:], 7, None, ALU.logical_shift_right))
            k(dve.tensor_copy(row[:, 2, :], rowi[:]))
            k(dve.memset(row[:, 3, :], 0.0))
            k(dve.tensor_tensor_scan(row[:, 4, :], row[:, 2, :], row[:, 3, :], 0.0, ALU.add, ALU.add))
            k(dve.tensor_tensor(row[:, 5, :], row[:, 4, :], row[:, 2, :], ALU.subtract))
            k(dve.scalar_tensor_tensor(out=row[:, 6, :], in0=row[:, 5, :], scalar=float(P), in1=psP[:, 0, :],
                                       op0=ALU.mult, op1=ALU.add))
            k(dve.tensor_tensor(slots[:], slots[:], row[:, 6:7, :].to_broadcast([P, G, E1]), ALU.add))
            k(dve.tensor_tensor(slots[:], slots[:], M[:], ALU.mult))
            k(dve.tensor_reduce(sel[:, 0, :], slots[:], AX.X, ALU.add))
            k(dve.tensor_copy(seli[:, 0, :], sel[:, 0, :]))
            dve.tensor_scalar(seli[:, 1, :], seli[:, 0, :], 7, None, ALU.logical_shift_right)
            k(dve.tensor_scalar(seli[:, 2, :], seli[:, 0, :], P - 1, None, ALU.bitwise_and))
            dve.tensor_copy(sel[:, 1, :], seli[:, 1, :])
            k(dve.tensor_copy(sel[:, 2, :], seli[:, 2, :]))
            dve.wait_ge(m.s["consts"], 2)
            for i in range(G):
                dve.tensor_scalar(hot[:, i, 0:P], m.iota_row[:], sel[:, 2, i:i + 1], None, ALU.is_equal)
                dve.tensor_scalar(hot[:, i, P:P + MAX1], m.iota_row[:, 0:MAX1], sel[:, 1, i:i + 1],
                                  m.tokcol[:, i:i + 1], ALU.is_equal, ALU.mult).then_inc(m.s["onehot"], 1)
            for n in range(BUFS):
                low(n)
            dve.wait_ge(m.s["gate_hi"], 1)
            dve.tensor_tensor(m.ghl[:, :, E2:], psG[:], m.ghl[:, :, 0:E2].bitcast(F32), ALU.subtract)
            for n in range(BUFS, 2 * BUFS):
                low(n)
            dve.wait_ge(m.s["table"], 1)
            k(dve.tensor_scalar(tabf[:, 0, :], psR[:], 0.0, m.pad_row[:, 0:1], ALU.is_equal, ALU.mult))
            k(dve.scalar_tensor_tensor(out=tabf[:, 1, :], in0=psR[:], scalar=-1.0, in1=tabf[:, 0, :],
                                       op0=ALU.add, op1=ALU.add))
            dve.tensor_copy(m.scatter1[:], tabf[:, 1, :])
            k(dve.tensor_scalar(tabf[:, 2, :], tabf[:, 1, :], float(TOKENS - 1), None, ALU.min))
            dve.tensor_copy(m.gather1[:], tabf[:, 2, :])
            k(dve.tensor_tensor(cmp[:], m.iota_row[0:1, 0:MAX1 + 1].rearrange("p (n o) -> p n o", o=1).to_broadcast([1, MAX1 + 1, E1]),
                                row[0:1, 4:5, :].to_broadcast([1, MAX1 + 1, E1]), ALU.is_ge))
            k(dve.memset(tbf[:], 0.0))
            k(dve.tensor_reduce(tbf[:, 0, BACK1:], cmp[:], AX.X, ALU.add))
            k(dve.tensor_scalar(tbf[:, 0, :], tbf[:, 0, :], float(E1 - 1), None, ALU.min))
            pack(dve, k, tbf[:, 1, 0:STEP_PAIRS1], tbf[:, 0, :], BACK1, E1, STEP_PAIRS1)
            k(dve.tensor_copy(m.tab1[:, 0, :], tbf[:, 1, 0:STEP_PAIRS1]))
            k(dve.tensor_scalar(tbf[:, 1, 0:1], row[0:1, 4, E1 - 1:E1], float(1 - 2 * MIN_PAIRS), None, ALU.add))
            k(dve.tensor_copy(m.tab1[:, 1, 0:1], tbf[:, 1, 0:1]))
            k(dve.tensor_scalar(m.tab1[:, 1, 0:1], m.tab1[:, 1, 0:1], 1, None, ALU.logical_shift_right))
            for n in range(2 * BUFS, E1 * C):
                low(n)


def build(nc, m):
    with ExitStack() as top:
        m.sb = lambda name, shape, dt, stack: stack.enter_context(nc.sbuf_tensor(name, shape, dt))
        tensors(nc, m, top)
        m.s = {n: top.enter_context(nc.semaphore(n)) for n in (
            "consts", "chain0", "chain1", "ctx_turned", "ctx_hi", "ctx_split", "gate_turned", "gate_hi", "gate_done", "counted",
            "onehot", "table", "tid_loaded", "norm_loaded", "gate_loaded", "sh_loaded", "sh_hi", "prefix", "zero_pad",
            "ctx_loaded0", "carried", "ctx_loaded1")}
        m.carry = lambda eng: eng.sem_inc(m.s["carried"], 1)
        with ExitStack() as st:
            m.cth = m.sb("cth", [P, E1, C, D], F32R, st)
            m.ctl = m.sb("ctl", [P, E1, C, D], F32R, st)
            setup(nc, m)
            context(nc, m)
        with ExitStack() as st:
            m.wh = m.sb("wh", [P, W_SETS, HL, D], F32R, st)
            m.wl = m.sb("wl", [P, W_SETS, HL, D], F32R, st)
            m.raw = m.sb("raw", [P, 2, HL, D], F32, st)
            shared_and_routing(nc, m)
            experts(nc, m)
        overflow(nc, m)


def context(nc, m):
    with ExitStack() as st:
        def sb(name, shape, dt=F32):
            return m.sb(name, shape, dt, st)

        def ps(name, shape):
            return st.enter_context(nc.psum_tensor(name, shape, F32))

        s = semaphores(nc, st, "c_", (
            "gx0", "gx1", "xr", "stat1", "mv1", "var1", "rstd1", "h", "t1", "t1hi", "t1lo", "g1", "sil", "a",
            "t2", "t2hi", "t2lo", "g2", "x1", "stat2", "mv2", "var2", "rstd2", "affine", "x2", "ss", "ms", "rrms",
            "hn", "base", "hb0", "hb1", "gi", "si"))
        gx, hbs = (s["gx0"], s["gx1"]), (s["hb0"], s["hb1"])
        KEPT = 8
        xg = sb("c_xg", [P, 2, D])
        xr = sb("c_xr", [P, KEPT, D])
        h = sb("c_h", [P, 2, D])
        hth = sb("c_hth", [P, 2, C, P], F32R)
        htl = sb("c_htl", [P, 2, C, P], F32R)
        a = sb("c_a", [P, 2, D])
        ath = sb("c_ath", [P, 2, C, P], F32R)
        atl = sb("c_atl", [P, 2, C, P], F32R)
        x1 = sb("c_x1", [P, 2, D])
        x2 = sb("c_x2", [P, 2, D])
        hb = sb("c_hb", [P, 2, 2, D])
        sq = sb("c_sq", [P, D])
        stat = sb("c_stat", [P, 2, 6])
        mv = sb("c_mv", [P, 2, 2, 2])
        rs = sb("c_rs", [P, 3, 2, 2])
        affine = sb("c_affine", [P, 2, 2])
        ss = sb("c_ss", [P, 2])
        gidx = sb("c_gidx", [P, 2], I32)
        sidx = sb("c_sidx", [P, 2], I32)
        ps_t1, ps_t2, ps_z = (ps(n, [P, D]) for n in ("ps_t1", "ps_t2", "ps_z"))
        ps_y = [ps(f"ps_y{i}", [P, D]) for i in range(2)]
        block = st.enter_context(nc.Block())

        @block.gpsimd
        def _(pool):
            pairs = number_of_pairs(pool, m.tab1[0:1, 1, 0:1], MAX1)

            def power(which, t, src, offset, scale, sem_mid, sem_out):
                m.carry(pool)
                nc.gpsimd.tensor_scalar(rs[:, which, t.par, 0:1], src, scale, offset, ALU.mult, ALU.add).then_inc(sem_mid, 1)
                pool.wait_ge(sem_mid, t.n + 1)
                nc.gpsimd.tensor_tensor(rs[:, which, t.par, 1:2], rs[:, which, t.par, 0:1], m.minus_half[:], ALU.pow).then_inc(sem_out, 1)

            def emit(part, t):
                if part == "gather":
                    wait(pool, s["xr"], t.n - 1)
                    wait(pool, s["h"], t.n - 1)
                    wait(pool, gx[t.par], 16 * t.half)
                    m.carry(pool)
                    nc.gpsimd.tensor_copy(gidx[:, t.par:t.par + 1], m.gather1[:, bass.ds(t.n, 1)]).then_inc(s["gi"], 1)
                    pool.wait_ge(s["gi"], t.n + 1)
                    m.carry(pool)
                    pool.indirect_dma_start(xg[:, t.par], None, m.x, bass.IndirectOffsetOnAxis(ap=gidx[:, t.par:t.par + 1], axis=0)
                                            ).then_inc(gx[t.par], 16)
                elif part == "rstd1":
                    pool.wait_ge(s["mv1"], t.n + 1)
                    power(0, t, mv[:, 0, t.par, 1:2], LN_EPS, 1.0, s["var1"], s["rstd1"])
                elif part == "rstd2":
                    pool.wait_ge(s["mv2"], t.n + 1)
                    power(1, t, mv[:, 1, t.par, 1:2], LN_EPS, 1.0, s["var2"], s["rstd2"])
                elif part == "affine":
                    pool.wait_ge(s["rstd2"], t.n + 1)
                    wait(pool, s["base"], t.n - 1)
                    m.carry(pool)
                    nc.gpsimd.tensor_scalar(affine[:, t.par, 0:1], rs[:, 1, t.par, 1:2], 1.0, None, ALU.add)
                    nc.gpsimd.tensor_scalar(affine[:, t.par, 1:2], mv[:, 1, t.par, 0:1], rs[:, 1, t.par, 1:2], -1.0,
                                            ALU.mult, ALU.mult).then_inc(s["affine"], 1)
                elif part == "rrms":
                    pool.wait_ge(s["ss"], t.n + 1)
                    power(2, t, ss[:, t.par:t.par + 1], RMS_EPS, 1.0 / D, s["ms"], s["rrms"])
                elif part == "scatter":
                    wait(pool, hbs[t.par], 16 * t.half)
                    m.carry(pool)
                    nc.gpsimd.tensor_copy(sidx[:, t.par:t.par + 1], m.scatter1[:, bass.ds(t.n, 1)]).then_inc(s["si"], 1)
                    pool.wait_ge(s["si"], t.n + 1)
                    pool.wait_ge(s["hn"], t.n + 1)
                    pool.wait_ge(s["base"], t.n + 1)
                    m.carry(pool)
                    pool.indirect_dma_start(m.hb_dram, bass.IndirectOffsetOnAxis(ap=sidx[:, t.par:t.par + 1], axis=0),
                                            hb[:, t.par].rearrange("p a n -> p (a n)"), None,
                                            bounds_check=TOKENS - 1, oob_is_err=False).then_inc(hbs[t.par], 16)

            pipeline(pool, pairs, [("scatter", 8), ("rstd2", 6), ("rstd1", 1), ("affine", 6), ("gather", 0), ("rrms", 6)], emit)
            for q in hbs:
                pool.wait_ge(q, 16 * pairs)
            pool.sem_inc(s["gi"], 1)

        @block.tensor
        def _(pe):
            pairs = number_of_pairs(pe, m.tab1[0:1, 1, 0:1], MAX1)

            expert = {}

            def turn(dst, src):
                for c in range(C):
                    mm = pe.transpose(dst[:, c * P:(c + 1) * P], src[:, c * P:(c + 1) * P], m.ident[:])
                return mm

            def product(dst, hi, lo, t):
                e = bass.ds(expert[t.off], 1)
                for c in range(C):
                    mm = three_products(pe, dst[:], hi[:, t.par, c], lo[:, t.par, c], m.cth[:, e, c, :], m.ctl[:, e, c, :],
                                        c == 0, c == C - 1)
                return mm

            def emit(part, t):
                if part == "t1":
                    pe.wait_ge(s["h"], t.n + 1)
                    wait(pe, s["t1lo"], t.n)
                    turn(ps_t1, h[:, t.par]).then_inc(s["t1"], 1)
                elif part == "g1":
                    pe.wait_ge(s["t1lo"], t.n + 1)
                    wait(pe, s["a"], t.n)
                    product(ps_z, hth, htl, t).then_inc(s["g1"], 1)
                elif part == "t2":
                    pe.wait_ge(s["a"], t.n + 1)
                    wait(pe, s["t2lo"], t.n)
                    turn(ps_t2, a[:, t.par]).then_inc(s["t2"], 1)
                elif part == "g2":
                    pe.wait_ge(s["t2lo"], t.n + 1)
                    wait(pe, s["x1"], t.n - 1)
                    product(ps_y[t.par], ath, atl, t).then_inc(s["g2"], 1)

            pipeline(pe, pairs, [("t1", 2), ("t2", 4), ("g1", 3), ("g2", 5)], emit,
                     looked_up(pe, m.tab1[0:1, 0, :], BACK1, E1, expert))

        @block.scalar
        def _(act):
            pairs = number_of_pairs(act, m.tab1[0:1, 1, 0:1], MAX1)

            def emit(part, t):
                if part == "keep":
                    act.wait_ge(gx[t.par], 16 * (t.half + 1))
                    wait(act, s["x1"], t.n - KEPT + 1)
                    kept = xr[:, bass.ds(t.n % KEPT, 1), :]
                    nc.scalar.activation(kept, xg[:, t.par:t.par + 1, :], ACT.Copy).then_inc(s["xr"], 1)
                elif part == "silu":
                    act.wait_ge(s["g1"], t.n + 1)
                    wait(act, s["t2"], t.n - 1)
                    nc.scalar.activation(a[:, t.par], ps_z[:], ACT.Silu).then_inc(s["sil"], 1)
                elif part == "t1hi":
                    act.wait_ge(s["t1"], t.n + 1)
                    wait(act, s["g1"], t.n - 1)
                    nc.scalar.activation(hth[:, t.par].rearrange("p c n -> p (c n)"), ps_t1[:], ACT.Copy).then_inc(s["t1hi"], 1)
                elif part == "t2hi":
                    act.wait_ge(s["t2"], t.n + 1)
                    wait(act, s["g2"], t.n - 1)
                    nc.scalar.activation(ath[:, t.par].rearrange("p c n -> p (c n)"), ps_t2[:], ACT.Copy).then_inc(s["t2hi"], 1)
                elif part == "squares":
                    act.wait_ge(s["x2"], t.n + 1)
                    wait(act, s["ms"], t.n - 1)
                    nc.scalar.activation(sq[:], x2[:, t.par], ACT.Square, accum_out=ss[:, t.par:t.par + 1]).then_inc(s["ss"], 1)
                elif part == "base":
                    act.wait_ge(s["affine"], t.n + 1)
                    wait(act, hbs[t.par], 16 * t.half)
                    nc.scalar.activation(hb[:, t.par, 1], x1[:, t.par], ACT.Identity, bias=affine[:, t.par, 1:2],
                                         scale=affine[:, t.par, 0:1]).then_inc(s["base"], 1)

            pipeline(act, pairs, [("t1hi", 2), ("t2hi", 4), ("keep", 1), ("base", 7), ("squares", 6), ("silu", 3)], emit)

        @block.vector
        def _(dve):
            pairs = number_of_pairs(dve, m.tab1[0:1, 1, 0:1], MAX1)

            def emit(part, t):
                if part == "stats1":
                    dve.wait_ge(gx[t.par], 16 * (t.half + 1))
                    dve.bn_stats(stat[:, 0, :], xg[:, t.par]).then_inc(s["stat1"], 1)
                    dve.wait_ge(s["stat1"], t.n + 1)
                    m.carry(dve)
                    dve.bn_aggr(mv[:, 0, t.par, :], stat[:, 0, :]).then_inc(s["mv1"], 1)
                elif part == "h":
                    dve.wait_ge(s["rstd1"], t.n + 1)
                    wait(dve, s["t1"], t.n - 1)
                    dve.tensor_scalar(h[:, t.par], xg[:, t.par], mv[:, 0, t.par, 0:1], rs[:, 0, t.par, 1:2],
                                      ALU.subtract, ALU.mult).then_inc(s["h"], 1)
                elif part == "a":
                    dve.wait_ge(s["sil"], t.n + 1)
                    dve.tensor_tensor(a[:, t.par], a[:, t.par], ps_z[:], ALU.mult).then_inc(s["a"], 1)
                elif part == "t1lo":
                    dve.wait_ge(s["t1hi"], t.n + 1)
                    dve.tensor_tensor(htl[:, t.par].rearrange("p c n -> p (c n)"), ps_t1[:],
                                      hth[:, t.par].rearrange("p c n -> p (c n)").bitcast(F32), ALU.subtract).then_inc(s["t1lo"], 1)
                elif part == "t2lo":
                    dve.wait_ge(s["t2hi"], t.n + 1)
                    dve.tensor_tensor(atl[:, t.par].rearrange("p c n -> p (c n)"), ps_t2[:],
                                      ath[:, t.par].rearrange("p c n -> p (c n)").bitcast(F32), ALU.subtract).then_inc(s["t2lo"], 1)
                elif part == "x1":
                    dve.wait_ge(s["g2"], t.n + 1)
                    dve.wait_ge(s["xr"], t.n + 1)
                    wait(dve, s["base"], t.n - 1)
                    kept = xr[:, bass.ds(t.n % KEPT, 1), :]
                    dve.tensor_tensor(x1[:, t.par:t.par + 1, :], kept, ps_y[t.par][:].rearrange("p (o n) -> p o n", o=1),
                                      ALU.add).then_inc(s["x1"], 1)
                    dve.wait_ge(s["x1"], t.n + 1)
                    dve.bn_stats(stat[:, 1, :], x1[:, t.par]).then_inc(s["stat2"], 1)
                    dve.wait_ge(s["stat2"], t.n + 1)
                    m.carry(dve)
                    dve.bn_aggr(mv[:, 1, t.par, :], stat[:, 1, :]).then_inc(s["mv2"], 1)
                elif part == "x2":
                    dve.wait_ge(s["rstd2"], t.n + 1)
                    wait(dve, s["ss"], t.n - 1)
                    dve.tensor_scalar(x2[:, t.par], x1[:, t.par], mv[:, 1, t.par, 0:1], rs[:, 1, t.par, 1:2],
                                      ALU.subtract, ALU.mult).then_inc(s["x2"], 1)
                elif part == "hn":
                    dve.wait_ge(s["rrms"], t.n + 1)
                    wait(dve, hbs[t.par], 16 * t.half)
                    dve.scalar_tensor_tensor(out=hb[:, t.par, 0], in0=x2[:, t.par], scalar=rs[:, 2, t.par, 1:2], in1=m.normw[:],
                                             op0=ALU.mult, op1=ALU.mult).then_inc(s["hn"], 1)

            pipeline(dve, pairs, [("x1", 6), ("stats1", 1), ("t1lo", 2), ("x2", 6), ("h", 1), ("t2lo", 4), ("a", 3),
                                  ("hn", 7)], emit)


def shared_and_routing(nc, m):
    with ExitStack() as st:
        def sb(name, shape, dt=F32):
            return m.sb(name, shape, dt, st)

        def ps(name, shape):
            return st.enter_context(nc.psum_tensor(name, shape, F32))

        s = semaphores(nc, st, "s_", (
            "gx0", "gx1", "bs0", "bs1", "t1", "t1raw", "t1hi", "t1lo", "g1", "u", "sil", "a", "t2", "t2raw", "t2hi",
            "t2lo", "g2", "y", "o", "st0", "st1", "lx0", "lx1", "lt", "lthi", "ltlo", "logits", "lraw", "lback", "lcopied", "low_copied", "chain", "shifted", "exp", "counted", "prefix", "tile_col", "tile_row", "hot",
            "table", "raw0", "raw1", "w_hi", "w_lo"))
        gx, bsl, stl = (s["gx0"], s["gx1"]), (s["bs0"], s["bs1"]), (s["st0"], s["st1"])
        CHUNK = 2 * HL * D // G
        wh_flat, wl_flat = (w[:].rearrange("p w r n -> p (w r n)") for w in (m.wh, m.wl))
        raw_flat = m.raw[:].rearrange("p w r n -> p (w r n)")
        COUNTED, TILED, SKEW_SLOTS = 2, 5, 8
        lx_sem = (s["lx0"], s["lx1"])
        free = m.wh[:].rearrange("p w r n -> p (w r n)")
        lx, lth, ltl = (free[:, i * 4 * D:(i + 1) * 4 * D].rearrange("p (b j n) -> p b j n", b=2, j=2) for i in range(3))
        lx = lx.bitcast(F32)
        lraw = wl_flat[0:2 * E2, 0:4 * P].rearrange("p (b n) -> p b n", b=2).bitcast(F32)
        xg = sb("s_xg", [P, 2, D])
        bs = sb("s_bs", [P, 2, D])
        traw = sb("s_traw", [P, 2, D])
        xth = sb("s_xth", [P, 2, C, P], F32R)
        xtl = sb("s_xtl", [P, 2, C, P], F32R)
        sg_ = sb("s_silu", [P, 2, INNER])
        u_ = sb("s_u", [P, 2, INNER])
        a = sb("s_a", [P, 2, INNER])
        araw = sb("s_araw", [P, 2, INNER])
        ath = sb("s_ath", [P, 2, CI, P], F32R)
        atl = sb("s_atl", [P, 2, CI, P], F32R)
        y = sb("s_y", [P, 2, D])
        o = sb("s_o", [P, 2, D])
        prob = sb("r_prob", [P, G, E2])
        low_part = sb("r_low_part", [P, 2, 2, E2])
        red = sb("r_red", [P, 4, G])
        top8 = sb("r_top8", [P, G, 8])
        idx8 = sb("r_idx8", [P, G, 8], U32)
        eid = sb("r_eid", [P, G, 8])
        oh = sb("r_oh", [P, K, G, E2])
        M = sb("r_m", [P, G, E2])
        rank = sb("r_rank", [P, G, E2])
        tmp = sb("r_tmp", [P, G, E2])
        row = sb("r_row", [P, 8, E2])
        cnt = sb("r_cnt", [P, 2, E2])
        rowi = sb("r_rowi", [P, E2], I32)
        sel = sb("r_sel", [P, 3, G, K])
        seli = sb("r_seli", [P, 3, G, K], I32)
        ovr = sb("r_ovr", [P, K, G])
        hot = sb("r_hot", [P, 2 * K, P + 3 * MAX2], F32R)
        whi = sb("r_whi", [P, G, K], F32R)
        slotval = sb("r_slotval", [P, G, K, 3])
        tabf = sb("r_tabf", [P, 3, MAX2])
        tbf = sb("r_tbf", [1, 6, 2 * STEP_PAIRS + 2])
        ps_t1, ps_t2, ps_gu = (ps(n, [P, D]) for n in ("sps_t1", "sps_t2", "sps_gu"))
        ps_y = [ps(f"sps_y{i}", [P, D]) for i in range(2)]
        ps_p = ps("sps_p", [P, 6, E2])
        ps_r = ps("sps_r", [P, 3 * MAX2])
        ps_e = ps_p[0:1].rearrange("p a e -> p (a e)")[:, 2 * E2:2 * E2 + P]
        ps_l = [ps("sps_l", [P, D]), ps_r]
        ps_b = [ps_gu, ps_y[0]]
        block = st.enter_context(nc.Block())
        pairs = TOKENS // P // 2

        @block.sync
        def _(sp):
            def columns(part, t):
                wait(sp, s["lt"], 2 * t.n - 2)
                sp.dma_start(lx[:, t.par], m.hb_dram.rearrange("(p g) n -> p g n", g=G)[:, bass.ds(2 * t.n, 2), 0:D]
                             ).then_inc(lx_sem[t.par], 16)

            pipeline(sp, G // 4, [("columns", 0)], columns)
            raw_sem = (s["raw0"], s["raw1"])
            for e in range(2):
                sp.dma_start(m.raw[:, e, 0:C], m.w13[e].rearrange("(c p) n -> p c n", p=P)).then_inc(raw_sem[e], 16)
                sp.dma_start(m.raw[:, e, C:HL], m.w2[e].rearrange("(c p) n -> p c n", p=P)).then_inc(raw_sem[e], 16)

            def emit(part, t):
                rows = bass.ds(t.n * P, P)
                if part == "load":
                    wait(sp, s["t1"], t.n - 1)
                    sp.dma_start(xg[:, t.par], m.hb_dram[rows, 0:D]).then_inc(gx[t.par], 16)
                elif part == "load_base":
                    wait(sp, s["o"], t.n - 1)
                    sp.dma_start(bs[:, t.par], m.hb_dram[rows, D:2 * D]).then_inc(bsl[t.par], 16)
                elif part == "third" and isinstance(t.n, int) and t.n == G - 1:
                    sp.wait_ge(s["w_lo"], G // 2)
                    sp.dma_start(m.raw[:, 0, 0:C], m.w13[2].rearrange("(c p) n -> p c n", p=P)).then_inc(raw_sem[0], 16)
                    sp.dma_start(m.raw[:, 0, C:HL], m.w2[2].rearrange("(c p) n -> p c n", p=P)).then_inc(raw_sem[0], 16)
                elif part == "store":
                    sp.wait_ge(s["o"], t.n + 1)
                    sp.dma_start(m.out[rows, :], o[:, t.par]).then_inc(stl[t.par], 16)

            pipeline(sp, pairs, [("third", 1), ("load", 0), ("store", 7), ("load_base", 5)], emit)
            for q in stl:
                sp.wait_ge(q, 16 * pairs)

        @block.gpsimd
        def _(pool):
            def emit(part, t):
                if part == "a":
                    pool.wait_ge(s["u"], t.n + 1)
                    wait(pool, s["t2"], t.n - 1)
                    nc.gpsimd.tensor_tensor(a[:, t.par], sg_[:, t.par], u_[:, t.par], ALU.mult).then_inc(s["a"], 1)
                elif part == "t1lo":
                    pool.wait_ge(s["t1hi"], t.n + 1)
                    wait(pool, s["g1"], t.n - 1)
                    nc.gpsimd.tensor_tensor(xtl[:, t.par].rearrange("p c n -> p (c n)"), traw[:, t.par],
                                            xth[:, t.par].rearrange("p c n -> p (c n)").bitcast(F32), ALU.subtract).then_inc(s["t1lo"], 1)
                elif part == "t2lo":
                    pool.wait_ge(s["t2hi"], t.n + 1)
                    wait(pool, s["g2"], t.n - 1)
                    nc.gpsimd.tensor_tensor(atl[:, t.par].rearrange("p c n -> p (c n)"), araw[:, t.par],
                                            ath[:, t.par].rearrange("p c n -> p (c n)").bitcast(F32), ALU.subtract).then_inc(s["t2lo"], 1)
                elif part == "o":
                    pool.wait_ge(s["y"], t.n + 1)
                    pool.wait_ge(bsl[t.par], 16 * (t.half + 1))
                    wait(pool, stl[t.par], 16 * t.half)
                    nc.gpsimd.tensor_tensor(o[:, t.par], y[:, t.par], bs[:, t.par], ALU.add).then_inc(s["o"], 1)

            pipeline(pool, pairs, [("t1lo", 0), ("t2lo", 2), ("o", 4), ("a", 1)], emit)

        @block.tensor
        def _(pe):
            def turn(dst, src, n):
                for c in range(n):
                    mm = pe.transpose(dst[:, c * P:(c + 1) * P], src[:, c * P:(c + 1) * P], m.ident[:])
                return mm

            def emit(part, t):
                if part == "t1":
                    pe.wait_ge(gx[t.par], 16 * (t.half + 1))
                    wait(pe, s["t1hi"], t.n)
                    turn(ps_t1, xg[:, t.par], C).then_inc(s["t1"], 1)
                elif part == "g1":
                    pe.wait_ge(s["t1lo"], t.n + 1)
                    wait(pe, s["u"], t.n)
                    for c in range(C):
                        mm = three_products(pe, ps_gu[:], xth[:, t.par, c], xtl[:, t.par, c], m.wh_s[:, c], m.wl_s[:, c],
                                            c == 0, c == C - 1)
                    mm.then_inc(s["g1"], 1)
                elif part == "t2":
                    pe.wait_ge(s["a"], t.n + 1)
                    wait(pe, s["t2hi"], t.n)
                    turn(ps_t2, a[:, t.par], CI).then_inc(s["t2"], 1)
                elif part == "g2":
                    pe.wait_ge(s["t2lo"], t.n + 1)
                    wait(pe, s["y"], t.n - 1)
                    for c in range(CI):
                        mm = three_products(pe, ps_y[t.par][:], ath[:, t.par, c], atl[:, t.par, c], m.wh_s[:, C + c],
                                            m.wl_s[:, C + c], c == 0, c == CI - 1)
                    mm.then_inc(s["g2"], 1)
                elif part == "counts" and isinstance(t.n, int) and t.n == COUNTED:
                    pe.wait_ge(s["counted"], 1)
                    pe.matmul(ps_p[:, 0, :], m.before[:], row[:, 0, :], start=True, stop=True)
                    pe.matmul(ps_p[:, 1, :], m.ones[:], row[:, 0, :], start=True, stop=True).then_inc(s["prefix"], 1)
                elif part == "counts" and isinstance(t.n, int) and t.n == TILED:
                    pe.wait_ge(s["tile_col"], 1)
                    pe.matmul(ps_e[:], red[:, 3, 0:1], m.ident[:], start=True, stop=True).then_inc(s["tile_row"], 1)
                elif part == "slots" and not (isinstance(t.n, int) and t.n >= G // 2):
                    for i in range(2 * K):
                        pe.wait_ge(s["hot"], t.n * 2 * K + (i + 1))
                        first = isinstance(t.n, int) and t.n == 0 and i == 0
                        pe.matmul(ps_r[:], hot[:, i, 0:P], hot[:, i, P:], start=first, stop=False,
                                  skip_group_check=True).then_inc(s["table"], 1)

            def logits(part, t):
                if part == "turn":
                    pe.wait_ge(lx_sem[t.par], 16 * (t.half + 1))
                    for j, dst in enumerate((ps_t1, ps_t2)):
                        wait(pe, s["ltlo"], 2 * t.n + (j - 1))
                        turn(dst, lx[:, t.par, j], C).then_inc(s["lt"], 1)
                elif part == "back":
                    pe.wait_ge(s["lraw"], t.n + 1)
                    wait(pe, s["lcopied"], t.n - 1)
                    m.carry(pe)
                    for j in range(2):
                        mm = pe.transpose(ps_b[t.par][:, 2 * j * E2:2 * (j + 1) * E2], lraw[:, t.par, j * P:(j + 1) * P],
                                          m.ident[0:2 * E2, 0:2 * E2])
                    mm.then_inc(s["lback"], 1)
                else:
                    pe.wait_ge(s["ltlo"], 2 * t.n + 2)
                    wait(pe, s["lraw"], t.n - 1)
                    out = ps_l[t.par][0:2 * E2, 0:2 * P].rearrange("p (j n) -> p j n", j=2)
                    for c in range(C):
                        rows = slice(c * P, (c + 1) * P)
                        pe.matmul(out, m.ghl[:, c, :], lth[:, t.par, :, rows], start=(c == 0), stop=False, skip_group_check=True)
                        mm = pe.matmul(out[0:E2], m.ghl[:, c, 0:E2], ltl[:, t.par, :, rows], start=False, stop=(c == C - 1),
                                       skip_group_check=True)
                    mm.then_inc(s["logits"], 1)

            pipeline(pe, G // 4, [("turn", 0), ("logits", 1), ("back", 2)], logits)
            pipeline(pe, pairs, [("t1", 0), ("t2", 2), ("g1", 1), ("g2", 3), ("counts", 0), ("slots", SKEW_SLOTS)], emit)

        @block.scalar
        def _(act):
            def logits(part, t):
                for j, src in enumerate((ps_t1, ps_t2)):
                    act.wait_ge(s["lt"], 2 * t.n + (j + 1))
                    wait(act, s["logits"], t.n - 1)
                    nc.scalar.activation(lth[:, t.par, j], src[:], ACT.Copy).then_inc(s["lthi"], 1)

            pipeline(act, G // 4, [("columns", 0)], logits)
            act.wait_ge(s["shifted"], 1)
            nc.scalar.activation(prob[:], prob[:], ACT.Exp).then_inc(s["exp"], 1)

            act.wait_ge(s["logits"], G // 2)
            for q in (s["raw0"], s["raw1"]):
                act.wait_ge(q, 32)

            def emit(part, t):
                if part == "silu":
                    act.wait_ge(s["g1"], t.n + 1)
                    wait(act, s["a"], t.n - 1)
                    nc.scalar.activation(sg_[:, t.par], ps_gu[:, 0:INNER], ACT.Silu)
                    nc.scalar.activation(u_[:, t.par], ps_gu[:, INNER:D], ACT.Copy).then_inc(s["u"], 1)
                elif part == "t1":
                    act.wait_ge(s["t1"], t.n + 1)
                    wait(act, s["t1lo"], t.n - 1)
                    nc.scalar.activation(traw[:, t.par], ps_t1[:], ACT.Copy)
                    wait(act, s["g1"], t.n - 1)
                    nc.scalar.activation(xth[:, t.par].rearrange("p c n -> p (c n)"), ps_t1[:], ACT.Copy).then_inc(s["t1hi"], 1)
                elif part == "t2":
                    act.wait_ge(s["t2"], t.n + 1)
                    wait(act, s["t2lo"], t.n - 1)
                    nc.scalar.activation(araw[:, t.par], ps_t2[:, 0:INNER], ACT.Copy)
                    wait(act, s["g2"], t.n - 1)
                    nc.scalar.activation(ath[:, t.par].rearrange("p c n -> p (c n)"), ps_t2[:, 0:INNER], ACT.Copy).then_inc(s["t2hi"], 1)
                elif part == "third" and isinstance(t.n, int) and t.n == G - 1:
                    act.wait_ge(s["raw0"], 64)
                    for rows in (slice(0, HL // 2), slice(HL // 2, HL)):
                        nc.scalar.activation(m.wh[:, 2, rows], m.raw[:, 0, rows], ACT.Copy).then_inc(s["w_hi"], 1)
                elif part == "chunk":
                    cols = bass.ds(t.n * CHUNK, CHUNK)
                    nc.scalar.activation(wh_flat[:, cols], raw_flat[:, cols], ACT.Copy).then_inc(s["w_hi"], 1)
                elif part == "y":
                    act.wait_ge(s["g2"], t.n + 1)
                    wait(act, s["o"], t.n - 1)
                    nc.scalar.activation(y[:, t.par], ps_y[t.par][:], ACT.Copy).then_inc(s["y"], 1)

            pipeline(act, pairs, [("t1", 0), ("t2", 2), ("y", 4), ("chunk", 0), ("silu", 1), ("third", 2)], emit)

        @block.vector
        def _(dve):
            k_ = Chain(dve, s["chain"])
            flat = "p g e -> p (g e)"

            def over_experts(ap):
                return ap.rearrange("p (g o) -> p g o", o=1).to_broadcast([P, G, E2])

            def over_tokens(ap):
                return ap.to_broadcast([P, G, E2])

            def logits(part, t):
                if part == "raw":
                    dve.wait_ge(s["logits"], t.n + 1)
                    wait(dve, s["lback"], t.n - 1)
                    dve.tensor_copy(lraw[:, t.par], ps_l[t.par][0:2 * E2, 0:2 * P]).then_inc(s["lraw"], 1)
                    return
                if part == "copy":
                    dve.wait_ge(s["lback"], t.n + 1)
                    parts = ps_b[t.par][:, 0:4 * E2].rearrange("p (g b e) -> p g b e", b=2, e=E2)
                    dve.tensor_copy(low_part[:, t.par], parts[:, :, 1]).then_inc(s["low_copied"], 1)
                    dve.wait_ge(s["low_copied"], t.n + 1)
                    dve.tensor_tensor(prob[:, bass.ds(2 * t.n, 2), :], parts[:, :, 0], low_part[:, t.par], ALU.add).then_inc(s["lcopied"], 1)
                    return
                for j, src in enumerate((ps_t1, ps_t2)):
                    dve.wait_ge(s["lthi"], 2 * t.n + (j + 1))
                    dve.tensor_tensor(ltl[:, t.par, j], src[:], lth[:, t.par, j].bitcast(F32), ALU.subtract).then_inc(s["ltlo"], 1)

            pipeline(dve, G // 4, [("columns", 0), ("raw", 1), ("copy", 2)], logits)
            dve.wait_ge(s["lcopied"], G // 2)
            k_(dve.tensor_reduce(red[:, 0, :], prob[:], AX.X, ALU.max))
            dve.tensor_tensor(prob[:], prob[:], over_experts(red[:, 0, :]), ALU.subtract).then_inc(s["shifted"], 1)
            dve.wait_ge(s["exp"], 1)
            k_(dve.tensor_reduce(red[:, 1, :], prob[:], AX.X, ALU.add))
            k_(dve.reciprocal(red[:, 2, :], red[:, 1, :]))
            k_(dve.tensor_tensor(prob[:], prob[:], over_experts(red[:, 2, :]), ALU.mult))
            for g in range(G):
                last = dve.max(top8[:, g, :], prob[:, g, :])
            k_(last)
            for g in range(G):
                last = dve.max_index(idx8[:, g, :], top8[:, g, :], prob[:, g, :])
            k_(last)
            dve.tensor_copy(eid[:], idx8[:])
            k_(dve.tensor_reduce(red[:, 3, :], top8[:, :, 0:K], AX.X, ALU.add))
            k_(dve.reciprocal(red[:, 3, :], red[:, 3, :]))
            dve.tensor_tensor(m.topw[:], top8[:, :, 0:K], red[:, 3, :].rearrange("p (g o) -> p g o", o=1).to_broadcast([P, G, K]), ALU.mult)
            for k in range(K):
                last = dve.tensor_tensor(oh[:, k], m.iota_row[:, 0:E2].rearrange("p (o e) -> p o e", o=1).to_broadcast([P, G, E2]),
                                         eid[:, :, k:k + 1].to_broadcast([P, G, E2]), ALU.is_equal)
            k_(last)
            k_(dve.tensor_tensor(M[:], oh[:, 0], oh[:, 1], ALU.add))
            k_(dve.tensor_tensor(tmp[:], oh[:, 2], oh[:, 3], ALU.add))
            k_(dve.tensor_tensor(M[:], M[:], tmp[:], ALU.add))
            dve.tensor_reduce(row[:, 0, :], M[:].rearrange("p g e -> p e g"), AX.X, ALU.add).then_inc(s["counted"], 1)
            k_(dve.memset(rank[:, 0, :], 0.0))
            for g in range(1, G):
                k_(dve.tensor_tensor(rank[:, g, :], rank[:, g - 1, :], M[:, g - 1, :], ALU.add))
            k_(dve.memset(tbf[:], 0.0))
            dve.tensor_copy(slotval[:, :, :, 0], m.tokcol[:].rearrange("p (g o) -> p g o", o=1).to_broadcast([P, G, K]))
            k_(dve.tensor_copy(whi[:], m.topw[:]))
            dve.tensor_copy(slotval[:, :, :, 1], whi[:].bitcast(F32))
            k_(dve.tensor_tensor(slotval[:, :, :, 2], m.topw[:], whi[:].bitcast(F32), ALU.subtract))
            k_(dve.tensor_copy(m.topk[:], m.topw[:].rearrange("p g k -> p k g")))
            dve.wait_ge(s["prefix"], 1)
            k_(dve.tensor_copy(cnt[:], ps_p[:, 0:2, :]))
            k_(dve.tensor_scalar(row[:, 1, :], cnt[:, 1, :], float(m.cap), float(P - 1), ALU.min, ALU.add))
            k_(dve.tensor_copy(rowi[:], row[:, 1, :]))
            k_(dve.tensor_scalar(rowi[:], rowi[:], 7, None, ALU.logical_shift_right))
            k_(dve.tensor_copy(row[:, 2, :], rowi[:]))
            k_(dve.tensor_scalar(row[:, 2, :], row[:, 2, :], 1.0, None, ALU.max))
            k_(dve.memset(row[:, 3, :], 0.0))
            k_(dve.tensor_tensor_scan(row[:, 4, :], row[:, 2, :], row[:, 3, :], 0.0, ALU.add, ALU.add))
            k_(dve.tensor_tensor(row[:, 5, :], row[:, 4, :], row[:, 2, :], ALU.subtract))
            k_(dve.tensor_scalar(tmp[:, 0, :], row[:, 4, :], float(BACK2), m.part_id[:, 0:1], ALU.add, ALU.is_le))
            dve.tensor_reduce(red[:, 3, 0:1], tmp[:, 0, :], AX.X, ALU.add).then_inc(s["tile_col"], 1)
            k_(dve.tensor_tensor(rank[:], rank[:], over_tokens(cnt[:, 0:1, :]), ALU.add))
            k_(dve.tensor_scalar(tmp[:], rank[:], float(m.cap), None, ALU.is_lt))
            k_(dve.tensor_scalar(row[:, 6, :], row[:, 5, :], float(P), None, ALU.mult))
            k_(dve.tensor_tensor(rank[:], rank[:], over_tokens(row[:, 6:7, :]), ALU.add))
            k_(dve.tensor_tensor(rank[:], rank[:], tmp[:], ALU.mult))
            k_(dve.tensor_scalar(row[:, 6, :], row[:, 4, :], float(MAX2 * P - 1), None, ALU.add))
            k_(dve.scalar_tensor_tensor(out=tmp[:], in0=tmp[:], scalar=1.0, in1=over_tokens(row[:, 6:7, :]), op0=ALU.is_lt, op1=ALU.mult))
            k_(dve.tensor_tensor(rank[:], rank[:], tmp[:], ALU.add))
            for k in range(K):
                k_(dve.tensor_tensor(tmp[:], oh[:, k], rank[:], ALU.mult))
                k_(dve.tensor_reduce(sel[:, 0, :, k], tmp[:], AX.X, ALU.add))
            k_(dve.tensor_copy(seli[:, 0], sel[:, 0]))
            dve.tensor_scalar(seli[:, 1], seli[:, 0], 7, None, ALU.logical_shift_right)
            k_(dve.tensor_scalar(seli[:, 2], seli[:, 0], P - 1, None, ALU.bitwise_and))
            dve.tensor_copy(sel[:, 1], seli[:, 1])
            k_(dve.tensor_copy(sel[:, 2], seli[:, 2]))

            k_(dve.tensor_scalar(red[:, 0, :], m.tokcol[:], m.pad_row[:, 0:1], None, ALU.subtract))
            slot = sel[:, 0].rearrange("p g k -> p k g")
            k_(dve.tensor_scalar(m.over_row[:], slot, -float(MAX2 * P), 0.0, ALU.add, ALU.max))
            k_(dve.scalar_tensor_tensor(out=ovr[:], in0=slot, scalar=float(MAX2 * P), in1=red[:, 0:1, :].to_broadcast([P, K, G]),
                                        op0=ALU.is_ge, op1=ALU.mult))
            k_(dve.tensor_scalar(m.over_tok[:], ovr[:], m.pad_row[:, 0:1], -1.0, ALU.add, ALU.add))
            dve.wait_ge(s["tile_row"], 1)
            k_(dve.tensor_scalar(tbf[:, 0, :], ps_e[:, 0:2 * STEP_PAIRS + 2], float(E2 - 1), None, ALU.min))
            k_(dve.tensor_tensor(tbf[:, 1, BACK2 + 1:], tbf[:, 0, BACK2 + 1:], tbf[:, 0, BACK2:-1], ALU.subtract))
            k_(dve.tensor_scalar(tbf[:, 2, :], tbf[:, 0, :], 2.0, None, ALU.add))
            k_(dve.tensor_tensor(tbf[:, 1, :], tbf[:, 1, :], tbf[:, 2, :], ALU.mult))
            k_(dve.tensor_scalar(tbf[:, 2, :], tbf[:, 1, :], float(E2 - 1), None, ALU.is_le))
            k_(dve.tensor_tensor(tbf[:, 1, :], tbf[:, 1, :], tbf[:, 2, :], ALU.mult))
            for r in range(2):
                pack(dve, k_, tbf[:, 2 + r, 0:STEP_PAIRS], tbf[:, r, :], BACK2, E2, STEP_PAIRS)
            k_(dve.tensor_copy(m.tab2[:, 0:2, :], tbf[:, 2:4, 0:STEP_PAIRS]))
            k_(dve.tensor_scalar(tbf[:, 4, 0:1], row[0:1, 4, E2 - 1:E2], float(1 - 2 * MIN_PAIRS), None, ALU.add))
            k_(dve.tensor_copy(m.tab2[:, 2, 0:1], tbf[:, 4, 0:1]))
            k_(dve.tensor_scalar(m.tab2[:, 2, 0:1], m.tab2[:, 2, 0:1], 1, None, ALU.logical_shift_right))
            k_(dve.tensor_reduce(tbf[:, 5, 0:1], cnt[0:1, 1, :], AX.X, ALU.max))
            k_(dve.tensor_scalar(tbf[:, 5, 0:1], tbf[:, 5, 0:1], float(m.cap), None, ALU.is_gt))
            k_(dve.tensor_copy(m.tab2[:, 2, 1:2], tbf[:, 5, 0:1]))

            def one_hot(g, par):
                for k in range(K):
                    column = lambda t: t[:, bass.ds(g, 1), k:k + 1].rearrange("p a b -> p (a b)")
                    wait(dve, s["table"], (g - 2) * K + k + 1)
                    dve.tensor_scalar(hot[:, par * K + k, 0:P], m.iota_row[:], column(sel[:, 2]), None, ALU.is_equal)
                    dve.scalar_tensor_tensor(out=hot[:, par * K + k, P:].rearrange("p (v n) -> p v n", v=3),
                                             in0=m.iota_row[:, 0:MAX2].rearrange("p (o n) -> p o n", o=1).to_broadcast([P, 3, MAX2]),
                                             scalar=column(sel[:, 1]),
                                             in1=slotval[:, bass.ds(g, 1), k].rearrange("p a (v o) -> p (a v) o", o=1).to_broadcast([P, 3, MAX2]),
                                             op0=ALU.is_equal, op1=ALU.mult).then_inc(s["hot"], 1)

            def chunk(g):
                cols = bass.ds(g * CHUNK, CHUNK)
                dve.wait_ge(s["w_hi"], g + 1)
                dve.tensor_tensor(wl_flat[:, cols], raw_flat[:, cols], wh_flat[:, cols].bitcast(F32), ALU.subtract).then_inc(s["w_lo"], 1)

            for g in range(2):
                one_hot(g, g)
                chunk(g)
            with dve.Fori(1, G // 2) as q:
                for b in range(2):
                    one_hot(2 * q + b, b)
                    chunk(2 * q + b)

            dve.wait_ge(s["table"], G * K)
            k_(dve.tensor_scalar(tabf[:, 0, :], ps_r[:, 0:MAX2], 0.0, m.pad_row[:, 0:1], ALU.is_equal, ALU.mult))
            k_(dve.scalar_tensor_tensor(out=tabf[:, 1, :], in0=ps_r[:, 0:MAX2], scalar=-1.0, in1=tabf[:, 0, :],
                                        op0=ALU.add, op1=ALU.add))
            dve.tensor_copy(m.scatter2[:], tabf[:, 1, :])
            k_(dve.tensor_scalar(tabf[:, 2, :], tabf[:, 1, :], float(TOKENS - 1), None, ALU.min))
            k_(dve.tensor_scalar(m.gather2[:], tabf[:, 2, :], 2.0, None, ALU.mult))
            k_(dve.tensor_copy(tabf[:, 0, :], ps_r[:, MAX2:2 * MAX2]))
            k_(dve.tensor_tensor(m.weight2[:], tabf[:, 0, :], ps_r[:, 2 * MAX2:], ALU.add))
            for i, rows in enumerate((slice(0, HL // 2), slice(HL // 2, HL))):
                dve.wait_ge(s["w_hi"], G + 1 + i)
                dve.tensor_tensor(m.wl[:, 2, rows], m.raw[:, 0, rows], m.wh[:, 2, rows].bitcast(F32), ALU.subtract)


def experts(nc, m):
    with ExitStack() as st:
        def sb(name, shape, dt=F32):
            return m.sb(name, shape, dt, st)

        def ps(name, shape):
            return st.enter_context(nc.psum_tensor(name, shape, F32))

        s = semaphores(nc, st, "e_", (
            "gx0", "gx1", "gi", "si", "add0", "add1", "t1", "t1hi", "t1lo", "g1", "sil", "a", "t2", "t2hi", "t2lo", "g2",
            "y", "last0", "last1", "raw", "lastrow", "carried",
            "hi_rows_a", "hi_rows_b", "hi_rows_c", "lo_rows_a", "lo_rows_b", "lo_rows_c"))
        gx, add, lst = (s["gx0"], s["gx1"]), (s["add0"], s["add1"]), (s["last0"], s["last1"])
        xg = sb("e_xg", [P, 2, D])
        xth = sb("e_xth", [P, 2, C, P], F32R)
        xtl = sb("e_xtl", [P, 2, C, P], F32R)
        a = sb("e_a", [P, 2, INNER])
        ath = sb("e_ath", [P, 2, CI, P], F32R)
        atl = sb("e_atl", [P, 2, CI, P], F32R)
        y = sb("e_y", [P, 2, D])
        lastrow = sb("e_lastrow", [P, 2, D])
        gidx = sb("e_gidx", [P, 2], I32)
        sidx = sb("e_sidx", [P, 2], I32)
        ps_t1, ps_t2, ps_gu = (ps(n, [P, D]) for n in ("eps_t1", "eps_t2", "eps_gu"))
        ps_y = [ps(f"eps_y{i}", [P, D]) for i in range(2)]
        hn_rows = m.hb_dram.rearrange("t (a n) -> (t a) n", a=2)
        block = st.enter_context(nc.Block())

        ROWS = {"rows_c": (4, 5), "rows_b": (2, 3), "rows_a": (0, 1)}

        @block.sync
        def _(sp):
            pairs = number_of_pairs(sp, m.tab2[0:1, 2, 0:1], MAX2)
            split = {}

            def load(e, par):
                ex = bass.ds(e, 1)
                sp.dma_start(m.raw[:, par, 0:C], m.w13[ex].rearrange("o (c p) n -> p (o c) n", p=P)).then_inc(s["raw"], 16)
                sp.dma_start(m.raw[:, par, C:HL], m.w2[ex].rearrange("o (c p) n -> p (o c) n", p=P)).then_inc(s["raw"], 16)

            def emit(part, t):
                if part == "load":
                    e = split[t.off]
                    with sp.If(e > 0):
                        with sp.If(e < E2 - 2):
                            sp.wait_ge(s["lo_rows_c"], 2 * e + 2)
                            sp.wait_ge(s["raw"], 32 * e + 64)
                            load((e + 2) % E2, bass.ds(e % 2, 1))
                elif part == "last_row":
                    sp.wait_ge(s["lastrow"], t.n + 1)
                    sp.dma_start(m.last_dram[bass.ds(t.n, 1), :], lastrow[P - 1:P, t.par]).then_inc(lst[t.par], 16)

            sp.sem_inc(s["raw"], 32 * W_SETS)
            load(W_SETS, slice(1, 2))
            sp.wait_ge(s["raw"], 32 * (W_SETS + 1))
            load(W_SETS + 1, slice(0, 1))
            pipeline(sp, pairs, [("load", 1), ("last_row", 2)], emit, looked_up(sp, m.tab2[0:1, 1, :], BACK2, E2, split))
            for q in lst:
                sp.wait_ge(q, 16 * pairs)
            sp.sem_inc(s["carried"], 1)

        @block.gpsimd
        def _(pool):
            pairs = number_of_pairs(pool, m.tab2[0:1, 2, 0:1], MAX2)

            def emit(part, t):
                if part == "gather":
                    wait(pool, s["t1"], t.n - 1)
                    wait(pool, gx[t.par], 16 * t.half)
                    m.carry(pool)
                    nc.gpsimd.tensor_copy(gidx[:, t.par:t.par + 1], m.gather2[:, bass.ds(t.n, 1)]).then_inc(s["gi"], 1)
                    pool.wait_ge(s["gi"], t.n + 1)
                    m.carry(pool)
                    pool.indirect_dma_start(xg[:, t.par], None, hn_rows, bass.IndirectOffsetOnAxis(ap=gidx[:, t.par:t.par + 1], axis=0)
                                            ).then_inc(gx[t.par], 16)
                elif part == "add":
                    wait(pool, add[t.par], 16 * t.half)
                    m.carry(pool)
                    nc.gpsimd.tensor_copy(sidx[:, t.par:t.par + 1], m.scatter2[:, bass.ds(t.n, 1)]).then_inc(s["si"], 1)
                    pool.wait_ge(s["si"], t.n + 1)
                    pool.wait_ge(s["y"], t.n + 1)
                    wait(pool, add[1 - t.par], 16 * (t.half + t.par))
                    m.carry(pool)
                    pool.indirect_dma_start(m.out, bass.IndirectOffsetOnAxis(ap=sidx[:, t.par:t.par + 1], axis=0), y[:, t.par], None,
                                            compute_op=ALU.add).then_inc(add[t.par], 16)

            pipeline(pool, pairs, [("gather", 0), ("add", 6)], emit)
            for q in add:
                pool.wait_ge(q, 16 * pairs)
            m.carry(pool)

        @block.tensor
        def _(pe):
            pairs = number_of_pairs(pe, m.tab2[0:1, 2, 0:1], MAX2)

            def turn(dst, src, n):
                for c in range(n):
                    mm = pe.transpose(dst[:, c * P:(c + 1) * P], src[:, c * P:(c + 1) * P], m.ident[:])
                return mm

            expert = {}

            def emit(part, t):
                if part == "t1":
                    pe.wait_ge(gx[t.par], 16 * (t.half + 1))
                    wait(pe, s["t1lo"], t.n)
                    turn(ps_t1, xg[:, t.par], C).then_inc(s["t1"], 1)
                elif part == "g1":
                    w = bass.ds(expert[t.off] % W_SETS, 1)
                    pe.wait_ge(s["lo_rows_b"], 2 * expert[t.off] + 2)
                    pe.wait_ge(s["t1lo"], t.n + 1)
                    wait(pe, s["a"], t.n)
                    for c in range(C):
                        mm = three_products(pe, ps_gu[:], xth[:, t.par, c], xtl[:, t.par, c], m.wh[:, w, c, :], m.wl[:, w, c, :],
                                            c == 0, c == C - 1)
                    mm.then_inc(s["g1"], 1)
                elif part == "t2":
                    pe.wait_ge(s["a"], t.n + 1)
                    wait(pe, s["t2lo"], t.n)
                    turn(ps_t2, a[:, t.par], CI).then_inc(s["t2"], 1)
                elif part == "g2":
                    w = bass.ds(expert[t.off] % W_SETS, 1)
                    pe.wait_ge(s["lo_rows_c"], 2 * expert[t.off] + 2)
                    pe.wait_ge(s["t2lo"], t.n + 1)
                    wait(pe, s["lastrow"], t.n - 1)
                    for c in range(CI):
                        mm = three_products(pe, ps_y[t.par][:], ath[:, t.par, c], atl[:, t.par, c], m.wh[:, w, C + c, :],
                                            m.wl[:, w, C + c, :], c == 0, c == CI - 1)
                    mm.then_inc(s["g2"], 1)

            pipeline(pe, pairs, [("t1", 0), ("t2", 2), ("g1", 1), ("g2", 3)], emit, looked_up(pe, m.tab2[0:1, 0, :], BACK2, E2, expert))

        @block.scalar
        def _(act):
            pairs = number_of_pairs(act, m.tab2[0:1, 2, 0:1], MAX2)
            for part in ROWS:
                act.sem_inc(s["hi_" + part], 2 * W_SETS)
            split = {}

            def emit(part, t):
                if part == "silu":
                    act.wait_ge(s["g1"], t.n + 1)
                    wait(act, s["t2"], t.n - 1)
                    nc.scalar.activation(a[:, t.par], ps_gu[:, 0:INNER], ACT.Silu).then_inc(s["sil"], 1)
                elif part == "t1hi":
                    act.wait_ge(s["t1"], t.n + 1)
                    wait(act, s["g1"], t.n - 1)
                    nc.scalar.activation(xth[:, t.par].rearrange("p c n -> p (c n)"), ps_t1[:], ACT.Copy).then_inc(s["t1hi"], 1)
                elif part == "t2hi":
                    act.wait_ge(s["t2"], t.n + 1)
                    wait(act, s["g2"], t.n - 1)
                    nc.scalar.activation(ath[:, t.par].rearrange("p c n -> p (c n)"), ps_t2[:, 0:INNER], ACT.Copy).then_inc(s["t2hi"], 1)
                elif part == "y":
                    act.wait_ge(s["g2"], t.n + 1)
                    wait(act, add[t.par], 16 * t.half)
                    nc.scalar.activation(y[:, t.par], ps_y[t.par][:], ACT.Copy, scale=m.weight2[:, bass.ds(t.n, 1)]).then_inc(s["y"], 1)
                    wait(act, lst[t.par], 16 * t.half)
                    nc.scalar.activation(lastrow[96:P, t.par], ps_y[t.par][96:P, :], ACT.Copy).then_inc(s["lastrow"], 1)
                elif part in ROWS:
                    e = split[t.off]
                    with act.If(e > 0):
                        act.wait_ge(s["raw"], 32 * e + 32)
                        wait(act, s["g2" if part == "rows_c" else "g1"], t.n)
                        for r in ROWS[part]:
                            nc.scalar.activation(m.wh[:, bass.ds(e % W_SETS, 1), r, :], m.raw[:, bass.ds(e % 2, 1), r, :],
                                                 ACT.Copy).then_inc(s["hi_" + part], 1)

            pipeline(act, pairs, [("t1hi", 0), ("t2hi", 2), ("rows_c", 3), ("y", 4), ("silu", 1), ("rows_b", 2), ("rows_a", 1)], emit,
                     looked_up(act, m.tab2[0:1, 1, :], BACK2, E2, split))

        @block.vector
        def _(dve):
            pairs = number_of_pairs(dve, m.tab2[0:1, 2, 0:1], MAX2)
            for part in ROWS:
                dve.sem_inc(s["lo_" + part], 2 * W_SETS)
            split = {}

            def emit(part, t):
                if part == "a":
                    dve.wait_ge(s["sil"], t.n + 1)
                    dve.tensor_tensor(a[:, t.par], a[:, t.par], ps_gu[:, INNER:D], ALU.mult).then_inc(s["a"], 1)
                elif part == "t1lo":
                    dve.wait_ge(s["t1hi"], t.n + 1)
                    dve.tensor_tensor(xtl[:, t.par].rearrange("p c n -> p (c n)"), ps_t1[:],
                                      xth[:, t.par].rearrange("p c n -> p (c n)").bitcast(F32), ALU.subtract).then_inc(s["t1lo"], 1)
                elif part == "t2lo":
                    dve.wait_ge(s["t2hi"], t.n + 1)
                    dve.tensor_tensor(atl[:, t.par].rearrange("p c n -> p (c n)"), ps_t2[:, 0:INNER],
                                      ath[:, t.par].rearrange("p c n -> p (c n)").bitcast(F32), ALU.subtract).then_inc(s["t2lo"], 1)
                elif part in ROWS:
                    e = split[t.off]
                    w = bass.ds(e % W_SETS, 1)
                    with dve.If(e > 0):
                        for i, r in enumerate(ROWS[part]):
                            dve.wait_ge(s["hi_" + part], 2 * e + (i + 1))
                            dve.tensor_tensor(m.wl[:, w, r, :], m.raw[:, bass.ds(e % 2, 1), r, :],
                                              m.wh[:, w, r, :].bitcast(F32), ALU.subtract).then_inc(s["lo_" + part], 1)

            pipeline(dve, pairs, [("t1lo", 0), ("t2lo", 2), ("rows_c", 3), ("a", 1), ("rows_b", 2), ("rows_a", 1)], emit,
                     looked_up(dve, m.tab2[0:1, 1, :], BACK2, E2, split))


def overflow(nc, m):
    with ExitStack() as st:
        s = semaphores(nc, st, "o_", ("rows", "add", "idx", "y"))
        rows = m.sb("o_rows", [P, D], F32, st)
        y = m.sb("o_y", [P, D], F32, st)
        ridx = m.sb("o_ridx", [P, 1], I32, st)
        tidx = m.sb("o_tidx", [P, 1], I32, st)
        wcol = m.sb("o_wcol", [P, 1], F32, st)
        block = st.enter_context(nc.Block())

        @block.gpsimd
        def _(pool):
            flag = pool.value_load(m.tab2[0:1, 2, 1:2], min_val=0, max_val=1)
            with pool.If(flag > 0):
                with pool.Fori(0, K * G) as i:
                    one = bass.ds(i, 1)
                    nc.gpsimd.tensor_copy(ridx[:], m.over_row[:].rearrange("p k g -> p (k g)")[:, one])
                    nc.gpsimd.tensor_copy(tidx[:], m.over_tok[:].rearrange("p k g -> p (k g)")[:, one])
                    nc.gpsimd.tensor_copy(wcol[:], m.topk[:].rearrange("p k g -> p (k g)")[:, one]).then_inc(s["idx"], 1)
                    pool.wait_ge(s["idx"], i + 1)
                    m.carry(pool)
                    pool.indirect_dma_start(rows[:], None, m.last_dram, bass.IndirectOffsetOnAxis(ap=ridx[:, 0:1], axis=0)
                                            ).then_inc(s["rows"], 16)
                    pool.wait_ge(s["rows"], 16 * (i + 1))
                    m.carry(pool)
                    nc.gpsimd.tensor_scalar(y[:], rows[:], wcol[:, 0:1], 0.0, ALU.mult, ALU.add).then_inc(s["y"], 1)
                    pool.wait_ge(s["y"], i + 1)
                    m.carry(pool)
                    pool.indirect_dma_start(m.out, bass.IndirectOffsetOnAxis(ap=tidx[:, 0:1], axis=0), y[:], None,
                                            compute_op=ALU.add).then_inc(s["add"], 16)
                    pool.wait_ge(s["add"], 16 * (i + 1))
                    m.carry(pool)


def kernel(x, itok_BxS_13_99985, ctx_2048, L0_ffn_norm_w, L0_ffn_gate_w, L0_ffn_w13, L0_ffn_w2,
           L0_ffn_shared_gate_w, L0_ffn_shared_up_w, L0_ffn_shared_down_w):
    import numpy as np
    import concourse.bacc as bacc
    from concourse.bass_utils import run_bass_kernel_spmd

    nc = bacc.Bacc("TRN2", target_bir_lowering=False, num_devices=1)
    arrays = {
        "x": x.reshape(TOKENS, D), "tid": itok_BxS_13_99985.reshape(P, G), "ctx_w": ctx_2048,
        "norm_w": L0_ffn_norm_w.reshape(1, D), "gate_w": L0_ffn_gate_w, "w13": L0_ffn_w13, "w2": L0_ffn_w2,
        "sg": L0_ffn_shared_gate_w, "su": L0_ffn_shared_up_w, "sd": L0_ffn_shared_down_w,
    }
    arrays = {"in_" + n: np.ascontiguousarray(a) for n, a in arrays.items()}
    given = {n: nc.dram_tensor(n, a.shape, mybir.dt.from_np(a.dtype), kind="ExternalInput").ap() for n, a in arrays.items()}
    m = Memory()
    m.cap = CAP
    m.x, m.tid, m.ctx_w, m.norm_w = given["in_x"], given["in_tid"], given["in_ctx_w"], given["in_norm_w"]
    m.gate_w, m.w13, m.w2 = given["in_gate_w"], given["in_w13"], given["in_w2"]
    m.sg, m.su, m.sd = given["in_sg"], given["in_su"], given["in_sd"]
    m.out = nc.dram_tensor("out", (TOKENS + PAD, D), F32, kind="ExternalOutput").ap()
    m.hb_dram = nc.dram_tensor("hb_dram", (TOKENS, 2 * D), F32, kind="Internal").ap()
    m.last_dram = nc.dram_tensor("last_dram", (MAX2, D), F32, kind="Internal").ap()
    build(nc, m)
    result = run_bass_kernel_spmd(nc, [arrays], core_ids=[0])
    return result.results[0]["out"][:TOKENS].reshape(4, 512, D)
```
